# Optimizing a Trainium2 kernel written in Bass

```python
import numpy as np
import jax
import jax.numpy as jnp

def _softmax(x, axis=-1):
    return jax.nn.softmax(x, axis=axis)

def _gelu(x):
    return jax.nn.gelu(x, approximate=True)

def _silu(x):
    return jax.nn.silu(x)

def _sigmoid(x):
    return jax.nn.sigmoid(x)

def _layernorm(x, axis=-1, eps=1e-05):
    m = jnp.mean(x, axis=axis, keepdims=True)
    v = jnp.var(x, axis=axis, keepdims=True)
    return (x - m) / jnp.sqrt(v + eps)

def _scatter_add(tgt, idx, src, axis=0):
    return tgt.at[idx].add(src)

def _segment_sum(src, seg, n):
    return jax.ops.segment_sum(src, seg, n)
kernel_name = 'mk_xattn_ffn_d1_seqx_r8_2e5a33'

def setup_inputs(seed: int=0):
    np.random.seed(seed)
    _w = jnp.asarray

    def _rec_inputs():
        import jax
        import jax.numpy as jnp
        _rk = jax.random.key(seed)
        x = 7.22e-05 + 1 * jax.random.normal(jax.random.fold_in(_rk, 1), (32, 128, 128), jnp.float32)
        _lenS = 128 - jax.random.randint(jax.random.fold_in(_rk, 7), (32,), 0, max(1, 128 // 4) + 1, jnp.int32)
        _lenS2 = 128 - jax.random.randint(jax.random.fold_in(_rk, 8), (32,), 0, max(1, 128 // 4) + 1, jnp.int32)
        _ctx_1024P = jax.random.normal(jax.random.fold_in(_rk, 11), (32, 16, 128), jnp.float32)
        _ctx_1024c = jax.random.dirichlet(jax.random.fold_in(_rk, 511), 0.3 * jnp.ones((16,), jnp.float32), (32, 128))
        _ctx_1024t = jnp.einsum('bsk,bkd->bsd', _ctx_1024c, _ctx_1024P)
        _ctx_1024t = _ctx_1024t * jax.lax.rsqrt(jnp.mean(jnp.square(_ctx_1024t)) + 1e-12) * 0.953939
        ctx_1024 = 4.13588e-05 + 0.999923 * (_ctx_1024t + 0.3 * jax.random.normal(jax.random.fold_in(_rk, 611), (32, 128, 128), jnp.float32))
        return (x, ctx_1024, _lenS2)
    x, ctx_1024, _lenS2 = _rec_inputs()

    def _L0_xattn_setup():
        import jax, jax.numpy as jnp
        import numpy as np
        import math
        NUM_HEADS = 16
        D_MODEL = 128
        BATCH = 4
        SEQ = 256
        NEG_INF = -1000000000.0
        key = jax.random.key(seed)
        ks = jax.random.split(key, 8)
        scale = 1.0 / math.sqrt(D_MODEL)
        return {'queries': jax.random.normal(ks[0], (BATCH, SEQ, D_MODEL), jnp.float32), 'keys': jax.random.normal(ks[1], (BATCH, SEQ, D_MODEL), jnp.float32), 'values': jax.random.normal(ks[2], (BATCH, SEQ, D_MODEL), jnp.float32), 'Wq': jax.random.normal(ks[3], (D_MODEL, D_MODEL), jnp.float32) * scale, 'Wk': jax.random.normal(ks[4], (D_MODEL, D_MODEL), jnp.float32) * scale, 'Wv': jax.random.normal(ks[5], (D_MODEL, D_MODEL), jnp.float32) * scale, 'Wo': jax.random.normal(ks[6], (D_MODEL, D_MODEL), jnp.float32) * scale, 'valid_lens': jax.random.randint(ks[7], (BATCH,), 1, SEQ + 1).astype(jnp.int64)}
    _L0_xattn_all = _L0_xattn_setup()
    _L0_xattn_in = {k: v for k, v in _L0_xattn_all.items() if k in ('Wq', 'Wk', 'Wv', 'Wo')}
    del _L0_xattn_all

    def _L0_ffn_setup():
        import jax, jax.numpy as jnp
        import numpy as np
        B, S, D, F, E = (1, 128, 128, 512, 8)
        EPS = 1e-05

        def _sublayer(xs, g, b, W1e, b1e, W2e, b2e):
            mu = jnp.mean(xs, axis=-1, keepdims=True)
            var = jnp.mean(jnp.square(xs - mu), axis=-1, keepdims=True)
            h = (xs - mu) * jax.lax.rsqrt(var + EPS) * g + b
            return xs + jax.nn.relu(h @ W1e.T + b1e) @ W2e.T + b2e
        key = jax.random.key(seed)
        ks = jax.random.split(key, 4)
        x = jax.random.normal(ks[0], (B, S, D), jnp.float32)
        centroids = jax.random.normal(ks[1], (E, D), jnp.float32) * 0.1
        gamma = jnp.ones((E, D), jnp.float32)
        beta = jnp.zeros((E, D), jnp.float32)
        W1 = jax.random.normal(ks[2], (E, F, D), jnp.float32) * 0.02
        b1 = jnp.zeros((E, F), jnp.float32)
        W2 = jax.random.normal(ks[3], (E, D, F), jnp.float32) * 0.02
        b2 = jnp.zeros((E, D), jnp.float32)
        return {'x': x, 'centroids': centroids, 'gamma': gamma, 'beta': beta, 'W1': W1, 'b1': b1, 'W2': W2, 'b2': b2}
    _L0_ffn_all = _L0_ffn_setup()
    _L0_ffn_in = {k: v for k, v in _L0_ffn_all.items() if k in ('centroids', 'gamma', 'beta', 'W1', 'b1', 'W2', 'b2')}
    del _L0_ffn_all
    return {'x': x, 'ctx_1024': ctx_1024, '_lenS2': _lenS2, 'L0_xattn_Wq': _L0_xattn_in['Wq'], 'L0_xattn_Wk': _L0_xattn_in['Wk'], 'L0_xattn_Wv': _L0_xattn_in['Wv'], 'L0_xattn_Wo': _L0_xattn_in['Wo'], 'L0_ffn_centroids': _L0_ffn_in['centroids'], 'L0_ffn_gamma': _L0_ffn_in['gamma'], 'L0_ffn_beta': _L0_ffn_in['beta'], 'L0_ffn_W1': _L0_ffn_in['W1'], 'L0_ffn_b1': _L0_ffn_in['b1'], 'L0_ffn_W2': _L0_ffn_in['W2'], 'L0_ffn_b2': _L0_ffn_in['b2']}

def reference(x, ctx_1024, _lenS2, L0_xattn_Wq, L0_xattn_Wk, L0_xattn_Wv, L0_xattn_Wo, L0_ffn_centroids, L0_ffn_gamma, L0_ffn_beta, L0_ffn_W1, L0_ffn_b1, L0_ffn_W2, L0_ffn_b2):
    import jax
    import jax.numpy as jnp

    def _L0_xattn_ref(queries, keys, values, Wq, Wk, Wv, Wo, valid_lens):
        import jax, jax.numpy as jnp
        import numpy as np
        import math
        NUM_HEADS = 16
        D_MODEL = 128
        BATCH = 4
        SEQ = 256
        NEG_INF = -1000000000.0
        B, S, D = queries.shape
        H = NUM_HEADS
        dh = D // H

        def split_heads(x, W):
            y = jnp.einsum('bsd,od->bso', x, W)
            return y.reshape(B, S, H, dh).transpose(0, 2, 1, 3)
        q = split_heads(queries, Wq)
        k = split_heads(keys, Wk)
        v = split_heads(values, Wv)
        scores = jnp.einsum('bhqd,bhkd->bhqk', q, k) / math.sqrt(dh)
        mask = jnp.arange(S)[None, None, None, :] >= valid_lens[:, None, None, None]
        scores = jnp.where(mask, NEG_INF, scores)
        attn = jax.nn.softmax(scores, axis=-1)
        out = jnp.einsum('bhqk,bhkd->bhqd', attn, v)
        out = out.transpose(0, 2, 1, 3).reshape(B, S, D)
        return jnp.einsum('bsd,od->bso', out, Wo)

    def _L0_ffn_ref(x, centroids, gamma, beta, W1, b1, W2, b2):
        import jax, jax.numpy as jnp
        import numpy as np
        B, S, D, F, E = (1, 128, 128, 512, 8)
        EPS = 1e-05

        def _sublayer(xs, g, b, W1e, b1e, W2e, b2e):
            mu = jnp.mean(xs, axis=-1, keepdims=True)
            var = jnp.mean(jnp.square(xs - mu), axis=-1, keepdims=True)
            h = (xs - mu) * jax.lax.rsqrt(var + EPS) * g + b
            return xs + jax.nn.relu(h @ W1e.T + b1e) @ W2e.T + b2e
        feats = x.reshape(-1, x.shape[-1])
        scores = jax.lax.stop_gradient(feats @ centroids.T)
        expert = jnp.argmax(scores, axis=1)
        onehot = jax.nn.one_hot(expert, E, dtype=feats.dtype)
        alpha = jax.nn.sigmoid(jnp.sum(feats * centroids[expert], axis=-1, keepdims=True))
        ys = jax.vmap(_sublayer, in_axes=(None, 0, 0, 0, 0, 0, 0))(feats, gamma, beta, W1, b1, W2, b2)
        y = jnp.einsum('te,etd->td', onehot, ys)
        out = alpha * y + (1.0 - alpha) * feats
        return out.reshape(x.shape)
    x = x + _L0_xattn_ref(_layernorm(x, axis=-1), ctx_1024, ctx_1024, L0_xattn_Wq, L0_xattn_Wk, L0_xattn_Wv, L0_xattn_Wo, _lenS2)
    x = x + _L0_ffn_ref(_layernorm(x, axis=-1), L0_ffn_centroids, L0_ffn_gamma, L0_ffn_beta, L0_ffn_W1, L0_ffn_b1, L0_ffn_W2, L0_ffn_b2)
    return x

_drawn_inputs = setup_inputs


def setup_inputs(seed=0):
    import zlib

    import numpy as np

    out = dict(_drawn_inputs(seed))
    spreads = {'L0_ffn_gamma': (1.0, 0.6),
     'L0_ffn_beta': (0.0, 2.0),
     'L0_ffn_b1': (0.0, 0.668),
     'L0_ffn_b2': (0.0, 0.1)}
    factors = {}
    for name, (base, spread) in spreads.items():
        noise = np.random.default_rng([zlib.crc32(name.encode()), seed]).standard_normal(out[name].shape)
        drawn = base * np.exp(spread * noise) if base else spread * noise
        out[name] = jnp.asarray(drawn.astype(out[name].dtype))
    for name, factor in factors.items():
        out[name] = (out[name] * factor).astype(out[name].dtype)
    return out
```

```python
import struct
from contextlib import ExitStack

import concourse.bass as bass
from concourse import mybir

F32 = mybir.dt.float32
BF16 = mybir.dt.bfloat16
I32 = mybir.dt.int32
ALU = mybir.AluOpType
ACT = mybir.ActivationFunctionType
AX = mybir.AxisListType


def xattn_ffn_kernel(nc, x_dram, ctx_dram, lens_dram, wq_dram, wk_dram, wv_dram, wo_dram,
                     cent_dram, gamma_dram, beta_dram, w1_dram, b1_dram, w2_dram, b2_dram, out_dram):
    B, S, D = x_dram.shape
    P = 128
    H, DH = 16, D // 16
    CB = 4
    NCH = B // CB
    TOK = CB * S
    SG = 4
    SLOTS = CB * (H // SG)
    NPAIR = H // 2
    NT = 6
    HROWS = NT * DH
    SROWS = 2 * HROWS
    MROWS = SROWS + 6
    VW = 32
    QSCALE = float(DH) ** -0.5
    EPS = 1e-5
    ONE_ONE = struct.unpack("<f", struct.pack("<I", 0x3F803F80))[0]
    E, F, _ = w1_dram.shape
    FC = F // P
    T = B * S
    NTILE = -(-(T // P + E - 1) // 4) * 4
    PW = 2 * D + 4
    GATE, TOKEN = 2 * D, 2 * D + 1
    NOWHERE = 1 << 20
    NRT = 17
    assert S == P and D == P and DH == 8

    es = ExitStack()
    with es:
        def sb(name, shape, dt=F32):
            return es.enter_context(nc.sbuf_tensor(name, shape, dt))

        def psum(name, shape, dt=F32):
            return es.enter_context(nc.psum_tensor(name, shape, dt))

        def sem(name):
            return es.enter_context(nc.semaphore(name))

        q_scr = nc.dram_tensor("q_scr", (P, NT, TOK), BF16, kind="Internal").ap()
        k_scr = nc.dram_tensor("k_scr", (P, NT, TOK), BF16, kind="Internal").ap()
        m_scr = nc.dram_tensor("m_scr", (96, S), BF16, kind="Internal").ap()

        routed = nc.dram_tensor("routed", (E * T + P, PW), F32, kind="Internal").ap()

        x_all = sb("x_all", [P, B, D])
        ctx_in = sb("ctx_in", [P, CB, D])
        ctx_first = sb("ctx_first", [P, CB, D])
        mask_chunk = sb("mask_chunk", [P, CB], I32)
        xn = sb("xn", [P, CB, D])
        xnT = sb("xnT", [P, TOK])
        ctxT = sb("ctxT", [P, TOK])
        q_parts = sb("q_parts", [P, 3, TOK], BF16)
        k_parts = sb("k_parts", [P, 3, TOK], BF16)
        q_rest = sb("q_rest", [P, TOK])
        k_rest = sb("k_rest", [P, TOK])
        q_stack = [sb(f"q_stack{i}", [P, NPAIR, 2, TOK], BF16) for i in range(2)]
        k_stack = [sb(f"k_stack{i}", [P, NPAIR, TOK], BF16) for i in range(2)]
        v_blk = [sb(f"v_blk{i}", [P, CB, H, VW]) for i in range(2)]
        e_ring = sb("e_ring", [P, 4, SG, S])
        oT_raw = sb("oT_raw", [P, 2, 4 * S])
        o_norm = sb("o_norm", [P, H, DH])
        oT_norm = sb("oT_norm", [P, S])
        z_inv = sb("z_inv", [P, H, 1])
        neg_max = sb("neg_max", [P, 2, H])
        m_parts = sb("m_parts", [P, 2, 2, 3, NPAIR], BF16)
        m_rest = sb("m_rest", [P, 2, 2, NPAIR])
        mT = sb("mT", [96, S], BF16)
        ident = sb("ident", [P, P])
        ident16 = sb("ident16", [P, P], BF16)
        w_raw = sb("w_raw", [P, 4, D])
        wT = sb("wT", [P, 4, D])
        stats = sb("stats", [P, B, 6])
        mean = sb("mean", [P, B])
        rstd = sb("rstd", [P, B])
        tmp_a = sb("tmp_a", [P, B])
        tmp_b = sb("tmp_b", [P, B])
        neg_half = sb("neg_half", [P, B])
        lens_i = sb("lens_i", [P, B], I32)
        lens_f = sb("lens_f", [P, B])
        key_id = sb("key_id", [P, 1])
        nonempty = sb("nonempty", [P, B])
        masked_f = sb("masked_f", [P, B])
        masked_i = sb("masked_i", [P, B], I32)
        keep = sb("keep", [P, B])

        w1_stage = [sb(f"w1_stage{i}", [P, FC, D]) for i in range(2)]
        w2_stage = [sb(f"w2_stage{i}", [P, F]) for i in range(2)]
        w1_rawT = [sb(f"w1_rawT{i}", [P, F]) for i in range(2)]
        beta_cols = [sb(f"beta_cols{i}", [P, P]) for i in range(2)]
        w1T = sb("w1T", [P, E, F])
        w2T = sb("w2T", [P, E, FC * D])
        b1_row = sb("b1_row", [P, E, F])
        b2_row = sb("b2_row", [P, E, D])
        gammaT = sb("gammaT", [P, E])
        betaT = sb("betaT", [P, E])
        cent = sb("cent", [E, D])
        centT = sb("centT", [P, E])
        f_stats = sb("f_stats", [P, CB, 6])
        f_mean = sb("f_mean", [P, CB])
        f_tmp = sb("f_tmp", [P, CB])
        f_var = sb("f_var", [P, CB])
        f_vare = sb("f_vare", [P, CB])
        f_rstd = sb("f_rstd", [P, CB])
        f_rz = sb("f_rz", [P, CB])
        p_tmp = sb("p_tmp", [P, CB])
        eps_t = sb("eps_t", [P, CB])
        feats = sb("feats", [P, CB, D])
        featsT = sb("featsT", [P, TOK])
        rows = sb("rows", [P, CB, PW])
        score = sb("score", [P, CB, E])
        best = sb("best", [P, CB, 1])
        gate_e = sb("gate_e", [P, CB, 1])
        choice = sb("choice", [P, CB, 1])
        cand = sb("cand", [P, CB, E])
        onehot = sb("onehot", [P, CB, E], BF16)
        before = sb("before", [P, CB + 1, E], BF16)
        place_f = sb("place_f", [P, CB, E])
        place = sb("place", [P, CB], I32)
        token_f = sb("token_f", [P, CB])
        expert_id = sb("expert_id", [P, E])
        expert_base = sb("expert_base", [P, E])
        upto = sb("upto", [P, P], BF16)
        ones16 = sb("ones16", [P, P], BF16)
        count = sb("count", [P, E])
        c_tmp = sb("c_tmp", [P, E])
        c_over = sb("c_over", [P, E])
        pad_place = sb("pad_place", [P, E], I32)
        tile_bound = sb("tile_bound", [P, T // P])
        has_tile = sb("has_tile", [P, E, T // P])
        tiles = sb("tiles", [P, E])
        ones_e = sb("ones_e", [P, E])
        tiles_to = sb("tiles_to", [P, E])
        tile_id = sb("tile_id", [P, NTILE])
        passed = sb("passed", [P, NTILE, E])
        tile_e = sb("tile_e", [P, NTILE, 1])
        tile_b = sb("tile_b", [P, NTILE, 1])
        tile_row = sb("tile_row", [P, NTILE], I32)
        tile_expert = sb("tile_expert", [P, NTILE], I32)
        empty = sb("empty", [P, PW])
        tile_in = [sb(f"tile_in{i}", [P, PW]) for i in range(4)]
        zT = [sb(f"zT{i}", [P, P]) for i in range(2)]
        hid = w1_rawT
        hidT = w2_stage
        y_sum = [sb(f"y_sum{i}", [P, D]) for i in range(2)]
        y_out = [sb(f"y_out{i}", [P, D]) for i in range(2)]

        s_bank = psum("s_bank", [P, 2, SG, S])
        st_bank = psum("st_bank", [P, 2, SG, S])
        pv_bank = psum("pv_bank", [P, 2, 4 * S])
        pj_bank = psum("pj_bank", [P, TOK])
        misc = psum("misc", [P, 512])
        mT_ps = misc[0:96, 0:S // 2].bitcast(BF16)

        names = ("weights_in ident_done x_in lens_in ctx_in_s wt_done wt_copied const_done mask_done "
                 "stats_done ln_step ln_pow ln_done xn_ready ctx_ready mchunk pj_done xT_ready ctxT_ready "
                 "q_hi k_hi q_rest_r k_rest_r q_mid k_mid q_lo k_lo keep_cols v_ready scr_written "
                 "stack_in s_done max_done m_hi m_rest1 m_mid m_rest2 mp_ready mt_done mT_ready m_written m_in "
                 "st_done exp_done pv_done otraw_ready oq_done zinv_ready on_ready onT_done onT_ready "
                 "wo_done x1_done out_done0 out_done1 stacks_init v_init pool_turn sp_turn "
                 "vec_in w_in0 w_in1 w1t_done w2t_done w1raw_ready w2T_ready beta_ready w1T_ready wb_done b1_ready "
                 "route_init route_step route_vars pl_step feats_ready base_ready fT_done fT_ready score_done "
                 "gate_exp place_ready onehot_ready rank_done rank_used scattered centT_done centT_ready "
                 "count_done table_step pad_ready padded table_ready tile_in0 tile_in1 tile_in2 tile_in3 empty_in "
                 "zt_done zT_ready up_done hid_ready ht_done hidT_ready down_done ysum_ready y_ready").split()
        s = {n: sem(n) for n in names}

        block = es.enter_context(nc.Block())

        CREDIT = 2
        PV_CREDIT = 4

        @block.sync
        def _(sp):
            sp.dma_start(lens_i[:, :], lens_dram.rearrange("(o b) -> o b", o=1).broadcast_to([P, B])).then_inc(s["lens_in"], 16)
            for g in range(4):
                sp.dma_start(x_all[:, 8 * g:8 * g + 8, :], x_dram[8 * g:8 * g + 8].rearrange("b t d -> t b d")).then_inc(s["x_in"], 16)
            for i, w in enumerate((wq_dram, wk_dram, wv_dram, wo_dram)):
                sp.dma_start(w_raw[:, i, :], w).then_inc(s["weights_in"], 16)

            with nc.allow_non_contiguous_dma(reason="8 x 128 values"):
                sp.dma_start(gammaT[:, :], gamma_dram.rearrange("e d -> d e")).then_inc(s["vec_in"], 16)
                sp.dma_start(betaT[:, :], beta_dram.rearrange("e d -> d e")).then_inc(s["vec_in"], 16)
            sp.dma_start(cent[:, :], cent_dram).then_inc(s["vec_in"], 16)

            def load_expert(t, r):
                e = 2 * t + r
                if not (isinstance(t, int) and t == 0):
                    sp.wait_ge(s["w2t_done"], e - 1)
                    sp.wait_ge(s["w1t_done"], e - 1)
                    sp.sem_inc(s["sp_turn"])
                sp.dma_start(w1_stage[r][:, :, :], w1_dram[bass.ds(e, 1)].rearrange("o (c f) d -> f (o c) d", f=P)).then_inc(s[f"w_in{r}"], 16)
                sp.dma_start(w2_stage[r][:, :], w2_dram[bass.ds(e, 1)].rearrange("o d f -> d (o f)")).then_inc(s[f"w_in{r}"], 16)

            def load_ctx(c):
                src = ctx_dram[bass.ds(CB * c, CB)]
                sp.dma_start(ctx_in[:, :, :], src.rearrange("b t d -> t b d")).then_inc(s["ctx_in_s"], 16)
                sp.dma_start(ctx_first[:, :, :], src[:, 0:1, :].rearrange("b o d -> o b d").broadcast_to([P, CB, D])).then_inc(s["ctx_in_s"], 16)

            m_rows_of = m_scr.rearrange("(b i p s) t -> i b p s t", b=2, i=2, p=3)

            def m_rows(c, bp, buf):
                sp.wait_ge(s["mT_ready"], 2 * c + bp + 1)
                sp.dma_start(m_scr, mT[:, :]).then_inc(s["m_written"], 16)
                sp.wait_ge(s["m_written"], 16 * (2 * c + bp + 1))
                for i in range(2):
                    for b in range(2):
                        sp.dma_start(q_stack[buf][SROWS + 3 * i:SROWS + 3 * i + 3, :, i, S * (2 * bp + b):S * (2 * bp + b + 1)],
                                     m_rows_of[i, b]).then_inc(s["m_in"], 16)
                sp.wait_ge(s["m_in"], 64 * (2 * c + bp + 1))
                sp.sem_inc(s["sp_turn"])

            load_ctx(0)
            load_expert(0, 0)
            load_expert(0, 1)
            sp.dma_start(b1_row[:, :, :], b1_dram.rearrange("(o e) f -> o e f", o=1).broadcast_to([P, E, F])).then_inc(s["vec_in"], 16)
            sp.dma_start(b2_row[:, :, :], b2_dram.rearrange("(o e) d -> o e d", o=1).broadcast_to([P, E, D])).then_inc(s["vec_in"], 16)

            def step(t, r, proj, sc, st, more):
                k = 2 * t + r
                if more:
                    sp.wait_ge(s["pj_done"], 5 * k + 2)
                    sp.sem_inc(s["sp_turn"])
                    load_ctx(k + 1)
                if proj:
                    sp.wait_ge(s["q_lo"], k + 1)
                    sp.wait_ge(s["k_lo"], k + 1)
                    qs = q_parts
                    sp.dma_start(q_scr[:, 0:3, :], q_parts[:, 0:1, :].broadcast_to([P, 3, TOK])).then_inc(s["scr_written"], 16)
                    sp.dma_start(q_scr[:, 3:5, :], q_parts[:, 1:2, :].broadcast_to([P, 2, TOK])).then_inc(s["scr_written"], 16)
                    sp.dma_start(q_scr[:, 5:6, :], q_parts[:, 2:3, :]).then_inc(s["scr_written"], 16)
                    sp.dma_start(k_scr[:, 0:3, :], k_parts[:, 0:3, :]).then_inc(s["scr_written"], 16)
                    sp.dma_start(k_scr[:, 3:5, :], k_parts[:, 0:2, :]).then_inc(s["scr_written"], 16)
                    sp.dma_start(k_scr[:, 5:6, :], k_parts[:, 0:1, :]).then_inc(s["scr_written"], 16)
                    sp.wait_ge(s["scr_written"], 96 * (k + 1))
                    sp.sem_inc(s["sp_turn"])
                if sc:
                    m_rows(k - 1, 0, (r + 1) % 2)
                if proj:
                    if st:
                        sp.wait_ge(s["st_done"], SLOTS * (k - 1))
                    q_rows = q_scr.rearrange("(s i d) c t -> i (d c) s t", i=2, d=DH)
                    for i in range(2):
                        sp.dma_start(q_stack[r][HROWS * i:HROWS * (i + 1), :, i, :], q_rows[i]).then_inc(s["stack_in"], 16)
                    sp.dma_start(k_stack[r][0:SROWS, :, :], k_scr.rearrange("(s i) c t -> (i c) s t", i=16)).then_inc(s["stack_in"], 16)
                    sp.wait_ge(s["stack_in"], 48 * (k + 1))
                    sp.sem_inc(s["sp_turn"])
                if sc:
                    m_rows(k - 1, 1, (r + 1) % 2)

            sp.wait_ge(s["stacks_init"], 4)
            step(0, 0, True, False, False, True)
            with sp.Fori(1, E // 2) as t:
                load_expert(t, 0)
                load_expert(t, 1)
            sp.wait_ge(s["route_init"], 1)
            sp.dma_start(routed[E * T:E * T + P, :], empty[:, :]).then_inc(s["empty_in"], 16)
            step(0, 1, True, True, False, True)
            with sp.Fori(1, NCH // 2 - 1) as t:
                step(t, 0, True, True, True, True)
                step(t, 1, True, True, True, True)
            step(NCH // 2 - 1, 0, True, True, True, True)
            step(NCH // 2 - 1, 1, True, True, True, False)
            step(NCH // 2, 0, False, True, True, False)

            sp.wait_ge(s["empty_in"], 16)
            sp.wait_ge(s["scattered"], 16 * B)
            sp.wait_ge(s["padded"], 16 * E)
            sp.wait_ge(s["table_ready"], 1)

            def load_tile(t, q):
                i = 4 * t + q
                if not (isinstance(t, int) and t == 0):
                    sp.wait_ge(s["y_ready"], i - 3)
                    sp.sem_inc(s["sp_turn"])
                    sp.wait_ge(s[f"out_done{q % 2}"], 16 * (2 * t + q // 2 - 1))
                    sp.sem_inc(s["sp_turn"])
                row = sp.value_load(tile_row[0:1, bass.ds(i, 1)], min_val=0, max_val=E * T)
                sp.dma_start(tile_in[q][:, :], routed[bass.ds(row, P), :]).then_inc(s[f"tile_in{q}"], 16)

            for q in range(4):
                load_tile(0, q)
            with sp.Fori(1, NTILE // 4) as t:
                for q in range(4):
                    load_tile(t, q)
            for q in range(2):
                sp.wait_ge(s[f"out_done{q}"], 16 * (NTILE // 2))

        @block.gpsimd
        def _(pool):
            for m in (ident, ident16):
                pool.memset(m[:, :], 0.0).then_inc(s["ident_done"], 1)
            pool.wait_ge(s["ident_done"], 2)
            for m in (ident, ident16):
                pool.affine_select(out=m[:, :], in_=m[:, :], compare_op=ALU.not_equal, fill=1.0, base=0,
                                   pattern=[[-1, P]], channel_multiplier=1).then_inc(s["ident_done"], 1)
            pool.iota(key_id[:, :], pattern=[[0, 1]], base=0, channel_multiplier=1,
                      allow_small_or_imprecise_dtypes=True).then_inc(s["const_done"], 1)
            pool.memset(neg_half[:, :], -0.5).then_inc(s["const_done"], 1)
            for i in range(2):
                pool.memset(v_blk[i][:, :, :, :], 0.0).then_inc(s["v_init"], 1)
            pool.memset(empty[:, :], 0.0).then_inc(s["pool_turn"], 1)
            pool.wait_ge(s["pool_turn"], 1)
            pool.memset(empty[:, TOKEN:TOKEN + 1].bitcast(I32), NOWHERE).then_inc(s["route_init"], 1)
            pool.wait_ge(s["const_done"], 2)
            pool.wait_ge(s["ln_step"], 5)
            pool.tensor_tensor(rstd[:, :], tmp_b[:, :], neg_half[:, :], ALU.pow).then_inc(s["ln_pow"], 1)
            pool.wait_ge(s["mask_done"], 1)
            pool.wait_ge(s["v_init"], 2)
            pool.memset(eps_t[:, :], EPS)
            pool.memset(ones16[:, :], 1.0)
            pool.memset(ones_e[:, :], 1.0)
            pool.memset(before[:, :, :], 0.0)
            pool.memset(rows[:, :, :], 0.0)
            pool.memset(upto[:, :], 1.0).then_inc(s["route_init"], 1)
            pool.wait_ge(s["route_init"], 2)
            pool.affine_select(out=upto[:, :], in_=upto[:, :], compare_op=ALU.is_gt, fill=0.0, base=0,
                               pattern=[[1, P]], channel_multiplier=-1)
            pool.iota(expert_id[:, :], pattern=[[1, E]], base=0, channel_multiplier=0, allow_small_or_imprecise_dtypes=True)
            pool.iota(expert_base[:, :], pattern=[[T, E]], base=0, channel_multiplier=0, allow_small_or_imprecise_dtypes=True)
            pool.iota(tile_bound[:, :], pattern=[[P, T // P]], base=0, channel_multiplier=0, allow_small_or_imprecise_dtypes=True)
            pool.iota(tile_id[:, :], pattern=[[1, NTILE]], base=0, channel_multiplier=0, allow_small_or_imprecise_dtypes=True)
            pool.iota(token_f[:, :], pattern=[[S, CB]], base=0, channel_multiplier=1,
                      allow_small_or_imprecise_dtypes=True).then_inc(s["route_init"], 1)
            pool.wait_ge(s["route_init"], 3)

            def route_vars(c):
                n = 6 * c
                pool.wait_ge(s["route_vars"], c + 1)
                pool.tensor_tensor(f_rstd[:, :], f_vare[:, :], neg_half[:, 0:CB], ALU.pow).then_inc(s["pl_step"], 1)
                pool.wait_ge(s["pl_step"], n + 1)
                pool.tensor_tensor(p_tmp[:, :], f_rstd[:, :], f_rstd[:, :], ALU.mult).then_inc(s["pl_step"], 1)
                pool.wait_ge(s["pl_step"], n + 2)
                pool.tensor_tensor(p_tmp[:, :], p_tmp[:, :], f_tmp[:, :], ALU.mult).then_inc(s["pl_step"], 1)
                pool.wait_ge(s["pl_step"], n + 3)
                pool.tensor_tensor(p_tmp[:, :], p_tmp[:, :], eps_t[:, :], ALU.add).then_inc(s["pl_step"], 1)
                pool.wait_ge(s["pl_step"], n + 4)
                pool.tensor_tensor(p_tmp[:, :], p_tmp[:, :], neg_half[:, 0:CB], ALU.pow).then_inc(s["pl_step"], 1)
                pool.wait_ge(s["pl_step"], n + 5)
                pool.tensor_tensor(f_rz[:, :], p_tmp[:, :], f_rstd[:, :], ALU.mult).then_inc(s["pl_step"], 1)

            def residual(c, known):
                if not (known and c == 0):
                    pool.wait_ge(s["scattered"], 16 * CB * c)
                pool.wait_ge(s["feats_ready"], c + 1)
                pool.tensor_tensor(rows[:, :, D:2 * D], feats[:, :, :], x_all[:, bass.ds(CB * c, CB), :], ALU.add).then_inc(s["base_ready"], 1)

            def scatter(c):
                pool.wait_ge(s["base_ready"], c + 1)
                pool.wait_ge(s["place_ready"], c + 1)
                pool.sem_inc(s["pool_turn"])
                for b in range(CB):
                    pool.indirect_dma_start(out=routed, out_offset=bass.IndirectOffsetOnAxis(ap=place[:, b:b + 1], axis=0),
                                            in_=rows[:, b, :], in_offset=None).then_inc(s["scattered"], 16)

            def step(t, r, proj, rt):
                k = 2 * t + r
                known = isinstance(t, int)
                first = known and k == 0
                if rt:
                    route_vars(k - 3)
                if proj:
                    low_parts(t, r, k, first)
                if rt:
                    residual(k - 3, known)
                if proj:
                    keep_columns(t, r, k)
                if rt:
                    scatter(k - 3)

            def low_parts(t, r, k, first):
                for j, (parts, rest, ready, mid, lo) in enumerate(((q_parts, q_rest, "q_rest_r", "q_mid", "q_lo"),
                                                    (k_parts, k_rest, "k_rest_r", "k_mid", "k_lo"))):
                    pool.wait_ge(s[ready], k + 1)
                    if not first:
                        pool.wait_ge(s["scr_written"], 96 * k)
                    pool.sem_inc(s["pool_turn"])
                    pool.tensor_copy(parts[:, 1, :], rest[:, :]).then_inc(s[mid], 1)
                    pool.wait_ge(s[mid], k + 1)
                    pool.tensor_tensor(parts[:, 2, :], rest[:, :], parts[:, 1, :], ALU.subtract).then_inc(s[lo], 1)

            def keep_columns(t, r, k):
                if not (isinstance(t, int) and t == 0):
                    pool.wait_ge(s["pv_done"], PV_CREDIT + SLOTS * (k - 1))
                pool.sem_inc(s["pool_turn"])
                pool.tensor_copy(v_blk[r][:, :, :, DH:2 * DH],
                                 keep[:, bass.ds(CB * k, CB)].unsqueeze(2).unsqueeze(3).broadcast_to([P, CB, H, DH])).then_inc(s["keep_cols"], 1)

            step(0, 0, True, False)
            step(0, 1, True, False)
            step(1, 0, True, False)
            step(1, 1, True, True)
            with pool.Fori(2, NCH // 2) as t:
                step(t, 0, True, True)
                step(t, 1, True, True)
            step(NCH // 2, 0, False, True)
            step(NCH // 2, 1, False, True)
            step(NCH // 2 + 1, 0, False, True)
            pool.wait_ge(s["pad_ready"], 1)
            for e in range(E):
                pool.indirect_dma_start(out=routed, out_offset=bass.IndirectOffsetOnAxis(ap=pad_place[:, e:e + 1], axis=0),
                                        in_=empty[:, :], in_offset=None, bounds_check=E * T - 1, oob_is_err=False).then_inc(s["padded"], 16)

            out_rows = out_dram.rearrange("b t d -> (b t) d")

            def store(t, q):
                pool.wait_ge(s["y_ready"], 4 * t + q + 1)
                pool.sem_inc(s["pool_turn"])
                pool.indirect_dma_start(out=out_rows, out_offset=bass.IndirectOffsetOnAxis(ap=tile_in[q][:, TOKEN:TOKEN + 1].bitcast(I32), axis=0),
                                        in_=y_out[q % 2][:, :], in_offset=None, bounds_check=T - 1, oob_is_err=False).then_inc(s[f"out_done{q % 2}"], 16)

            with pool.Fori(0, NTILE // 4) as t:
                for q in range(4):
                    store(t, q)

        @block.scalar
        def _(act):
            act.sem_inc(s["exp_done"], CREDIT)
            act.sem_inc(s["otraw_ready"], CREDIT)
            act.wait_ge(s["wt_done"], 1)
            act.activation(wT[:, :, :].rearrange("p a b -> p (a b)"), pj_bank[:, :], ACT.Copy).then_inc(s["wt_copied"], 1)

            act.wait_ge(s["centT_done"], 1)
            act.activation(centT[:, :], pj_bank[:, 0:E], ACT.Copy).then_inc(s["centT_ready"], 1)

            def expert_weights(t, r):
                e = 2 * t + r
                late = not (isinstance(t, int) and t == 0)
                act.wait_ge(s["w1t_done"], e + 1)
                if late:
                    act.wait_ge(s["wb_done"], e - 1)
                    act.wait_ge(s["w1T_ready"], e - 1)
                act.activation(w1_rawT[r][:, :], st_bank[:, r].rearrange("p a b -> p (a b)"), ACT.Copy).then_inc(s["w1raw_ready"], 1)
                act.wait_ge(s["w2t_done"], e + 1)
                act.activation(w2T[:, bass.ds(e, 1), :].rearrange("p o n -> p (o n)"), s_bank[:, r].rearrange("p a b -> p (a b)"),
                               ACT.Copy).then_inc(s["w2T_ready"], 1)

            def step(t, r, proj, sc, st, rt=False):
                k = 2 * t + r
                known = isinstance(t, int)
                for pos in range(23):
                    if rt and pos == 6:
                        act.wait_ge(s["fT_done"], k - 2)
                        if not (known and k == 3):
                            act.wait_ge(s["score_done"], k - 3)
                        act.activation(featsT[:, :], pj_bank[:, :], ACT.Copy).then_inc(s["fT_ready"], 1)
                    if rt and pos == 10:
                        act.wait_ge(s["route_step"], NRT * (k - 3) + 6)
                        act.activation(gate_e[:, :, :], best[:, :, :], ACT.Exp, scale=-1.0).then_inc(s["gate_exp"], 1)
                    if st and pos < SLOTS:
                        act.wait_ge(s["st_done"], SLOTS * (k - 2) + pos + 1)
                        act.wait_ge(s["pv_done"], SLOTS * (k - 2) + pos + 1)
                        act.activation(e_ring[:, pos % 4], st_bank[:, pos % 2], ACT.Exp).then_inc(s["exp_done"], 1)
                    if proj and pos == 0:
                        act.wait_ge(s["pj_done"], 5 * k + 1)
                        act.activation(xnT[:, :], pj_bank[:, :], ACT.Copy).then_inc(s["xT_ready"], 1)
                    if proj and pos == 1:
                        act.wait_ge(s["pj_done"], 5 * k + 2)
                        act.activation(ctxT[:, :], pj_bank[:, :], ACT.Copy).then_inc(s["ctxT_ready"], 1)
                    if proj and pos == 2:
                        act.wait_ge(s["pj_done"], 5 * k + 3)
                        if not (known and k == 0):
                            act.wait_ge(s["scr_written"], 96 * k)
                        act.activation(q_parts[:, 0, :], pj_bank[:, :], ACT.Copy, scale=QSCALE).then_inc(s["q_hi"], 1)
                    if proj and pos == 3:
                        act.wait_ge(s["pj_done"], 5 * k + 4)
                        act.activation(k_parts[:, 0, :], pj_bank[:, :], ACT.Copy).then_inc(s["k_hi"], 1)
                    if st and pos in (5, 9, 13, 17):
                        b = (pos - 5) // 4
                        act.wait_ge(s["pv_done"], PV_CREDIT + SLOTS * (k - 2) + 4 * b + 4)
                        act.wait_ge(s["oq_done"], CB * (k - 2) + b + 1)
                        act.activation(oT_raw[:, b % 2, :], pv_bank[:, b % 2, :], ACT.Copy).then_inc(s["otraw_ready"], 1)
                    if sc and pos in (14, 22):
                        bp = (pos - 14) // 8
                        act.wait_ge(s["mt_done"], 2 * (k - 1) + bp + 1)
                        if not (known and k - 1 == 0 and bp == 0):
                            act.wait_ge(s["m_written"], 16 * (2 * (k - 1) + bp))
                        act.activation(mT[:, :], mT_ps, ACT.Copy).then_inc(s["mT_ready"], 1)
                    if proj and pos == 19:
                        act.wait_ge(s["pj_done"], 5 * k + 5)
                        act.wait_ge(s["mask_done"], 1)
                        act.wait_ge(s["v_init"], 2)
                        if not (known and t == 0):
                            act.wait_ge(s["pv_done"], PV_CREDIT + SLOTS * (k - 1))
                        for b in range(CB):
                            act.activation(v_blk[r][:, b, :, 0:DH], pj_bank[:, S * b:S * (b + 1)].rearrange("p (h d) -> p h d", h=H),
                                           ACT.Copy, scale=keep[:, bass.ds(CB * k + b, 1)]).then_inc(s["v_ready"], 1)

            step(0, 0, True, False, False)
            expert_weights(0, 0)
            expert_weights(0, 1)
            with act.Fori(1, E // 2) as t:
                expert_weights(t, 0)
                expert_weights(t, 1)
            step(0, 1, True, True, False)
            step(1, 0, True, True, True)
            step(1, 1, True, True, True, True)
            with act.Fori(2, NCH // 2) as t:
                step(t, 0, True, True, True, True)
                step(t, 1, True, True, True, True)
            step(NCH // 2, 0, False, True, True, True)
            step(NCH // 2, 1, False, False, True, True)
            step(NCH // 2 + 1, 0, False, False, False, True)

            def hidden(t, q):
                i = 4 * t + q
                act.wait_ge(s["ht_done"], i + 1)
                if not (isinstance(t, int) and i < 2):
                    act.wait_ge(s["down_done"], i - 1)
                act.activation(hidT[q % 2][:, :], st_bank[:, q % 2].rearrange("p a b -> p (a b)"), ACT.Relu).then_inc(s["hidT_ready"], 1)

            for q in range(4):
                hidden(0, q)
            with act.Fori(1, NTILE // 4) as t:
                for q in range(4):
                    hidden(t, q)

        @block.vector
        def _(dve):
            dve.sem_inc(s["max_done"], CREDIT)
            dve.sem_inc(s["x1_done"], 1)
            for i in range(2):
                dve.memset(q_stack[i][:, :, :, :].rearrange("p a b t -> p (a b t)").bitcast(F32), 0.0).then_inc(s["stacks_init"], 1)
                dve.memset(k_stack[i][SROWS:MROWS, :, :].rearrange("p s t -> p (s t)").bitcast(F32), ONE_ONE).then_inc(s["stacks_init"], 1)
            dve.wait_ge(s["lens_in"], 16)
            dve.wait_ge(s["const_done"], 1)
            dve.tensor_copy(lens_f[:, :], lens_i[:, :]).then_inc(s["mchunk"], 1)
            dve.wait_ge(s["mchunk"], 1)
            dve.tensor_scalar(nonempty[:, :], lens_f[:, :], 0.0, None, ALU.is_gt).then_inc(s["mchunk"], 1)
            dve.tensor_scalar(masked_f[:, :], lens_f[:, :], key_id[:, 0:1], None, ALU.is_le).then_inc(s["mchunk"], 1)
            dve.wait_ge(s["mchunk"], 3)
            dve.tensor_tensor(tmp_a[:, :], masked_f[:, :], nonempty[:, :], ALU.mult).then_inc(s["mchunk"], 1)
            dve.wait_ge(s["mchunk"], 4)
            dve.tensor_copy(masked_i[:, :], tmp_a[:, :]).then_inc(s["mchunk"], 1)
            dve.tensor_scalar(keep[:, :], tmp_a[:, :], -1.0, 1.0, ALU.mult, ALU.add).then_inc(s["mask_done"], 1)
            dve.wait_ge(s["x_in"], 64)
            with dve.Fori(0, B) as b:
                dve.bn_stats(stats[:, bass.ds(b, 1), :], x_all[:, bass.ds(b, 1), :]).then_inc(s["stats_done"], 1)
            dve.wait_ge(s["stats_done"], B)
            dve.wait_ge(s["mask_done"], 1)
            dve.tensor_tensor(mean[:, :], stats[:, :, 1], stats[:, :, 4], ALU.add).then_inc(s["ln_step"], 1)
            dve.tensor_tensor(tmp_a[:, :], stats[:, :, 1], stats[:, :, 4], ALU.subtract).then_inc(s["ln_step"], 1)
            dve.tensor_tensor(tmp_b[:, :], stats[:, :, 2], stats[:, :, 5], ALU.add).then_inc(s["ln_step"], 1)
            dve.wait_ge(s["ln_step"], 3)
            dve.scalar_tensor_tensor(out=tmp_a[:, :], in0=tmp_a[:, :], scalar=D / 4.0, in1=tmp_a[:, :], op0=ALU.mult, op1=ALU.mult).then_inc(s["ln_step"], 1)
            dve.tensor_scalar(mean[:, :], mean[:, :], 0.5, None, ALU.mult).then_inc(s["ln_done"], 1)
            dve.wait_ge(s["ln_step"], 4)
            dve.tensor_tensor(tmp_b[:, :], tmp_b[:, :], tmp_a[:, :], ALU.add).then_inc(s["ln_done"], 1)
            dve.wait_ge(s["ln_done"], 2)
            dve.tensor_scalar(tmp_b[:, :], tmp_b[:, :], 1.0 / D, EPS, ALU.mult, ALU.add).then_inc(s["ln_step"], 1)
            dve.wait_ge(s["ln_pow"], 1)
            dve.tensor_tensor(rstd[:, :], rstd[:, :], nonempty[:, :], ALU.mult).then_inc(s["ln_done"], 1)
            dve.wait_ge(s["ln_done"], 3)

            def prepare(c):
                dve.tensor_copy(mask_chunk[:, :], masked_i[:, bass.ds(CB * c, CB)]).then_inc(s["mchunk"], 1)
                dve.wait_ge(s["mchunk"], 6 + c)
                dve.wait_ge(s["ctx_in_s"], 32 * (c + 1))
                for b in range(CB):
                    last = dve.tensor_scalar(xn[:, b, :], x_all[:, bass.ds(CB * c + b, 1), :], mean[:, bass.ds(CB * c + b, 1)],
                                             rstd[:, bass.ds(CB * c + b, 1)], ALU.subtract, ALU.mult)
                last.then_inc(s["xn_ready"], 1)
                dve.copy_predicated(ctx_in[:, :, :], mask_chunk[:, :].unsqueeze(2).broadcast_to([P, CB, D]), ctx_first[:, :, :]).then_inc(s["ctx_ready"], 1)

            prepare(0)

            def max_parts(c, bp, known):
                nm = neg_max[:, :, :].rearrange("q b (s i) -> q b i s", i=2)
                dve.wait_ge(s["max_done"], CREDIT + SLOTS * c + 8 * bp + 8)
                if not (known and c == 0 and bp == 0):
                    dve.wait_ge(s["mt_done"], 2 * c + bp)
                n = 2 * c + bp + 1
                dve.tensor_copy(m_parts[:, :, :, 0, :], nm).then_inc(s["m_hi"], 1)
                dve.wait_ge(s["m_hi"], n)
                dve.tensor_tensor(m_rest[:, :, :, :], nm, m_parts[:, :, :, 0, :], ALU.subtract).then_inc(s["m_rest1"], 1)
                dve.wait_ge(s["m_rest1"], n)
                dve.tensor_copy(m_parts[:, :, :, 1, :], m_rest[:, :, :, :]).then_inc(s["m_mid"], 1)
                dve.wait_ge(s["m_mid"], n)
                dve.tensor_tensor(m_parts[:, :, :, 2, :], m_rest[:, :, :, :], m_parts[:, :, :, 1, :], ALU.subtract).then_inc(s["mp_ready"], 1)

            def expert_weights(t, r):
                e = 2 * t + r
                late = not (isinstance(t, int) and t == 0)
                if late:
                    dve.wait_ge(s["wb_done"], e - 1)
                dve.tensor_copy(beta_cols[r][:, :], betaT[:, bass.ds(e, 1)].broadcast_to([P, P])).then_inc(s["beta_ready"], 1)
                dve.wait_ge(s["w1raw_ready"], e + 1)
                dve.tensor_scalar(w1T[:, bass.ds(e, 1), :].rearrange("p o n -> p (o n)"), w1_rawT[r][:, :], gammaT[:, bass.ds(e, 1)], None,
                                  ALU.mult).then_inc(s["w1T_ready"], 1)
                dve.wait_ge(s["wb_done"], e + 1)
                br = b1_row[:, bass.ds(e, 1), :].rearrange("p o n -> p (o n)")
                dve.tensor_tensor(br, pv_bank[:, r, :], br, ALU.add).then_inc(s["b1_ready"], 1)

            def route(c, known, part, chain=[0]):
                def link(ins):
                    chain[0] += 1
                    ins.then_inc(s["route_step"], 1)
                    dve.wait_ge(s["route_step"], NRT * c + chain[0])

                if part == 0:
                    chain[0] = 0
                    dve.wait_ge(s["x1_done"], 1 + CB * (c + 1))
                    for b in range(CB):
                        last = dve.bn_stats(f_stats[:, b, :], x_all[:, bass.ds(CB * c + b, 1), :])
                    link(last)
                    dve.tensor_tensor(f_mean[:, :], f_stats[:, :, 1], f_stats[:, :, 4], ALU.add)
                    dve.tensor_tensor(f_tmp[:, :], f_stats[:, :, 1], f_stats[:, :, 4], ALU.subtract)
                    link(dve.tensor_tensor(f_var[:, :], f_stats[:, :, 2], f_stats[:, :, 5], ALU.add))
                    dve.tensor_scalar(f_mean[:, :], f_mean[:, :], 0.5, None, ALU.mult)
                    link(dve.scalar_tensor_tensor(out=f_tmp[:, :], in0=f_tmp[:, :], scalar=D / 4.0, in1=f_tmp[:, :], op0=ALU.mult, op1=ALU.mult))
                    link(dve.tensor_tensor(f_var[:, :], f_var[:, :], f_tmp[:, :], ALU.add))
                    dve.tensor_scalar(f_vare[:, :], f_var[:, :], 1.0 / D, EPS, ALU.mult, ALU.add)
                    dve.tensor_scalar(f_tmp[:, :], f_var[:, :], 1.0 / D, None, ALU.mult).then_inc(s["route_vars"], 1)
                if part == 1:
                    dve.wait_ge(s["pl_step"], 6 * (c + 1))
                    if not (known and c == 0):
                        dve.wait_ge(s["base_ready"], c)
                        dve.wait_ge(s["scattered"], 16 * CB * c)
                    xs = [x_all[:, bass.ds(CB * c + b, 1), :].rearrange("p o d -> p (o d)") for b in range(CB)]
                    for b in range(CB):
                        last = dve.tensor_scalar(feats[:, b, :], xs[b], f_mean[:, b:b + 1], f_rstd[:, b:b + 1], ALU.subtract, ALU.mult)
                    last.then_inc(s["feats_ready"], 1)
                    for b in range(CB):
                        dve.tensor_scalar(rows[:, b, 0:D], xs[b], f_mean[:, b:b + 1], f_rz[:, b:b + 1], ALU.subtract, ALU.mult)
                if part == 2:
                    dve.wait_ge(s["score_done"], c + 1)
                    wide = [P, CB, E]
                    link(dve.tensor_copy(score[:, :, :], pj_bank[:, 0:CB * E].rearrange("p (b e) -> p b e", e=E)))
                    link(dve.tensor_reduce(best[:, :, 0], score[:, :, :], AX.X, ALU.max))
                    link(dve.tensor_tensor(cand[:, :, :], score[:, :, :], best[:, :, :].broadcast_to(wide), ALU.is_lt))
                    link(dve.scalar_tensor_tensor(out=cand[:, :, :], in0=cand[:, :, :], scalar=float(E), in1=expert_id[:, :].unsqueeze(1).broadcast_to(wide),
                                                  op0=ALU.mult, op1=ALU.add))
                    link(dve.tensor_reduce(choice[:, :, 0], cand[:, :, :], AX.X, ALU.min))
                    if not (known and c == 0):
                        dve.wait_ge(s["rank_done"], c)
                    link(dve.tensor_tensor(onehot[:, :, :], choice[:, :, :].broadcast_to(wide), expert_id[:, :].unsqueeze(1).broadcast_to(wide), ALU.is_equal))
                    link(dve.tensor_copy(before[:, 0, :], before[:, CB, :]))
                    for b in range(CB):
                        link(dve.tensor_tensor(before[:, b + 1, :], before[:, b, :], onehot[:, b, :], ALU.add))
                if part == 3:
                    dve.wait_ge(s["rank_done"], c + 1)
                    link(dve.tensor_tensor(place_f[:, :, :], pj_bank[:, 64:64 + CB * E].rearrange("p (b e) -> p b e", e=E),
                                           expert_base[:, :].unsqueeze(1).broadcast_to([P, CB, E]), ALU.add))
                    dve.wait_ge(s["gate_exp"], c + 1)
                    dve.tensor_scalar(gate_e[:, :, :], gate_e[:, :, :], 1.0, None, ALU.add)
                    link(dve.tensor_tensor(place_f[:, :, :], place_f[:, :, :], onehot[:, :, :], ALU.mult))
                    dve.reciprocal(rows[:, :, GATE:GATE + 1], gate_e[:, :, :])
                    dve.tensor_copy(rows[:, :, TOKEN].bitcast(I32), token_f[:, :]).then_inc(s["rank_used"], 1)
                    dve.wait_ge(s["rank_used"], c + 1)
                    dve.tensor_scalar(token_f[:, :], token_f[:, :], float(TOK), None, ALU.add)
                    with nc.allow_low_precision(reason="whole numbers below 2**24, one of them not zero"):
                        dve.tensor_reduce(place[:, :], place_f[:, :, :], AX.X, ALU.add).then_inc(s["place_ready"], 1)
                    assert chain[0] == NRT

            def step(t, r, proj, sc, st, more, rt=False):
                k = 2 * t + r
                known = isinstance(t, int)
                for pos in range(23):
                    if rt and pos in (0, 4, 9, 13):
                        route(k - 3, known, (0, 4, 9, 13).index(pos))
                    if sc and 5 <= pos < 5 + SLOTS:
                        n = pos - 5
                        dve.wait_ge(s["s_done"], SLOTS * (k - 1) + n + 1)
                        if n % 8 == 0 and not (known and k == 1 and n == 0):
                            dve.wait_ge(s["mp_ready"], 2 * (k - 1) + n // 8)
                        dve.tensor_reduce(neg_max[:, (n // 4) % 2, SG * (n % 4):SG * (n % 4 + 1)], s_bank[:, n % 2], AX.X, ALU.max,
                                          negate=True).then_inc(s["max_done"], 1)
                        if n % 8 == 7:
                            max_parts(k - 1, n // 8, known)
                    if proj and pos == 3:
                        dve.wait_ge(s["q_hi"], k + 1)
                        if not (known and k == 0):
                            dve.wait_ge(s["q_lo"], k)
                        dve.scalar_tensor_tensor(out=q_rest[:, :], in0=pj_bank[:, :], scalar=QSCALE, in1=q_parts[:, 0, :],
                                                 op0=ALU.mult, op1=ALU.subtract).then_inc(s["q_rest_r"], 1)
                    if proj and pos == 4:
                        dve.wait_ge(s["k_hi"], k + 1)
                        if not (known and k == 0):
                            dve.wait_ge(s["k_lo"], k)
                        dve.tensor_tensor(k_rest[:, :], pj_bank[:, :], k_parts[:, 0, :], ALU.subtract).then_inc(s["k_rest_r"], 1)
                    if st and pos >= 7:
                        b, what = (pos - 7) // 4, (pos - 7) % 4
                        cc = CB * (k - 2)
                        if what == 0:
                            oq = misc[:, :].rearrange("q (h w) -> q h w", w=VW)
                            dve.wait_ge(s["oq_done"], CREDIT + cc + b + 1)
                            dve.reciprocal(z_inv[:, :, :], oq[:, :, DH:DH + 1]).then_inc(s["zinv_ready"], 1)
                            dve.wait_ge(s["zinv_ready"], cc + b + 1)
                            dve.wait_ge(s["onT_done"], 1 + cc + b)
                            dve.tensor_tensor(o_norm[:, :, :], oq[:, :, 0:DH], z_inv[:, :, :].broadcast_to([P, H, DH]), ALU.mult).then_inc(s["on_ready"], 1)
                        if what == 1:
                            dve.wait_ge(s["onT_done"], 1 + cc + b + 1)
                            dve.tensor_copy(oT_norm[:, :], misc[:, 0:S]).then_inc(s["onT_ready"], 1)
                        if what == 2:
                            dve.wait_ge(s["wo_done"], cc + b + 1)
                            xr = x_all[:, bass.ds(CB * (k - 2) + b, 1), :].rearrange("p o d -> p (o d)")
                            dve.tensor_tensor(xr, misc[:, S:2 * S], xr, ALU.add).then_inc(s["x1_done"], 1)
                    if more and pos == 17:
                        dve.wait_ge(s["pj_done"], 5 * k + 2)
                        prepare(k + 1)

            step(0, 0, True, False, False, True)
            dve.wait_ge(s["vec_in"], 80)
            expert_weights(0, 0)
            expert_weights(0, 1)
            with dve.Fori(1, E // 2) as t:
                expert_weights(t, 0)
                expert_weights(t, 1)
            dve.wait_ge(s["route_init"], 3)
            step(0, 1, True, True, False, True)
            step(1, 0, True, True, True, True)
            step(1, 1, True, True, True, True, True)
            with dve.Fori(2, NCH // 2 - 1) as t:
                step(t, 0, True, True, True, True, True)
                step(t, 1, True, True, True, True, True)
            step(NCH // 2 - 1, 0, True, True, True, True, True)
            step(NCH // 2 - 1, 1, True, True, True, False, True)
            step(NCH // 2, 0, False, True, True, False, True)
            step(NCH // 2, 1, False, False, True, False, True)
            step(NCH // 2 + 1, 0, False, False, False, False, True)

            n = [0]

            def link(ins):
                n[0] += 1
                ins.then_inc(s["table_step"], 1)
                dve.wait_ge(s["table_step"], n[0])

            dve.wait_ge(s["count_done"], 1)
            link(dve.tensor_copy(count[:, :], pj_bank[:, 0:E]))
            link(dve.tensor_scalar(c_tmp[:, :], count[:, :], key_id[:, 0:1], None, ALU.add))
            link(dve.tensor_scalar(c_over[:, :], c_tmp[:, :], float(T), float(NOWHERE), ALU.is_ge, ALU.mult))
            link(dve.tensor_tensor(c_tmp[:, :], c_tmp[:, :], expert_base[:, :], ALU.add))
            dve.tensor_tensor(pad_place[:, :], c_tmp[:, :], c_over[:, :], ALU.add).then_inc(s["pad_ready"], 1)
            link(dve.tensor_tensor(has_tile[:, :, :], count[:, :].unsqueeze(2).broadcast_to([P, E, T // P]),
                                   tile_bound[:, :].unsqueeze(1).broadcast_to([P, E, T // P]), ALU.is_gt))
            link(dve.tensor_reduce(tiles[:, :], has_tile[:, :, :], AX.X, ALU.add))
            link(dve.tensor_tensor_scan(tiles_to[:, :], ones_e[:, :], tiles[:, :], 0.0, ALU.mult, ALU.add))
            wide = [P, NTILE, E]
            link(dve.tensor_tensor(passed[:, :, :], tile_id[:, :].unsqueeze(2).broadcast_to(wide), tiles_to[:, :].unsqueeze(1).broadcast_to(wide), ALU.is_ge))
            link(dve.tensor_reduce(tile_e[:, :, 0], passed[:, :, :], AX.X, ALU.add))
            link(dve.tensor_tensor(passed[:, :, :], passed[:, :, :], tiles[:, :].unsqueeze(1).broadcast_to(wide), ALU.mult))
            link(dve.tensor_reduce(tile_b[:, :, 0], passed[:, :, :], AX.X, ALU.add))
            link(dve.scalar_tensor_tensor(out=tile_b[:, :, 0], in0=tile_e[:, :, 0], scalar=float(T // P), in1=tile_b[:, :, 0], op0=ALU.mult, op1=ALU.subtract))
            link(dve.tensor_tensor(tile_b[:, :, 0], tile_b[:, :, 0], tile_id[:, :], ALU.add))
            dve.tensor_scalar(tile_expert[:, :], tile_e[:, :, 0], float(E - 1), None, ALU.min)
            dve.tensor_scalar(tile_row[:, :], tile_b[:, :, 0], float(P), float(E * T), ALU.mult, ALU.min).then_inc(s["table_ready"], 1)
            dve.wait_ge(s["table_ready"], 1)

            def turn_z(t, q):
                i = 4 * t + q
                dve.wait_ge(s["zt_done"], i + 1)
                if not (isinstance(t, int) and i < 2):
                    dve.wait_ge(s["up_done"], i - 1)
                dve.tensor_copy(zT[q % 2][:, :], (misc, pj_bank)[q % 2][:, 0:P]).then_inc(s["zT_ready"], 1)

            def add_b1(t, q):
                i = 4 * t + q
                e = dve.value_load(tile_expert[0:1, bass.ds(i, 1)], min_val=0, max_val=E - 1)
                dve.wait_ge(s["up_done"], i + 1)
                if not (isinstance(t, int) and i < 2):
                    dve.wait_ge(s["ht_done"], i - 1)
                dve.tensor_tensor(hid[q % 2][:, :], s_bank[:, q % 2].rearrange("p a b -> p (a b)"),
                                  b1_row[:, bass.ds(e, 1), :].rearrange("p o n -> p (o n)"), ALU.add).then_inc(s["hid_ready"], 1)

            def finish(t, q):
                i = 4 * t + q
                e = dve.value_load(tile_expert[0:1, bass.ds(i, 1)], min_val=0, max_val=E - 1)
                dve.wait_ge(s["down_done"], i + 1)
                dve.tensor_tensor(y_sum[q % 2][:, :], pv_bank[:, q % 2, 0:D], b2_row[:, bass.ds(e, 1), :].rearrange("p o n -> p (o n)"),
                                  ALU.add).then_inc(s["ysum_ready"], 1)
                if not (isinstance(t, int) and i < 2):
                    dve.wait_ge(s[f"out_done{q % 2}"], 16 * (2 * t + q // 2))
                dve.wait_ge(s["ysum_ready"], i + 1)
                dve.scalar_tensor_tensor(out=y_out[q % 2][:, :], in0=y_sum[q % 2][:, :], scalar=tile_in[q][:, GATE:GATE + 1],
                                         in1=tile_in[q][:, D:2 * D], op0=ALU.mult, op1=ALU.add).then_inc(s["y_ready"], 1)

            def tiles_of(t, first, last):
                for q in range(4):
                    add_b1(t, q)
                    if not (first and q == 0):
                        finish(t if q else t - 1, (q - 1) % 4)
                    if not (last and q == 3):
                        turn_z(t if q < 3 else t + 1, (q + 1) % 4)

            turn_z(0, 0)
            tiles_of(0, True, False)
            with dve.Fori(1, NTILE // 4 - 1) as t:
                tiles_of(t, False, False)
            tiles_of(NTILE // 4 - 1, False, True)
            finish(NTILE // 4 - 1, 3)

        @block.tensor
        def _(pe):
            pe.sem_inc(s["pv_done"], PV_CREDIT)
            pe.sem_inc(s["oq_done"], CREDIT)
            pe.sem_inc(s["onT_done"], 1)
            pe.wait_ge(s["weights_in"], 64)
            pe.wait_ge(s["ident_done"], 4)
            for i in range(4):
                last = pe.transpose(pj_bank[:, D * i:D * (i + 1)], w_raw[:, i, :], ident[:, :])
            last.then_inc(s["wt_done"], 1)
            pe.wait_ge(s["wt_copied"], 1)
            pe.wait_ge(s["vec_in"], 80)
            pe.transpose(pj_bank[:, 0:E], cent[:, :], ident[0:E, 0:E]).then_inc(s["centT_done"], 1)
            pe.wait_ge(s["centT_ready"], 1)
            pe.wait_ge(s["stacks_init"], 4)
            pe.wait_ge(s["v_init"], 2)

            def expert_weights(t, r):
                e = 2 * t + r
                late = not (isinstance(t, int) and t == 0)
                pe.wait_ge(s[f"w_in{r}"], 32 * (t + 1))
                if late:
                    pe.wait_ge(s["w1raw_ready"], e - 1)
                    pe.wait_ge(s["w2T_ready"], e - 1)
                for c in range(FC):
                    last = pe.transpose(st_bank[:, r, c, :], w1_stage[r][:, c, :], ident[:, :])
                last.then_inc(s["w1t_done"], 1)
                for c in range(FC):
                    last = pe.transpose(s_bank[:, r, c, :], w2_stage[r][:, P * c:P * (c + 1)], ident[:, :])
                last.then_inc(s["w2t_done"], 1)
                pe.wait_ge(s["beta_ready"], e + 1)
                pe.wait_ge(s["w1raw_ready"], e + 1)
                if late:
                    pe.wait_ge(s["b1_ready"], e - 1)
                pe.matmul(pv_bank[:, r, :], beta_cols[r][:, :], w1_rawT[r][:, :], start=True, stop=True).then_inc(s["wb_done"], 1)

            def step(t, r, proj, sc, st, rt=False):
                k = 2 * t + r
                known = isinstance(t, int)
                for pos in range(23):
                    if rt and pos == 6:
                        pe.wait_ge(s["feats_ready"], k - 2)
                        if proj:
                            pe.wait_ge(s["k_rest_r"], k + 1)
                        else:
                            pe.wait_ge(s["v_ready"], CB * NCH)
                            pe.wait_ge(s["place_ready"], k - 3)
                        for b in range(CB):
                            last = pe.transpose(pj_bank[:, S * b:S * (b + 1)], feats[:, b, :], ident[:, :])
                        last.then_inc(s["fT_done"], 1)
                    if rt and pos == 8:
                        pe.wait_ge(s["fT_ready"], k - 2)
                        for b in range(CB):
                            last = pe.matmul(pj_bank[:, E * b:E * (b + 1)], featsT[:, S * b:S * (b + 1)], centT[:, :], start=True, stop=True)
                        last.then_inc(s["score_done"], 1)
                    if rt and pos == 12:
                        pe.wait_ge(s["route_step"], NRT * (k - 3) + 15)
                        ranks = pj_bank[:, 64:64 + CB * E]
                        pe.matmul(ranks, upto[:, :], onehot[:, :, :].rearrange("p b e -> p (b e)"), start=True, stop=False)
                        pe.matmul(ranks, ones16[:, :], before[:, 0:CB, :].rearrange("p b e -> p (b e)"), start=False, stop=True).then_inc(s["rank_done"], 1)
                    if st and pos < SLOTS:
                        b, g = pos // 4, pos % 4
                        if pos % 8 == 0:
                            pe.wait_ge(s["m_in"], 64 * (2 * (k - 2) + pos // 8 + 1))
                        pe.wait_ge(s["exp_done"], SLOTS * (k - 2) + pos + 1)
                        for j in range(2):
                            last = pe.matmul(st_bank[:, pos % 2, 2 * j:2 * j + 2, :], k_stack[r][0:MROWS, 2 * g + j, S * b:S * (b + 1)],
                                             q_stack[r][0:MROWS, 2 * g + j, :, S * b:S * (b + 1)], start=True, stop=True)
                        last.then_inc(s["st_done"], 1)
                    if sc and 5 <= pos < 5 + SLOTS:
                        n = pos - 5
                        b, g = n // 4, n % 4
                        if n == 0:
                            pe.wait_ge(s["stack_in"], 48 * k)
                        pe.wait_ge(s["max_done"], SLOTS * (k - 1) + n + 1)
                        for j in range(4):
                            pr = 2 * g + j // 2
                            last = pe.matmul(s_bank[:, n % 2, j, :], q_stack[(r + 1) % 2][0:SROWS, pr, j % 2, S * b:S * (b + 1)],
                                             k_stack[(r + 1) % 2][0:SROWS, pr, S * b:S * (b + 1)], start=True, stop=True)
                        last.then_inc(s["s_done"], 1)
                    if st and 2 <= pos < 2 + SLOTS:
                        n = pos - 2
                        b, g = n // 4, n % 4
                        if n == 0:
                            pe.wait_ge(s["v_ready"], CB * (k - 1))
                            pe.wait_ge(s["keep_cols"], k - 1)
                        if g == 0:
                            pe.wait_ge(s["otraw_ready"], CB * (k - 2) + b + 1)
                        pe.wait_ge(s["exp_done"], CREDIT + SLOTS * (k - 2) + n + 1)
                        for j in range(SG):
                            last = pe.matmul(pv_bank[32 * j:32 * (j + 1), b % 2, S * g:S * (g + 1)], v_blk[r][:, b, SG * g + j, :],
                                             e_ring[:, n % 4, j, :], start=True, stop=True)
                        last.then_inc(s["pv_done"], 1)
                    if proj and pos == 0:
                        pe.wait_ge(s["xn_ready"], k + 1)
                        if not (known and k == 0):
                            pe.wait_ge(s["v_ready"], CB * k)
                        for b in range(CB):
                            last = pe.transpose(pj_bank[:, S * b:S * (b + 1)], xn[:, b, :], ident[:, :])
                        last.then_inc(s["pj_done"], 1)
                    if proj and pos == 1:
                        pe.wait_ge(s["ctx_ready"], k + 1)
                        pe.wait_ge(s["xT_ready"], k + 1)
                        for b in range(CB):
                            last = pe.transpose(pj_bank[:, S * b:S * (b + 1)], ctx_in[:, b, :], ident[:, :])
                        last.then_inc(s["pj_done"], 1)
                    if proj and pos == 2:
                        pe.wait_ge(s["ctxT_ready"], k + 1)
                        pe.matmul(pj_bank[:, :], wT[:, 0, :], xnT[:, :], start=True, stop=True).then_inc(s["pj_done"], 1)
                    if proj and pos == 3:
                        pe.wait_ge(s["q_rest_r"], k + 1)
                        pe.matmul(pj_bank[:, :], wT[:, 1, :], ctxT[:, :], start=True, stop=True).then_inc(s["pj_done"], 1)
                    if proj and pos == 19:
                        pe.wait_ge(s["k_rest_r"], k + 1)
                        if rt:
                            pe.wait_ge(s["place_ready"], k - 2)
                        for b in range(CB):
                            last = pe.matmul(pj_bank[:, S * b:S * (b + 1)], ctxT[:, S * b:S * (b + 1)], wT[:, 2, :], start=True, stop=True)
                        last.then_inc(s["pj_done"], 1)
                    if st and pos >= 7:
                        b, what = (pos - 7) // 4, (pos - 7) % 4
                        n = CB * (k - 2) + b
                        if what == 0:
                            pe.wait_ge(s["otraw_ready"], CREDIT + n + 1)
                            pe.wait_ge(s["x1_done"], 1 + n)
                            if b == 0 or (b == 2 and sc):
                                pe.wait_ge(s["mT_ready"], 2 * (k - 1) + b // 2)
                            for g in range(4):
                                last = pe.transpose(misc[:, S * g:S * (g + 1)], oT_raw[:, b % 2, S * g:S * (g + 1)], ident[:, :])
                            last.then_inc(s["oq_done"], 1)
                        if what == 1:
                            pe.wait_ge(s["on_ready"], n + 1)
                            pe.transpose(misc[:, 0:S], o_norm[:, :, :].rearrange("q h d -> q (h d)"), ident[:, :]).then_inc(s["onT_done"], 1)
                        if what == 2:
                            pe.wait_ge(s["onT_ready"], n + 1)
                            pe.matmul(misc[:, S:2 * S], oT_norm[:, :], wT[:, 3, :], start=True, stop=True).then_inc(s["wo_done"], 1)
                    if sc and pos in (14, 22):
                        bp = (pos - 14) // 8
                        m = 2 * (k - 1) + bp
                        pe.wait_ge(s["mp_ready"], m + 1)
                        if not (known and k == 1 and bp == 0):
                            pe.wait_ge(s["mT_ready"], m)
                        if st:
                            pe.wait_ge(s["x1_done"], 1 + CB * (k - 2) + 2 * (bp + 1))
                        pe.transpose(mT_ps, m_parts[:, :, :, :, :].rearrange("q b i p s -> q (b i p s)"), ident16[:, :]).then_inc(s["mt_done"], 1)

            step(0, 0, True, False, False)
            expert_weights(0, 0)
            expert_weights(0, 1)
            with pe.Fori(1, E // 2) as t:
                expert_weights(t, 0)
                expert_weights(t, 1)
            pe.wait_ge(s["w1raw_ready"], E)
            pe.wait_ge(s["w2T_ready"], E)
            pe.wait_ge(s["b1_ready"], E)
            pe.wait_ge(s["route_init"], 3)
            step(0, 1, True, True, False)
            step(1, 0, True, True, True)
            step(1, 1, True, True, True, True)
            with pe.Fori(2, NCH // 2) as t:
                step(t, 0, True, True, True, True)
                step(t, 1, True, True, True, True)
            step(NCH // 2, 0, False, True, True, True)
            step(NCH // 2, 1, False, False, True, True)
            step(NCH // 2 + 1, 0, False, False, False, True)
            pe.wait_ge(s["place_ready"], NCH)
            pe.matmul(pj_bank[:, 0:E], ones16[:, :], before[:, CB, :], start=True, stop=True).then_inc(s["count_done"], 1)

            def turn_z(t, q):
                pe.wait_ge(s[f"tile_in{q}"], 16 * (t + 1))
                pe.transpose((misc, pj_bank)[q % 2][:, 0:P], tile_in[q][:, 0:D], ident[:, :]).then_inc(s["zt_done"], 1)

            def up(t, q):
                i = 4 * t + q
                e = pe.value_load(tile_expert[0:1, bass.ds(i, 1)], min_val=0, max_val=E - 1)
                pe.wait_ge(s["zT_ready"], i + 1)
                if not (isinstance(t, int) and i < 2):
                    pe.wait_ge(s["hid_ready"], i - 1)
                pe.matmul(s_bank[:, q % 2].rearrange("p a b -> p (a b)"), zT[q % 2][:, :], w1T[:, bass.ds(e, 1), :].rearrange("p o n -> p (o n)"),
                          start=True, stop=True).then_inc(s["up_done"], 1)

            def turn_hidden(t, q):
                pe.wait_ge(s["hid_ready"], 4 * t + q + 1)
                for c in range(FC):
                    last = pe.transpose(st_bank[:, q % 2, c, :], hid[q % 2][:, P * c:P * (c + 1)], ident[:, :])
                last.then_inc(s["ht_done"], 1)

            def down(t, q):
                i = 4 * t + q
                e = pe.value_load(tile_expert[0:1, bass.ds(i, 1)], min_val=0, max_val=E - 1)
                pe.wait_ge(s["hidT_ready"], i + 1)
                if not (isinstance(t, int) and i < 2):
                    pe.wait_ge(s["ysum_ready"], i - 1)
                for c in range(FC):
                    last = pe.matmul(pv_bank[:, q % 2, 0:D], hidT[q % 2][:, P * c:P * (c + 1)],
                                     w2T[:, bass.ds(e, 1), D * c:D * (c + 1)].rearrange("p o n -> p (o n)"), start=(c == 0), stop=(c == FC - 1))
                last.then_inc(s["down_done"], 1)

            def tiles_of(t, first, last):
                for q in range(4):
                    if not (first and q == 0):
                        turn_hidden(t if q else t - 1, (q - 1) % 4)
                    up(t, q)
                    if not (first and q == 0):
                        down(t if q else t - 1, (q - 1) % 4)
                    if not (last and q == 3):
                        turn_z(t if q < 3 else t + 1, (q + 1) % 4)

            pe.wait_ge(s["table_ready"], 1)
            turn_z(0, 0)
            tiles_of(0, True, False)
            with pe.Fori(1, NTILE // 4 - 1) as t:
                tiles_of(t, False, False)
            tiles_of(NTILE // 4 - 1, False, True)
            turn_hidden(NTILE // 4 - 1, 3)
            down(NTILE // 4 - 1, 3)


_INS = ['x', 'ctx_1024', '_lenS2', 'L0_xattn_Wq', 'L0_xattn_Wk', 'L0_xattn_Wv', 'L0_xattn_Wo', 'L0_ffn_centroids',
        'L0_ffn_gamma', 'L0_ffn_beta', 'L0_ffn_W1', 'L0_ffn_b1', 'L0_ffn_W2', 'L0_ffn_b2']
_OUT = (32, 128, 128)


def kernel(**inputs):
    import numpy as _np
    import concourse.bacc as _bacc
    from concourse import mybir as _mybir
    from concourse.bass_utils import run_bass_kernel_spmd as _run

    nc = _bacc.Bacc("TRN2", target_bir_lowering=False, num_devices=1)
    arrays, args = {}, []
    for name in _INS:
        a = _np.ascontiguousarray(inputs[name])
        arrays[f"in_{name}_dram"] = a
        args.append(nc.dram_tensor(f"in_{name}_dram", a.shape, _mybir.dt.from_np(a.dtype), kind="ExternalInput").ap())
    out = nc.dram_tensor("out_dram", _OUT, F32, kind="ExternalOutput").ap()
    xattn_ffn_kernel(nc, *args, out)
    r = _run(nc, [arrays], core_ids=[0])
    return r.results[0]["out_dram"]
```

```python
import struct
from contextlib import ExitStack

import concourse.bass as bass
from concourse import mybir

F32 = mybir.dt.float32
BF16 = mybir.dt.bfloat16
I32 = mybir.dt.int32
ALU = mybir.AluOpType
ACT = mybir.ActivationFunctionType
AX = mybir.AxisListType


def xattn_ffn_kernel(nc, x_dram, ctx_dram, lens_dram, wq_dram, wk_dram, wv_dram, wo_dram,
                     cent_dram, gamma_dram, beta_dram, w1_dram, b1_dram, w2_dram, b2_dram, out_dram):
    B, S, D = x_dram.shape
    P = 128
    H, DH = 16, D // 16
    CB = 4
    NCH = B // CB
    TOK = CB * S
    SG = 4
    SLOTS = CB * (H // SG)
    NPAIR = H // 2
    NT = 6
    HROWS = NT * DH
    SROWS = 2 * HROWS
    MROWS = SROWS + 3
    VW = 32
    QSCALE = float(DH) ** -0.5
    EPS = 1e-5
    ONE_ONE = struct.unpack("<f", struct.pack("<I", 0x3F803F80))[0]
    E, F, _ = w1_dram.shape
    FC = F // P
    T = B * S
    UN = 8
    NTILE = -(-(T // P + E - 1) // UN) * UN
    PW = 2 * D + 4
    GATE, TOKEN = 2 * D, 2 * D + 1
    NOWHERE = 1 << 20
    XT, QQ, CT, KK, VV, FT = 0, 2, 3, 5, 7, 12
    NXIN = 1 + NCH // 2
    NPL = 7
    POS = SLOTS
    STEPS = NCH + 4
    assert S == P and D == P and DH == 8

    es = ExitStack()
    with es:
        def sb(name, shape, dt=F32):
            return es.enter_context(nc.sbuf_tensor(name, shape, dt))

        def psum(name, shape, dt=F32):
            return es.enter_context(nc.psum_tensor(name, shape, dt))

        def sem(name):
            return es.enter_context(nc.semaphore(name))

        q_scr = nc.dram_tensor("q_scr", (P, NT, TOK), BF16, kind="Internal").ap()
        k_scr = nc.dram_tensor("k_scr", (P, NT, TOK), BF16, kind="Internal").ap()
        m_scr = nc.dram_tensor("m_scr", (96, S), BF16, kind="Internal").ap()

        routed = nc.dram_tensor("routed", (E * T + P, PW), F32, kind="Internal").ap()

        x_all = sb("x_all", [P, B, D])
        ctx_in = sb("ctx_in", [P, CB, D])
        ctx_first = sb("ctx_first", [P, CB, D])
        mask_chunk = sb("mask_chunk", [P, CB], I32)
        xn = sb("xn", [P, CB, D])
        xnT = sb("xnT", [P, TOK])
        ctxT = [sb(f"ctxT{i}", [P, TOK]) for i in range(2)]
        q_parts = sb("q_parts", [P, 3, TOK], BF16)
        k_parts = sb("k_parts", [P, 3, TOK], BF16)
        q_rest = sb("q_rest", [P, TOK])
        k_rest = sb("k_rest", [P, TOK])
        q_stack = [sb(f"q_stack{i}", [P, NPAIR, 2, TOK], BF16) for i in range(2)]
        k_stack = [sb(f"k_stack{i}", [P, NPAIR, TOK], BF16) for i in range(2)]
        v_blk = [sb(f"v_blk{i}", [P, CB, H, VW]) for i in range(2)]
        e_ring = sb("e_ring", [P, 4, SG, S])
        oT_raw = sb("oT_raw", [P, 2, 4 * S])
        o_norm = sb("o_norm", [P, H, DH])
        oT_norm = sb("oT_norm", [P, S])
        z_inv = sb("z_inv", [P, H, 1])
        neg_max = sb("neg_max", [P, 2, H])
        m_parts = sb("m_parts", [P, 3, H, 2], BF16)
        m_rest = sb("m_rest", [P, H, 2])
        mT = sb("mT", [96, S], BF16)
        ident = sb("ident", [P, P])
        ident16 = sb("ident16", [P, P], BF16)
        w_raw = sb("w_raw", [P, 4, D])
        wT = sb("wT", [P, 4, D])
        stats = sb("stats", [P, CB, 6])
        x_mv = sb("x_mv", [P, CB, 2])
        x_neg_mean = sb("x_neg_mean", [P, B])
        x_bias = sb("x_bias", [P, B])
        rstd = sb("rstd", [P, B])
        x_vare = sb("x_vare", [P, B])
        tmp_a = sb("tmp_a", [P, B])
        tmp_b = sb("tmp_b", [P, B])
        neg_half = sb("neg_half", [P, B])
        lens_i = sb("lens_i", [P, B], I32)
        lens_f = sb("lens_f", [P, B])
        key_id = sb("key_id", [P, 1])
        nonempty = sb("nonempty", [P, B])
        masked_f = sb("masked_f", [P, B])
        masked_i = sb("masked_i", [P, B], I32)
        keep = sb("keep", [P, B])

        w1_stage = [sb(f"w1_stage{i}", [P, FC, D]) for i in range(2)]
        w2_stage = [sb(f"w2_stage{i}", [P, F]) for i in range(2)]
        w1_rawT = [sb(f"w1_rawT{i}", [P, F]) for i in range(2)]
        beta_cols = [sb(f"beta_cols{i}", [P, P]) for i in range(2)]
        w1T = sb("w1T", [P, E, F])
        w2T = sb("w2T", [P, E, FC * D])
        b1_row = sb("b1_row", [P, E, F])
        b2_row = sb("b2_row", [P, E, D])
        gammaT = sb("gammaT", [P, E])
        betaT = sb("betaT", [P, E])
        cent = sb("cent", [E, D])
        centT = sb("centT", [P, E])
        f_stats = sb("f_stats", [P, CB, 6])
        f_mv = sb("f_mv", [P, CB, 2])
        f_neg_mean = sb("f_neg_mean", [P, CB])
        f_bias = sb("f_bias", [P, CB])
        f_vare = sb("f_vare", [P, CB])
        f_rstd = sb("f_rstd", [P, CB])
        f_rz = sb("f_rz", [P, CB])
        p_tmp = sb("p_tmp", [P, CB])
        eps_t = sb("eps_t", [P, CB])
        feats = sb("feats", [P, CB, D])
        featsT = sb("featsT", [P, TOK])
        rows = [sb(f"rows{i}", [P, CB, PW]) for i in range(2)]
        score = sb("score", [P, CB, E])
        best = sb("best", [P, CB, 1])
        gate_e = sb("gate_e", [P, CB, 1])
        choice = sb("choice", [P, CB, 1])
        cand = sb("cand", [P, CB, E])
        onehot = sb("onehot", [P, CB, E], BF16)
        here = sb("here", [P, E], BF16)
        before = sb("before", [P, E], BF16)
        place_f = sb("place_f", [P, CB, E])
        place = [sb(f"place{i}", [P, CB], I32) for i in range(2)]
        token_f = sb("token_f", [P, CB])
        expert_id = sb("expert_id", [P, E])
        expert_base = sb("expert_base", [P, E])
        upto = sb("upto", [P, P], BF16)
        ones16 = sb("ones16", [P, P], BF16)
        count = sb("count", [P, E])
        c_tmp = sb("c_tmp", [P, E])
        c_over = sb("c_over", [P, E])
        pad_place = sb("pad_place", [P, E], I32)
        tile_bound = sb("tile_bound", [P, T // P])
        has_tile = sb("has_tile", [P, E, T // P])
        tiles = sb("tiles", [P, E])
        ones_e = sb("ones_e", [P, E])
        tiles_to = sb("tiles_to", [P, E])
        tile_id = sb("tile_id", [P, NTILE])
        passed = sb("passed", [P, NTILE, E])
        tile_e = sb("tile_e", [P, NTILE, 1])
        tile_b = sb("tile_b", [P, NTILE, 1])
        tile_row = sb("tile_row", [P, NTILE], I32)
        tile_expert = sb("tile_expert", [P, NTILE], I32)
        empty = sb("empty", [P, PW])
        stack_mem = q_stack[0][:, :, :, :].rearrange("p s i t -> p (s i t)").bitcast(F32)
        tile_in = [stack_mem[:, 512 * i:512 * i + PW] for i in range(UN)]
        zT = [oT_raw[:, 0, P * i:P * (i + 1)] for i in range(4)]
        hid = w1_rawT
        hidT = w2_stage
        y_sum = [oT_raw[:, 1, D * i:D * (i + 1)] for i in range(2)]
        y_out = [xn[:, i] for i in range(4)]

        s_bank = psum("s_bank", [P, 2, SG, S])
        st_bank = psum("st_bank", [P, 2, SG, S])
        pv_bank = psum("pv_bank", [P, 2, 4 * S])
        pj_bank = psum("pj_bank", [P, TOK])
        misc = psum("misc", [P, 512])
        mT_ps = misc[0:96, 384:384 + S // 2].bitcast(BF16)
        score_ps = misc[:, 448:448 + CB * E]
        rank_ps = misc[:, 480:480 + CB * E]

        names = ("weights_in ident_done x_in lens_in ctx_in_s wt_done wt_copied const_done mask_done "
                 "stats_done ln_step ln_pow rstd_ready ln_done xn_ready ctx_ready mchunk pj_done xT_ready ctxT_ready "
                 "q_hi k_hi q_rest_r k_rest_r q_mid k_mid q_lo k_lo keep_cols v_done v_ready scr_written "
                 "stack_in s_done max_done m_hi m_rest1 m_mid m_rest2 mp_ready mt_done mT_ready m_written m_in "
                 "st_done exp_done pv_done otraw_ready oq_done zinv_ready on_ready onT_done onT_ready "
                 "wo_done x1_done out_done0 out_done1 out_done2 out_done3 stacks_init v_init pool_turn sp_turn "
                 "vec_in w_in0 w_in1 w1t_done w2t_done w1raw_ready w2T_ready beta_ready w1T_ready wb_done b1_ready "
                 "route_init stat_step stats_ready route_vars pl_step feats_ready z_ready residual_ready best_ready choice_step here_ready before_ready rank_read fT_done fT_ready score_done "
                 "gate_exp place_step place_ready onehot_ready rank_done row_ready score_read vec_turn moments_read token_next scattered centT_done centT_ready "
                 "count_done table_step pad_ready padded table_ready tile_in0 tile_in1 tile_in2 tile_in3 tile_in4 tile_in5 tile_in6 tile_in7 empty_in "
                 "zt_done zT_ready up_done hid_ready ht_done hidT_ready down_done ysum_ready y_ready").split()
        s = {n: sem(n) for n in names}

        block = es.enter_context(nc.Block())

        CREDIT = 2
        PV_CREDIT = 4

        @block.sync
        def _(sp):
            sp.dma_start(lens_i[:, :], lens_dram.rearrange("(o b) -> o b", o=1).broadcast_to([P, B])).then_inc(s["lens_in"], 16)
            sp.dma_start(x_all[:, 0:CB, :], x_dram[0:CB].rearrange("b t d -> t b d")).then_inc(s["x_in"], 16)
            for i, w in enumerate((wq_dram, wk_dram, wv_dram, wo_dram)):
                sp.dma_start(w_raw[:, i, :], w).then_inc(s["weights_in"], 16)

            with nc.allow_non_contiguous_dma(reason="8 x 128 values"):
                sp.dma_start(gammaT[:, :], gamma_dram.rearrange("e d -> d e")).then_inc(s["vec_in"], 16)
                sp.dma_start(betaT[:, :], beta_dram.rearrange("e d -> d e")).then_inc(s["vec_in"], 16)
            sp.dma_start(cent[:, :], cent_dram).then_inc(s["vec_in"], 16)

            def load_expert(t, r):
                e = 2 * t + r
                if not (isinstance(t, int) and t == 0):
                    sp.wait_ge(s["w2t_done"], e - 1)
                    sp.wait_ge(s["w1t_done"], e - 1)
                    sp.sem_inc(s["sp_turn"])
                sp.dma_start(w1_stage[r][:, :, :], w1_dram[bass.ds(e, 1)].rearrange("o (c f) d -> f (o c) d", f=P)).then_inc(s[f"w_in{r}"], 16)
                sp.dma_start(w2_stage[r][:, :], w2_dram[bass.ds(e, 1)].rearrange("o d f -> d (o f)")).then_inc(s[f"w_in{r}"], 16)

            def load_ctx(c):
                src = ctx_dram[bass.ds(CB * c, CB)]
                sp.dma_start(ctx_in[:, :, :], src.rearrange("b t d -> t b d")).then_inc(s["ctx_in_s"], 16)
                sp.dma_start(ctx_first[:, :, :], src[:, 0:1, :].rearrange("b o d -> o b d").broadcast_to([P, CB, D])).then_inc(s["ctx_in_s"], 16)

            load_ctx(0)
            sp.wait_ge(s["x_in"], 16)
            for b in [CB] + [CB * c for c in range(2, NCH, 2)]:
                n = CB if b == CB else 2 * CB
                sp.dma_start(x_all[:, b:b + n, :], x_dram[b:b + n].rearrange("b t d -> t b d")).then_inc(s["x_in"], 16)
            load_expert(0, 0)
            load_expert(0, 1)
            sp.dma_start(b1_row[:, :, :], b1_dram.rearrange("(o e) f -> o e f", o=1).broadcast_to([P, E, F])).then_inc(s["vec_in"], 16)
            sp.dma_start(b2_row[:, :, :], b2_dram.rearrange("(o e) d -> o e d", o=1).broadcast_to([P, E, D])).then_inc(s["vec_in"], 16)

            def load_stack(r, half, columns):
                q_rows = q_scr.rearrange("(s i d) c t -> i (d c) s t", i=2, d=DH)
                for i in range(2):
                    sp.dma_start(q_stack[r][HROWS * i:HROWS * (i + 1), :, i, columns], q_rows[i][:, :, columns]).then_inc(s["stack_in"], 16)
                sp.dma_start(k_stack[r][0:SROWS, :, columns], k_scr.rearrange("(s i) c t -> (i c) s t", i=16)[:, :, columns]).then_inc(s["stack_in"], 16)

            def step(t, r):
                k = 2 * t + r
                known = isinstance(t, int)
                if not known or 1 <= k <= NCH:
                    if not known or k >= 3:
                        sp.wait_ge(s["st_done"], SLOTS * (k - 2))
                    sp.wait_ge(s["stack_in"], 96 * (k - 1) + 48)
                    sp.sem_inc(s["sp_turn"])
                    load_stack((r + 1) % 2, 1, slice(TOK // 2, TOK))
                if not known or k < NCH - 1:
                    sp.wait_ge(s["pj_done"], 4 * k + 3)
                    sp.sem_inc(s["sp_turn"])
                    load_ctx(k + 1)
                if not known or k < NCH:
                    if not (known and k == 0):
                        sp.wait_ge(s["stack_in"], 96 * k)
                    for scr, parts, ready, times in ((q_scr, q_parts, ("q_hi", "q_mid", "q_lo"), ((0, 1, 3), (1, 1, 2), (2, 1, 1))),
                                                     (k_scr, k_parts, ("k_hi", "k_mid", "k_lo"), ((0, 1, 1), (0, 2, 1), (0, 3, 1)))):
                        at = NT if parts is k_parts else 0
                        for name, (part, n, copies) in zip(ready, times):
                            sp.wait_ge(s[name], k + 1)
                            at = at - n if parts is k_parts else at
                            sp.dma_start(scr[:, at:at + n * copies, :], parts[:, part:part + n, :].broadcast_to([P, n * copies, TOK]) if copies > 1
                                         else parts[:, part:part + n, :]).then_inc(s["scr_written"], 16)
                            at = at + n * copies if parts is q_parts else at
                    sp.wait_ge(s["scr_written"], 96 * (k + 1))
                    if not known or k >= 2:
                        sp.wait_ge(s["st_done"], SLOTS * (k - 2) + SLOTS // 2)
                    sp.sem_inc(s["sp_turn"])
                    load_stack(r, 0, slice(0, TOK // 2))

            sp.wait_ge(s["stacks_init"], 4)
            step(0, 0)
            with sp.Fori(1, E // 2) as t:
                load_expert(t, 0)
                load_expert(t, 1)
            step(0, 1)
            step(1, 0)
            step(1, 1)
            with sp.Fori(2, NCH // 2 - 1) as t:
                step(t, 0)
                step(t, 1)
            step(NCH // 2 - 1, 0)
            step(NCH // 2 - 1, 1)
            step(NCH // 2, 0)

            sp.wait_ge(s["scattered"], 16 * (B + 1))
            sp.wait_ge(s["padded"], 16 * E)
            sp.wait_ge(s["table_ready"], 1)

            def load_tile(t, q):
                i = UN * t + q
                if not (isinstance(t, int) and t == 0):
                    sp.wait_ge(s["y_ready"], i - UN + 1)
                    sp.sem_inc(s["sp_turn"])
                    sp.wait_ge(s[f"out_done{q % 4}"], 16 * (2 * t + q // 4 - 1))
                    sp.sem_inc(s["sp_turn"])
                row = sp.value_load(tile_row[0:1, bass.ds(i, 1)], min_val=0, max_val=E * T)
                sp.dma_start(tile_in[q], routed[bass.ds(row, P), :]).then_inc(s[f"tile_in{q}"], 16)

            for q in range(UN):
                load_tile(0, q)
            with sp.Fori(1, NTILE // UN) as t:
                for q in range(UN):
                    load_tile(t, q)
            for q in range(4):
                sp.wait_ge(s[f"out_done{q}"], 16 * (NTILE // 4))

        @block.gpsimd
        def _(pool):
            for m in (ident, ident16):
                pool.memset(m[:, :], 0.0).then_inc(s["ident_done"], 1)
            pool.wait_ge(s["ident_done"], 2)
            for m in (ident, ident16):
                pool.affine_select(out=m[:, :], in_=m[:, :], compare_op=ALU.not_equal, fill=1.0, base=0,
                                   pattern=[[-1, P]], channel_multiplier=1).then_inc(s["ident_done"], 1)
            pool.iota(key_id[:, :], pattern=[[0, 1]], base=0, channel_multiplier=1,
                      allow_small_or_imprecise_dtypes=True).then_inc(s["const_done"], 1)
            pool.memset(neg_half[:, :], -0.5).then_inc(s["const_done"], 1)
            for i in range(2):
                pool.memset(v_blk[i][:, :, :, :], 0.0).then_inc(s["v_init"], 1)
            pool.memset(empty[:, :], 0.0).then_inc(s["pool_turn"], 1)
            pool.wait_ge(s["pool_turn"], 1)
            pool.memset(empty[:, TOKEN:TOKEN + 1].bitcast(I32), NOWHERE).then_inc(s["route_init"], 1)
            pool.wait_ge(s["const_done"], 2)
            for i, bs in enumerate((slice(0, CB), slice(CB, B))):
                pool.wait_ge(s["moments_read"], 2 if i == 0 else 2 * NCH)
                pool.tensor_tensor(tmp_b[:, bs], x_vare[:, bs], neg_half[:, bs], ALU.pow).then_inc(s["ln_pow"], 1)
            pool.wait_ge(s["mask_done"], 1)
            pool.wait_ge(s["v_init"], 2)
            pool.memset(eps_t[:, :], EPS)
            pool.memset(ones16[:, :], 1.0)
            pool.memset(ones_e[:, :], 1.0)
            pool.memset(before[:, :], 0.0)
            for i in range(2):
                pool.memset(rows[i][:, :, :], 0.0)
            pool.memset(upto[:, :], 1.0).then_inc(s["route_init"], 1)
            pool.wait_ge(s["route_init"], 2)
            pool.affine_select(out=upto[:, :], in_=upto[:, :], compare_op=ALU.is_gt, fill=0.0, base=0,
                               pattern=[[1, P]], channel_multiplier=-1)
            pool.iota(expert_id[:, :], pattern=[[1, E]], base=0, channel_multiplier=0, allow_small_or_imprecise_dtypes=True)
            pool.iota(expert_base[:, :], pattern=[[T, E]], base=0, channel_multiplier=0, allow_small_or_imprecise_dtypes=True)
            pool.iota(tile_bound[:, :], pattern=[[P, T // P]], base=0, channel_multiplier=0, allow_small_or_imprecise_dtypes=True)
            pool.iota(tile_id[:, :], pattern=[[1, NTILE]], base=0, channel_multiplier=0, allow_small_or_imprecise_dtypes=True)
            pool.iota(token_f[:, :], pattern=[[S, CB]], base=0, channel_multiplier=1,
                      allow_small_or_imprecise_dtypes=True).then_inc(s["route_init"], 1)
            pool.wait_ge(s["route_init"], 3)

            pool.dma_start(routed[E * T:E * T + P, :], empty[:, :]).then_inc(s["scattered"], 16)

            def route_vars(c):
                steps = ((f_rstd, f_vare[:, :], neg_half[:, 0:CB], ALU.pow), (p_tmp, f_rstd[:, :], f_rstd[:, :], ALU.mult),
                         (p_tmp, p_tmp[:, :], f_mv[:, :, 1], ALU.mult), (p_tmp, p_tmp[:, :], eps_t[:, :], ALU.add),
                         (p_tmp, p_tmp[:, :], neg_half[:, 0:CB], ALU.pow), (f_rz, p_tmp[:, :], f_rstd[:, :], ALU.mult),
                         (f_bias, f_rz[:, :], f_neg_mean[:, :], ALU.mult))
                pool.wait_ge(s["route_vars"], c + 1)
                if not (isinstance(c, int) and c == 0):
                    pool.wait_ge(s["z_ready"], c)
                for i, (out, a, b, op) in enumerate(steps):
                    if i:
                        pool.wait_ge(s["pl_step"], NPL * c + i)
                    pool.tensor_tensor(out[:, :], a, b, op).then_inc(s["pl_step"], 1)
                assert NPL == len(steps)

            def residual(c, buf):
                if not (isinstance(c, int) and c == 0):
                    pool.wait_ge(s["scattered"], 16 + 16 * CB * (c - 1))
                pool.wait_ge(s["feats_ready"], c + 1)
                pool.tensor_tensor(rows[buf][:, :, D:2 * D], feats[:, :, :], x_all[:, bass.ds(CB * c, CB), :], ALU.add).then_inc(s["residual_ready"], 1)

            def scatter(c, buf):
                pool.wait_ge(s["residual_ready"], c + 1)
                pool.wait_ge(s["z_ready"], c + 1)
                pool.wait_ge(s["place_ready"], c + 1)
                pool.sem_inc(s["pool_turn"])
                for b in range(CB):
                    pool.indirect_dma_start(out=routed, out_offset=bass.IndirectOffsetOnAxis(ap=place[buf][:, b:b + 1], axis=0),
                                            in_=rows[buf][:, b, :], in_offset=None).then_inc(s["scattered"], 16)

            def low_part(k, parts, rest, ready, lo):
                pool.wait_ge(s[ready], k + 1)
                pool.tensor_tensor(parts[:, 2, :], rest[:, :], parts[:, 1, :], ALU.subtract).then_inc(s[lo], 1)

            def keep_columns(c, buf):
                if not (isinstance(c, int) and c < 2):
                    pool.wait_ge(s["pv_done"], PV_CREDIT + SLOTS * (c - 1))
                pool.sem_inc(s["pool_turn"])
                pool.tensor_copy(v_blk[buf][:, :, :, DH:2 * DH],
                                 keep[:, bass.ds(CB * c, CB)].unsqueeze(2).unsqueeze(3).broadcast_to([P, CB, H, DH])).then_inc(s["keep_cols"], 1)

            def step(t, r):
                k = 2 * t + r
                known = isinstance(t, int)
                if not known or k < NCH:
                    low_part(k, q_parts, q_rest, "q_mid", "q_lo")
                if not known or 1 <= k <= NCH:
                    keep_columns(k - 1, (r + 1) % 2)
                if not known or k < NCH:
                    low_part(k, k_parts, k_rest, "k_mid", "k_lo")
                if not known or 3 <= k < NCH + 3:
                    route_vars(k - 3)
                    residual(k - 3, (r + 1) % 2)
                if not known or 4 <= k < NCH + 4:
                    scatter(k - 4, r)

            for k in range(4):
                step(k // 2, k % 2)
            with pool.Fori(2, NCH // 2) as t:
                step(t, 0)
                step(t, 1)
            for k in range(NCH, STEPS):
                step(k // 2, k % 2)
            pool.wait_ge(s["pad_ready"], 1)
            for e in range(E):
                pool.indirect_dma_start(out=routed, out_offset=bass.IndirectOffsetOnAxis(ap=pad_place[:, e:e + 1], axis=0),
                                        in_=empty[:, :], in_offset=None, bounds_check=E * T - 1, oob_is_err=False).then_inc(s["padded"], 16)

            out_rows = out_dram.rearrange("b t d -> (b t) d")

            def store(t, q):
                pool.wait_ge(s["y_ready"], UN * t + q + 1)
                pool.sem_inc(s["pool_turn"])
                pool.indirect_dma_start(out=out_rows, out_offset=bass.IndirectOffsetOnAxis(ap=tile_in[q][:, TOKEN:TOKEN + 1].bitcast(I32), axis=0),
                                        in_=y_out[q % 4], in_offset=None, bounds_check=T - 1, oob_is_err=False).then_inc(s[f"out_done{q % 4}"], 16)

            with pool.Fori(0, NTILE // UN) as t:
                for q in range(UN):
                    store(t, q)

        @block.scalar
        def _(act):
            act.sem_inc(s["exp_done"], CREDIT)
            act.sem_inc(s["otraw_ready"], CREDIT)
            act.wait_ge(s["wt_done"], 1)
            act.activation(wT[:, :, :].rearrange("p a b -> p (a b)"), pj_bank[:, :], ACT.Copy).then_inc(s["wt_copied"], 1)

            act.wait_ge(s["centT_done"], 1)
            act.activation(centT[:, :], pj_bank[:, 0:E], ACT.Copy).then_inc(s["centT_ready"], 1)

            def expert_weights(t, r):
                e = 2 * t + r
                late = not (isinstance(t, int) and t == 0)
                act.wait_ge(s["w1t_done"], e + 1)
                if late:
                    act.wait_ge(s["wb_done"], e - 1)
                    act.wait_ge(s["w1T_ready"], e - 1)
                act.activation(w1_rawT[r][:, :], st_bank[:, r].rearrange("p a b -> p (a b)"), ACT.Copy).then_inc(s["w1raw_ready"], 1)
                act.wait_ge(s["w2t_done"], e + 1)
                act.activation(w2T[:, bass.ds(e, 1), :].rearrange("p o n -> p (o n)"), s_bank[:, r].rearrange("p a b -> p (a b)"),
                               ACT.Copy).then_inc(s["w2T_ready"], 1)

            def normalise(c):
                act.wait_ge(s["ln_done"], (1 if isinstance(c, int) and c == 0 else 2))
                for b in range(CB):
                    last = act.activation(xn[:, b, :], x_all[:, bass.ds(CB * c + b, 1), :].rearrange("p o d -> p (o d)"), ACT.Identity,
                                          bias=x_bias[:, bass.ds(CB * c + b, 1)], scale=rstd[:, bass.ds(CB * c + b, 1)])
                last.then_inc(s["xn_ready"], 1)

            def outputs_out(c, b):
                act.wait_ge(s["pv_done"], PV_CREDIT + SLOTS * c + 4 * b + 4)
                act.wait_ge(s["oq_done"], CB * c + b + 1)
                act.activation(oT_raw[:, b % 2, :], pv_bank[:, b % 2, :], ACT.Copy).then_inc(s["otraw_ready"], 1)

            def normed_out(c, b):
                act.wait_ge(s["onT_done"], 1 + CB * c + b + 1)
                act.activation(oT_norm[:, :], misc[:, 0:S], ACT.Copy).then_inc(s["onT_ready"], 1)

            def max_out(c, half):
                act.wait_ge(s["mt_done"], 2 * c + half + 1)
                if not (isinstance(c, int) and c == 0 and half == 0):
                    act.wait_ge(s["m_in"], 16 * (2 * c + half))
                act.activation(mT[:, :], mT_ps, ACT.Copy).then_inc(s["mT_ready"], 1)
                act.wait_ge(s["mT_ready"], 2 * c + half + 1)
                act.dma_start(m_scr, mT[:, :]).then_inc(s["m_written"], 16)

            def max_rows(c, half, buf):
                act.wait_ge(s["m_written"], 16 * (2 * c + half + 1))
                act.dma_start(q_stack[buf][SROWS:MROWS, :, :, 2 * S * half:2 * S * (half + 1)].rearrange("p s i t -> p (s i) t"),
                              m_scr.rearrange("(p h b) t -> p h (b t)", p=3, b=2)).then_inc(s["m_in"], 16)

            def step(t, r):
                k = 2 * t + r
                known = isinstance(t, int)
                proj, vals, sc = (not known or a <= k < a + NCH for a in (0, 1, 1))
                st, tail, pick = (not known or a <= k < a + NCH for a in (2, 3, 4))
                more = not known or k < NCH - 1
                for pos in range(POS):
                    if st:
                        act.wait_ge(s["st_done"], SLOTS * (k - 2) + pos + 1)
                        act.wait_ge(s["pv_done"], SLOTS * (k - 2) + pos + 1)
                        act.activation(e_ring[:, pos % 4], st_bank[:, pos % 2], ACT.Exp).then_inc(s["exp_done"], 1)
                    if proj and pos == XT:
                        act.wait_ge(s["pj_done"], 4 * k + 1)
                        act.activation(xnT[:, :], pj_bank[:, :], ACT.Copy).then_inc(s["xT_ready"], 1)
                    if proj and pos == QQ:
                        act.wait_ge(s["pj_done"], 4 * k + 2)
                        if not (known and k == 0):
                            act.wait_ge(s["scr_written"], 96 * k)
                        act.activation(q_parts[:, 0, :], pj_bank[:, :], ACT.Copy, scale=QSCALE).then_inc(s["q_hi"], 1)
                    if proj and pos == QQ + 2:
                        act.wait_ge(s["q_rest_r"], k + 1)
                        act.activation(q_parts[:, 1, :], q_rest[:, :], ACT.Copy).then_inc(s["q_mid"], 1)
                    if vals and pos == VV:
                        act.wait_ge(s["v_done"], k)
                        if known and k == 1:
                            act.wait_ge(s["v_init"], 2)
                        if not known or k >= 3:
                            act.wait_ge(s["pv_done"], PV_CREDIT + SLOTS * (k - 2))
                        for b in range(CB):
                            act.activation(v_blk[(r + 1) % 2][:, b, :, 0:DH], pj_bank[:, S * b:S * (b + 1)].rearrange("p (h d) -> p h d", h=H),
                                           ACT.Copy, scale=keep[:, bass.ds(CB * (k - 1) + b, 1)]).then_inc(s["v_ready"], 1)
                    if proj and pos == CT:
                        act.wait_ge(s["pj_done"], 4 * k + 3)
                        act.activation(ctxT[r][:, :], pj_bank[:, :], ACT.Copy).then_inc(s["ctxT_ready"], 1)
                    if proj and pos == KK:
                        act.wait_ge(s["pj_done"], 4 * k + 4)
                        act.activation(k_parts[:, 0, :], pj_bank[:, :], ACT.Copy).then_inc(s["k_hi"], 1)
                    if proj and pos == KK + 2:
                        act.wait_ge(s["k_rest_r"], k + 1)
                        act.activation(k_parts[:, 1, :], k_rest[:, :], ACT.Copy).then_inc(s["k_mid"], 1)
                    if st and pos in (5, 9, 13):
                        outputs_out(k - 2, (pos - 5) // 4)
                    if tail and pos == 1:
                        outputs_out(k - 3, 3)
                    if st and pos in (8, 12):
                        normed_out(k - 2, (pos - 8) // 4)
                    if tail and pos in (0, 4):
                        normed_out(k - 3, 2 + pos // 4)
                    if sc and pos == 10:
                        max_out(k - 1, 0)
                    if sc and pos == 12:
                        max_rows(k - 1, 0, (r + 1) % 2)
                    if st and pos == 2:
                        max_out(k - 2, 1)
                    if st and pos == 4:
                        max_rows(k - 2, 1, r)
                    if pick and pos == 3:
                        act.wait_ge(s["best_ready"], k - 3)
                        act.activation(gate_e[:, :, :], best[:, :, :], ACT.Exp, scale=-1.0).then_inc(s["gate_exp"], 1)
                    if tail and pos == 11:
                        act.wait_ge(s["pl_step"], NPL * (k - 2))
                        if not (known and k == 3):
                            act.wait_ge(s["scattered"], 16 + 16 * CB * (k - 4))
                        for b in range(CB):
                            last = act.activation(rows[(r + 1) % 2][:, b, 0:D], x_all[:, bass.ds(CB * (k - 3) + b, 1), :].rearrange("p o d -> p (o d)"),
                                                  ACT.Identity, bias=f_bias[:, b:b + 1], scale=f_rz[:, b:b + 1])
                        last.then_inc(s["z_ready"], 1)
                    if tail and pos == FT:
                        act.wait_ge(s["fT_done"], k - 2)
                        act.activation(featsT[:, :], pj_bank[:, :], ACT.Copy).then_inc(s["fT_ready"], 1)
                    if more and pos == 14:
                        act.wait_ge(s["pj_done"], 4 * k + 1)
                        normalise(k + 1)

            normalise(0)
            step(0, 0)
            expert_weights(0, 0)
            expert_weights(0, 1)
            with act.Fori(1, E // 2) as t:
                expert_weights(t, 0)
                expert_weights(t, 1)
            act.wait_ge(s["route_init"], 3)
            for k in range(1, 4):
                step(k // 2, k % 2)
            with act.Fori(2, NCH // 2 - 1) as t:
                step(t, 0)
                step(t, 1)
            for k in range(NCH - 2, STEPS):
                step(k // 2, k % 2)

            def hidden(t, q):
                i = UN * t + q
                act.wait_ge(s["ht_done"], i + 1)
                if not (isinstance(t, int) and i < 2):
                    act.wait_ge(s["down_done"], i - 1)
                act.activation(hidT[q % 2][:, :], st_bank[:, q % 2].rearrange("p a b -> p (a b)"), ACT.Relu).then_inc(s["hidT_ready"], 1)

            def turned_z(t, q):
                i = UN * t + q
                act.wait_ge(s["zt_done"], i + 1)
                if not (isinstance(t, int) and i < 4):
                    act.wait_ge(s["up_done"], i - 3)
                act.activation(zT[q % 4], (misc, pj_bank)[q % 2][:, 0:P], ACT.Copy).then_inc(s["zT_ready"], 1)

            def tiles_of(t, first, last):
                for q in range(UN):
                    if not (first and q == 0):
                        hidden(t if q else t - 1, (q - 1) % UN)
                    if not (last and q >= UN - 2):
                        turned_z(t if q < UN - 2 else t + 1, (q + 2) % UN)

            turned_z(0, 0)
            turned_z(0, 1)
            tiles_of(0, True, False)
            with act.Fori(1, NTILE // UN - 1) as t:
                tiles_of(t, False, False)
            tiles_of(NTILE // UN - 1, False, True)
            hidden(NTILE // UN - 1, UN - 1)

        @block.vector
        def _(dve):
            dve.sem_inc(s["max_done"], CREDIT)
            dve.sem_inc(s["x1_done"], 1)
            for i in range(2):
                dve.memset(q_stack[i][:, :, :, :].rearrange("p a b t -> p (a b t)").bitcast(F32), 0.0).then_inc(s["stacks_init"], 1)
                dve.memset(k_stack[i][SROWS:MROWS, :, :].rearrange("p s t -> p (s t)").bitcast(F32), ONE_ONE).then_inc(s["stacks_init"], 1)
            dve.wait_ge(s["lens_in"], 16)
            dve.wait_ge(s["const_done"], 1)
            dve.tensor_copy(lens_f[:, :], lens_i[:, :]).then_inc(s["mchunk"], 1)
            dve.wait_ge(s["mchunk"], 1)
            dve.tensor_scalar(nonempty[:, :], lens_f[:, :], 0.0, None, ALU.is_gt).then_inc(s["mchunk"], 1)
            dve.tensor_scalar(masked_f[:, :], lens_f[:, :], key_id[:, 0:1], None, ALU.is_le).then_inc(s["mchunk"], 1)
            dve.wait_ge(s["mchunk"], 3)
            dve.tensor_tensor(tmp_a[:, :], masked_f[:, :], nonempty[:, :], ALU.mult).then_inc(s["mchunk"], 1)
            dve.wait_ge(s["mchunk"], 4)
            dve.tensor_copy(masked_i[:, :], tmp_a[:, :]).then_inc(s["mchunk"], 1)
            dve.tensor_scalar(keep[:, :], tmp_a[:, :], -1.0, 1.0, ALU.mult, ALU.add).then_inc(s["mask_done"], 1)
            def chunk_stats(c):
                for b in range(CB):
                    last = dve.bn_stats(stats[:, b, :], x_all[:, bass.ds(CB * c + b, 1), :])
                last.then_inc(s["stats_done"], 1)
                dve.wait_ge(s["stats_done"], c + 1)
                if not (isinstance(c, int) and c == 0):
                    dve.wait_ge(s["moments_read"], 2 * c)
                dve.sem_inc(s["vec_turn"])
                for b in range(CB):
                    last = dve.bn_aggr(x_mv[:, b, :], stats[:, b, :])
                last.then_inc(s["ln_step"], 1)
                dve.wait_ge(s["ln_step"], c + 1)
                dve.tensor_scalar(x_neg_mean[:, bass.ds(CB * c, CB)], x_mv[:, :, 0], -1.0, None, ALU.mult).then_inc(s["moments_read"], 1)
                dve.tensor_scalar(x_vare[:, bass.ds(CB * c, CB)], x_mv[:, :, 1], EPS, None, ALU.add).then_inc(s["moments_read"], 1)

            def x_stats(i, lo, hi):
                dve.wait_ge(s["x_in"], 16 * (1 if i == 0 else NXIN))
                if i == 0:
                    chunk_stats(0)
                else:
                    with dve.Fori(1, NCH) as c:
                        chunk_stats(c)
                dve.wait_ge(s["ln_pow"], i + 1)
                dve.wait_ge(s["moments_read"], 2 * (hi // CB))
                dve.tensor_tensor(rstd[:, lo:hi], tmp_b[:, lo:hi], nonempty[:, lo:hi], ALU.mult).then_inc(s["rstd_ready"], 1)
                dve.wait_ge(s["rstd_ready"], i + 1)
                dve.tensor_tensor(x_bias[:, lo:hi], x_neg_mean[:, lo:hi], rstd[:, lo:hi], ALU.mult).then_inc(s["ln_done"], 1)

            x_stats(0, 0, CB)

            def mask_ctx(c):
                dve.tensor_copy(mask_chunk[:, :], masked_i[:, bass.ds(CB * c, CB)]).then_inc(s["mchunk"], 1)
                dve.wait_ge(s["mchunk"], 6 + c)
                dve.wait_ge(s["ctx_in_s"], 32 * (c + 1))
                dve.copy_predicated(ctx_in[:, :, :], mask_chunk[:, :].unsqueeze(2).broadcast_to([P, CB, D]), ctx_first[:, :, :]).then_inc(s["ctx_ready"], 1)

            mask_ctx(0)

            def max_parts(c, bp, known):
                nm = neg_max[:, :, :].rearrange("q b h -> q h b")
                dve.wait_ge(s["max_done"], CREDIT + SLOTS * c + 8 * bp + 8)
                if not (known and c == 0 and bp == 0):
                    dve.wait_ge(s["mt_done"], 2 * c + bp)
                n = 2 * c + bp + 1
                dve.tensor_copy(m_parts[:, 0], nm).then_inc(s["m_hi"], 1)
                dve.wait_ge(s["m_hi"], n)
                dve.tensor_tensor(m_rest[:, :, :], nm, m_parts[:, 0], ALU.subtract).then_inc(s["m_rest1"], 1)
                dve.wait_ge(s["m_rest1"], n)
                dve.tensor_copy(m_parts[:, 1], m_rest[:, :, :]).then_inc(s["m_mid"], 1)
                dve.wait_ge(s["m_mid"], n)
                dve.tensor_tensor(m_parts[:, 2], m_rest[:, :, :], m_parts[:, 1], ALU.subtract).then_inc(s["mp_ready"], 1)

            def expert_weights(t, r):
                e = 2 * t + r
                late = not (isinstance(t, int) and t == 0)
                if late:
                    dve.wait_ge(s["wb_done"], e - 1)
                dve.tensor_copy(beta_cols[r][:, :], betaT[:, bass.ds(e, 1)].broadcast_to([P, P])).then_inc(s["beta_ready"], 1)
                dve.wait_ge(s["w1raw_ready"], e + 1)
                dve.tensor_scalar(w1T[:, bass.ds(e, 1), :].rearrange("p o n -> p (o n)"), w1_rawT[r][:, :], gammaT[:, bass.ds(e, 1)], None,
                                  ALU.mult).then_inc(s["w1T_ready"], 1)
                dve.wait_ge(s["wb_done"], e + 1)
                br = b1_row[:, bass.ds(e, 1), :].rearrange("p o n -> p (o n)")
                dve.tensor_tensor(br, pv_bank[:, r, :], br, ALU.add).then_inc(s["b1_ready"], 1)

            def row_stats(c):
                dve.wait_ge(s["x1_done"], 1 + CB * (c + 1))
                for b in range(CB):
                    last = dve.bn_stats(f_stats[:, b, :], x_all[:, bass.ds(CB * c + b, 1), :])
                last.then_inc(s["stat_step"], 1)
                if not (isinstance(c, int) and c == 0):
                    dve.wait_ge(s["pl_step"], NPL * c)
                dve.wait_ge(s["stat_step"], c + 1)
                dve.sem_inc(s["vec_turn"])
                for b in range(CB):
                    last = dve.bn_aggr(f_mv[:, b, :], f_stats[:, b, :])
                last.then_inc(s["stats_ready"], 1)
                dve.wait_ge(s["stats_ready"], c + 1)
                dve.tensor_scalar(f_neg_mean[:, :], f_mv[:, :, 0], -1.0, None, ALU.mult)
                dve.tensor_scalar(f_vare[:, :], f_mv[:, :, 1], EPS, None, ALU.add).then_inc(s["route_vars"], 1)

            def normalise_rows(c):
                dve.wait_ge(s["pl_step"], NPL * c + 1)
                if not (isinstance(c, int) and c == 0):
                    dve.wait_ge(s["residual_ready"], c)
                    dve.wait_ge(s["fT_done"], c)
                for b in range(CB):
                    last = dve.tensor_scalar(feats[:, b, :], x_all[:, bass.ds(CB * c + b, 1), :].rearrange("p o d -> p (o d)"),
                                             f_mv[:, b, 0:1], f_rstd[:, b:b + 1], ALU.subtract, ALU.mult)
                last.then_inc(s["feats_ready"], 1)

            wide = [P, CB, E]
            every_expert = expert_id[:, :].unsqueeze(1).broadcast_to(wide)

            def choose(c, part):
                n = 3 * c
                if part == 0:
                    dve.wait_ge(s["score_done"], c + 1)
                    dve.tensor_copy(score[:, :, :], score_ps.rearrange("p (b e) -> p b e", e=E)).then_inc(s["score_read"], 1)
                    dve.wait_ge(s["score_read"], c + 1)
                    dve.tensor_reduce(best[:, :, 0], score[:, :, :], AX.X, ALU.max).then_inc(s["best_ready"], 1)
                if part == 1:
                    dve.wait_ge(s["best_ready"], c + 1)
                    dve.tensor_tensor(cand[:, :, :], score[:, :, :], best[:, :, :].broadcast_to(wide), ALU.is_lt).then_inc(s["choice_step"], 1)
                if part == 2:
                    dve.wait_ge(s["choice_step"], n + 1)
                    dve.scalar_tensor_tensor(out=cand[:, :, :], in0=cand[:, :, :], scalar=float(E), in1=every_expert,
                                             op0=ALU.mult, op1=ALU.add).then_inc(s["choice_step"], 1)
                if part == 3:
                    dve.wait_ge(s["choice_step"], n + 2)
                    dve.tensor_reduce(choice[:, :, 0], cand[:, :, :], AX.X, ALU.min).then_inc(s["choice_step"], 1)
                if part == 4:
                    dve.wait_ge(s["choice_step"], n + 3)
                    dve.tensor_tensor(onehot[:, :, :], choice[:, :, :].broadcast_to(wide), every_expert, ALU.is_equal).then_inc(s["onehot_ready"], 1)

            def placing(c, buf, part):
                if part == 0:
                    dve.wait_ge(s["onehot_ready"], c + 1)
                    with nc.allow_low_precision(reason="counts up to 32"):
                        dve.tensor_reduce(here[:, :], onehot[:, :, :].rearrange("p b e -> p e b"), AX.X, ALU.add).then_inc(s["here_ready"], 1)
                    dve.wait_ge(s["rank_done"], c + 1)
                    dve.tensor_tensor(place_f[:, :, :], rank_ps.rearrange("p (b e) -> p b e", e=E),
                                      expert_base[:, :].unsqueeze(1).broadcast_to(wide), ALU.add).then_inc(s["rank_read"], 1)
                    dve.wait_ge(s["gate_exp"], c + 1)
                    dve.tensor_scalar(gate_e[:, :, :], gate_e[:, :, :], 1.0, None, ALU.add).then_inc(s["place_step"], 1)
                if part == 1:
                    dve.wait_ge(s["rank_read"], c + 1)
                    dve.tensor_tensor(place_f[:, :, :], place_f[:, :, :], onehot[:, :, :], ALU.mult).then_inc(s["place_step"], 1)
                    dve.wait_ge(s["here_ready"], c + 1)
                    dve.tensor_tensor(before[:, :], before[:, :], here[:, :], ALU.add).then_inc(s["before_ready"], 1)
                if part == 2:
                    if not (isinstance(c, int) and c == 0):
                        dve.wait_ge(s["scattered"], 16 + 16 * CB * (c - 1))
                    dve.wait_ge(s["place_step"], 2 * c + 2)
                    dve.reciprocal(rows[buf][:, :, GATE:GATE + 1], gate_e[:, :, :])
                    dve.tensor_copy(rows[buf][:, :, TOKEN].bitcast(I32), token_f[:, :]).then_inc(s["row_ready"], 1)
                    with nc.allow_low_precision(reason="whole numbers below 2**24, one of them not zero"):
                        dve.tensor_reduce(place[buf][:, :], place_f[:, :, :], AX.X, ALU.add).then_inc(s["place_ready"], 1)
                    dve.wait_ge(s["row_ready"], c + 1)
                    dve.tensor_scalar(token_f[:, :], token_f[:, :], float(TOK), None, ALU.add).then_inc(s["token_next"], 1)
                    dve.wait_ge(s["token_next"], c + 1)

            def weigh(c, b):
                oq = misc[:, :].rearrange("q (h w) -> q h w", w=VW)
                n = CB * c + b
                dve.wait_ge(s["oq_done"], CREDIT + n + 1)
                dve.reciprocal(z_inv[:, :, :], oq[:, :, DH:DH + 1]).then_inc(s["zinv_ready"], 1)
                dve.wait_ge(s["zinv_ready"], n + 1)
                dve.wait_ge(s["onT_done"], 1 + n)
                dve.tensor_tensor(o_norm[:, :, :], oq[:, :, 0:DH], z_inv[:, :, :].broadcast_to([P, H, DH]), ALU.mult).then_inc(s["on_ready"], 1)

            def add_to_x(c, b):
                dve.wait_ge(s["wo_done"], CB * c + b + 1)
                xr = x_all[:, bass.ds(CB * c + b, 1), :].rearrange("p o d -> p (o d)")
                dve.tensor_tensor(xr, misc[:, S:2 * S], xr, ALU.add).then_inc(s["x1_done"], 1)

            def step(t, r):
                k = 2 * t + r
                known = isinstance(t, int)
                proj, sc = (not known or a <= k < a + NCH for a in (0, 1))
                st, tail, pick = (not known or a <= k < a + NCH for a in (2, 3, 4))
                more = not known or k < NCH - 1
                for pos in range(POS):
                    if tail and pos in (2, 6):
                        add_to_x(k - 3, 2 + pos // 4)
                    if st and pos in (10, 14):
                        add_to_x(k - 2, (pos - 10) // 4)
                    if proj and pos == QQ + 1:
                        dve.wait_ge(s["q_hi"], k + 1)
                        if not (known and k == 0):
                            dve.wait_ge(s["q_lo"], k)
                        dve.scalar_tensor_tensor(out=q_rest[:, :], in0=pj_bank[:, :], scalar=QSCALE, in1=q_parts[:, 0, :],
                                                 op0=ALU.mult, op1=ALU.subtract).then_inc(s["q_rest_r"], 1)
                    if proj and pos == KK + 1:
                        dve.wait_ge(s["k_hi"], k + 1)
                        if not (known and k == 0):
                            dve.wait_ge(s["k_lo"], k)
                        dve.tensor_tensor(k_rest[:, :], pj_bank[:, :], k_parts[:, 0, :], ALU.subtract).then_inc(s["k_rest_r"], 1)
                    if pick and pos < 4:
                        choose(k - 4, pos + 1)
                    if pick and 7 <= pos <= 9:
                        placing(k - 4, r, pos - 7)
                    if sc:
                        dve.wait_ge(s["s_done"], SLOTS * (k - 1) + pos + 1)
                        if pos % 8 == 0 and not (known and k == 1 and pos == 0):
                            dve.wait_ge(s["mp_ready"], 2 * (k - 1) + pos // 8)
                        dve.tensor_reduce(neg_max[:, (pos // 4) % 2, SG * (pos % 4):SG * (pos % 4 + 1)], s_bank[:, pos % 2], AX.X, ALU.max,
                                          negate=True).then_inc(s["max_done"], 1)
                    if tail and pos == 14:
                        choose(k - 3, 0)
                    if st and pos in (7, 11, 15):
                        weigh(k - 2, (pos - 7) // 4)
                    if sc and pos % 8 == 7:
                        max_parts(k - 1, pos // 8, known)
                    if tail and pos == 3:
                        weigh(k - 3, 3)
                    if tail and pos == 6:
                        row_stats(k - 3)
                    if tail and pos == 10:
                        normalise_rows(k - 3)
                    if more and pos == 13:
                        dve.wait_ge(s["pj_done"], 4 * k + 3)
                        mask_ctx(k + 1)

            step(0, 0)
            x_stats(1, CB, B)
            dve.wait_ge(s["vec_in"], 80)
            expert_weights(0, 0)
            expert_weights(0, 1)
            with dve.Fori(1, E // 2) as t:
                expert_weights(t, 0)
                expert_weights(t, 1)
            dve.wait_ge(s["route_init"], 3)
            for k in range(1, 4):
                step(k // 2, k % 2)
            with dve.Fori(2, NCH // 2 - 1) as t:
                step(t, 0)
                step(t, 1)
            for k in range(NCH - 2, STEPS):
                step(k // 2, k % 2)

            n = [0]

            def link(ins):
                n[0] += 1
                ins.then_inc(s["table_step"], 1)
                dve.wait_ge(s["table_step"], n[0])

            dve.wait_ge(s["count_done"], 1)
            link(dve.tensor_copy(count[:, :], pj_bank[:, 0:E]))
            link(dve.tensor_scalar(c_tmp[:, :], count[:, :], key_id[:, 0:1], None, ALU.add))
            link(dve.tensor_scalar(c_over[:, :], c_tmp[:, :], float(T), float(NOWHERE), ALU.is_ge, ALU.mult))
            link(dve.tensor_tensor(c_tmp[:, :], c_tmp[:, :], expert_base[:, :], ALU.add))
            dve.tensor_tensor(pad_place[:, :], c_tmp[:, :], c_over[:, :], ALU.add).then_inc(s["pad_ready"], 1)
            link(dve.tensor_tensor(has_tile[:, :, :], count[:, :].unsqueeze(2).broadcast_to([P, E, T // P]),
                                   tile_bound[:, :].unsqueeze(1).broadcast_to([P, E, T // P]), ALU.is_gt))
            link(dve.tensor_reduce(tiles[:, :], has_tile[:, :, :], AX.X, ALU.add))
            link(dve.tensor_tensor_scan(tiles_to[:, :], ones_e[:, :], tiles[:, :], 0.0, ALU.mult, ALU.add))
            wide = [P, NTILE, E]
            link(dve.tensor_tensor(passed[:, :, :], tile_id[:, :].unsqueeze(2).broadcast_to(wide), tiles_to[:, :].unsqueeze(1).broadcast_to(wide), ALU.is_ge))
            link(dve.tensor_reduce(tile_e[:, :, 0], passed[:, :, :], AX.X, ALU.add))
            link(dve.tensor_tensor(passed[:, :, :], passed[:, :, :], tiles[:, :].unsqueeze(1).broadcast_to(wide), ALU.mult))
            link(dve.tensor_reduce(tile_b[:, :, 0], passed[:, :, :], AX.X, ALU.add))
            link(dve.scalar_tensor_tensor(out=tile_b[:, :, 0], in0=tile_e[:, :, 0], scalar=float(T // P), in1=tile_b[:, :, 0], op0=ALU.mult, op1=ALU.subtract))
            link(dve.tensor_tensor(tile_b[:, :, 0], tile_b[:, :, 0], tile_id[:, :], ALU.add))
            dve.tensor_scalar(tile_expert[:, :], tile_e[:, :, 0], float(E - 1), None, ALU.min)
            dve.tensor_scalar(tile_row[:, :], tile_b[:, :, 0], float(P), float(E * T), ALU.mult, ALU.min).then_inc(s["table_ready"], 1)
            dve.wait_ge(s["table_ready"], 1)

            def add_b1(t, q):
                i = UN * t + q
                e = dve.value_load(tile_expert[0:1, bass.ds(i, 1)], min_val=0, max_val=E - 1)
                dve.wait_ge(s["up_done"], i + 1)
                if not (isinstance(t, int) and i < 2):
                    dve.wait_ge(s["ht_done"], i - 1)
                dve.tensor_tensor(hid[q % 2][:, :], s_bank[:, q % 2].rearrange("p a b -> p (a b)"),
                                  b1_row[:, bass.ds(e, 1), :].rearrange("p o n -> p (o n)"), ALU.add).then_inc(s["hid_ready"], 1)

            def finish(t, q):
                i = UN * t + q
                e = dve.value_load(tile_expert[0:1, bass.ds(i, 1)], min_val=0, max_val=E - 1)
                dve.wait_ge(s["down_done"], i + 1)
                dve.tensor_tensor(y_sum[q % 2], pv_bank[:, q % 2, 0:D], b2_row[:, bass.ds(e, 1), :].rearrange("p o n -> p (o n)"),
                                  ALU.add).then_inc(s["ysum_ready"], 1)
                if not (isinstance(t, int) and i < 4):
                    dve.wait_ge(s[f"out_done{q % 4}"], 16 * (2 * t + q // 4))
                dve.wait_ge(s["ysum_ready"], i + 1)
                dve.scalar_tensor_tensor(out=y_out[q % 4], in0=y_sum[q % 2], scalar=tile_in[q][:, GATE:GATE + 1],
                                         in1=tile_in[q][:, D:2 * D], op0=ALU.mult, op1=ALU.add).then_inc(s["y_ready"], 1)

            def tiles_of(t, first):
                for q in range(UN):
                    add_b1(t, q)
                    if not (first and q == 0):
                        finish(t if q else t - 1, (q - 1) % UN)

            tiles_of(0, True)
            with dve.Fori(1, NTILE // UN) as t:
                tiles_of(t, False)
            finish(NTILE // UN - 1, UN - 1)

        @block.tensor
        def _(pe):
            pe.sem_inc(s["pv_done"], PV_CREDIT)
            pe.sem_inc(s["oq_done"], CREDIT)
            pe.sem_inc(s["onT_done"], 1)
            pe.wait_ge(s["weights_in"], 64)
            pe.wait_ge(s["ident_done"], 4)
            for i in range(4):
                last = pe.transpose(pj_bank[:, D * i:D * (i + 1)], w_raw[:, i, :], ident[:, :])
            last.then_inc(s["wt_done"], 1)
            pe.wait_ge(s["wt_copied"], 1)
            pe.wait_ge(s["vec_in"], 80)
            pe.transpose(pj_bank[:, 0:E], cent[:, :], ident[0:E, 0:E]).then_inc(s["centT_done"], 1)
            pe.wait_ge(s["centT_ready"], 1)
            pe.wait_ge(s["stacks_init"], 4)
            pe.wait_ge(s["v_init"], 2)

            def expert_weights(t, r):
                e = 2 * t + r
                late = not (isinstance(t, int) and t == 0)
                pe.wait_ge(s[f"w_in{r}"], 32 * (t + 1))
                if late:
                    pe.wait_ge(s["w1raw_ready"], e - 1)
                    pe.wait_ge(s["w2T_ready"], e - 1)
                for c in range(FC):
                    last = pe.transpose(st_bank[:, r, c, :], w1_stage[r][:, c, :], ident[:, :])
                last.then_inc(s["w1t_done"], 1)
                for c in range(FC):
                    last = pe.transpose(s_bank[:, r, c, :], w2_stage[r][:, P * c:P * (c + 1)], ident[:, :])
                last.then_inc(s["w2t_done"], 1)
                pe.wait_ge(s["beta_ready"], e + 1)
                pe.wait_ge(s["w1raw_ready"], e + 1)
                if late:
                    pe.wait_ge(s["b1_ready"], e - 1)
                pe.matmul(pv_bank[:, r, :], beta_cols[r][:, :], w1_rawT[r][:, :], start=True, stop=True).then_inc(s["wb_done"], 1)

            def queries_first(c, b):
                n = CB * c + b
                pe.wait_ge(s["otraw_ready"], CREDIT + n + 1)
                pe.wait_ge(s["x1_done"], 1 + n)
                for g in range(4):
                    last = pe.transpose(misc[:, S * g:S * (g + 1)], oT_raw[:, b % 2, S * g:S * (g + 1)], ident[:, :])
                last.then_inc(s["oq_done"], 1)

            def heads_first(c, b):
                pe.wait_ge(s["on_ready"], CB * c + b + 1)
                pe.transpose(misc[:, 0:S], o_norm[:, :, :].rearrange("q h d -> q (h d)"), ident[:, :]).then_inc(s["onT_done"], 1)

            def through_wo(c, b):
                pe.wait_ge(s["onT_ready"], CB * c + b + 1)
                pe.matmul(misc[:, S:2 * S], oT_norm[:, :], wT[:, 3, :], start=True, stop=True).then_inc(s["wo_done"], 1)

            def turn_max(c, half):
                pe.wait_ge(s["mp_ready"], 2 * c + half + 1)
                if not (isinstance(c, int) and c == 0 and half == 0):
                    pe.wait_ge(s["mT_ready"], 2 * c + half)
                pe.transpose(mT_ps, m_parts[:, :, :, :].rearrange("q p h b -> q (p h b)"), ident16[:, :]).then_inc(s["mt_done"], 1)

            def weighed(c, b, g, buf):
                n = SG * b + g
                if n == 0:
                    pe.wait_ge(s["v_ready"], CB * (c + 1))
                    pe.wait_ge(s["keep_cols"], c + 1)
                if g == 0:
                    pe.wait_ge(s["otraw_ready"], CB * c + b + 1)
                pe.wait_ge(s["exp_done"], CREDIT + SLOTS * c + n + 1)
                for j in range(SG):
                    last = pe.matmul(pv_bank[32 * j:32 * (j + 1), b % 2, S * g:S * (g + 1)], v_blk[buf][:, b, SG * g + j, :],
                                     e_ring[:, n % 4, j, :], start=True, stop=True)
                last.then_inc(s["pv_done"], 1)

            def step(t, r):
                k = 2 * t + r
                known = isinstance(t, int)
                proj, vals, sc = (not known or a <= k < a + NCH for a in (0, 1, 1))
                st, tail, pick = (not known or a <= k < a + NCH for a in (2, 3, 4))
                for pos in range(POS):
                    b, g = pos // 4, pos % 4
                    if st:
                        if pos % 8 == 0:
                            pe.wait_ge(s["m_in"], 16 * (2 * (k - 2) + pos // 8 + 1))
                        pe.wait_ge(s["exp_done"], SLOTS * (k - 2) + pos + 1)
                        for j in range(2):
                            last = pe.matmul(st_bank[:, pos % 2, 2 * j:2 * j + 2, :], k_stack[r][0:MROWS, 2 * g + j, S * b:S * (b + 1)],
                                             q_stack[r][0:MROWS, 2 * g + j, :, S * b:S * (b + 1)], start=True, stop=True)
                        last.then_inc(s["st_done"], 1)
                    if sc:
                        if pos % 8 == 0:
                            pe.wait_ge(s["stack_in"], 96 * (k - 1) + 6 * pos + 48)
                        pe.wait_ge(s["max_done"], SLOTS * (k - 1) + pos + 1)
                        for j in range(4):
                            pr = 2 * g + j // 2
                            last = pe.matmul(s_bank[:, pos % 2, j, :], q_stack[(r + 1) % 2][0:SROWS, pr, j % 2, S * b:S * (b + 1)],
                                             k_stack[(r + 1) % 2][0:SROWS, pr, S * b:S * (b + 1)], start=True, stop=True)
                        last.then_inc(s["s_done"], 1)
                    if st and pos >= 2:
                        weighed(k - 2, (pos - 2) // 4, (pos - 2) % 4, r)
                    if tail and pos < 2:
                        weighed(k - 3, 3, 2 + pos, (r + 1) % 2)
                    if proj and pos == XT:
                        pe.wait_ge(s["xn_ready"], k + 1)
                        if not known or k >= 4:
                            pe.wait_ge(s["fT_ready"], k - 3)
                        elif k == 1:
                            pe.wait_ge(s["k_rest_r"], 1)
                        elif k:
                            pe.wait_ge(s["v_ready"], CB * (k - 1))
                        for b in range(CB):
                            last = pe.transpose(pj_bank[:, S * b:S * (b + 1)], xn[:, b, :], ident[:, :])
                        last.then_inc(s["pj_done"], 1)
                    if proj and pos == QQ:
                        pe.wait_ge(s["xT_ready"], k + 1)
                        pe.matmul(pj_bank[:, :], wT[:, 0, :], xnT[:, :], start=True, stop=True).then_inc(s["pj_done"], 1)
                    if vals and pos == VV:
                        if proj:
                            pe.wait_ge(s["k_rest_r"], k + 1)
                        else:
                            pe.wait_ge(s["fT_ready"], k - 3)
                        for b in range(CB):
                            last = pe.matmul(pj_bank[:, S * b:S * (b + 1)], ctxT[(r + 1) % 2][:, S * b:S * (b + 1)], wT[:, 2, :], start=True, stop=True)
                        last.then_inc(s["v_done"], 1)
                    if proj and pos == CT:
                        pe.wait_ge(s["ctx_ready"], k + 1)
                        pe.wait_ge(s["q_rest_r"], k + 1)
                        for b in range(CB):
                            last = pe.transpose(pj_bank[:, S * b:S * (b + 1)], ctx_in[:, b, :], ident[:, :])
                        last.then_inc(s["pj_done"], 1)
                    if proj and pos == KK:
                        pe.wait_ge(s["ctxT_ready"], k + 1)
                        pe.matmul(pj_bank[:, :], wT[:, 1, :], ctxT[r][:, :], start=True, stop=True).then_inc(s["pj_done"], 1)
                    if tail and pos == FT:
                        pe.wait_ge(s["feats_ready"], k - 2)
                        if vals:
                            pe.wait_ge(s["v_ready"], CB * k)
                        else:
                            pe.wait_ge(s["fT_ready"], k - 3)
                        for b in range(CB):
                            last = pe.transpose(pj_bank[:, S * b:S * (b + 1)], feats[:, b, :], ident[:, :])
                        last.then_inc(s["fT_done"], 1)
                    if tail and pos == 3:
                        if st:
                            pe.wait_ge(s["mT_ready"], 2 * (k - 1))
                        queries_first(k - 3, 3)
                    if st and pos in (7, 11, 15):
                        if pos == 7 and pick:
                            pe.wait_ge(s["rank_read"], k - 3)
                        if pos == 11 and sc:
                            pe.wait_ge(s["mT_ready"], 2 * (k - 1) + 1)
                        if pos == 15 and tail:
                            pe.wait_ge(s["score_read"], k - 2)
                        queries_first(k - 2, (pos - 7) // 4)
                    if st and pos in (8, 12):
                        heads_first(k - 2, (pos - 8) // 4)
                    if tail and pos in (0, 4):
                        heads_first(k - 3, 2 + pos // 4)
                    if st and pos in (9, 13):
                        through_wo(k - 2, (pos - 9) // 4)
                    if tail and pos in (1, 5):
                        through_wo(k - 3, 2 + pos // 4)
                    if sc and pos == 10:
                        if st:
                            pe.wait_ge(s["x1_done"], 1 + CB * (k - 2) + 1)
                        turn_max(k - 1, 0)
                    if st and pos == 2:
                        if tail:
                            pe.wait_ge(s["x1_done"], 1 + CB * (k - 3) + 3)
                        turn_max(k - 2, 1)
                    if tail and pos == 14:
                        pe.wait_ge(s["fT_ready"], k - 2)
                        pe.wait_ge(s["x1_done"], 1 + (CB * (k - 2) + 2 if st else CB * (k - 2)))
                        for b in range(CB):
                            last = pe.matmul(score_ps[:, E * b:E * (b + 1)], featsT[:, S * b:S * (b + 1)], centT[:, :], start=True, stop=True)
                        last.then_inc(s["score_done"], 1)
                    if pick and pos == 6:
                        if tail:
                            pe.wait_ge(s["x1_done"], 1 + CB * (k - 2))
                        pe.wait_ge(s["onehot_ready"], k - 3)
                        pe.wait_ge(s["before_ready"], k - 4) if not (known and k == 4) else None
                        pe.matmul(rank_ps, upto[:, :], onehot[:, :, :].rearrange("p b e -> p (b e)"), start=True, stop=False)
                        pe.matmul(rank_ps, ones16[:, :], before[:, :].unsqueeze(1).broadcast_to([P, CB, E]), start=False, stop=False)
                        for b in range(CB - 1):
                            last = pe.matmul(rank_ps[:, E * (b + 1):], ones16[:, :], onehot[:, b:b + 1, :].broadcast_to([P, CB - 1 - b, E]),
                                             start=False, stop=(b == CB - 2))
                        last.then_inc(s["rank_done"], 1)

            step(0, 0)
            expert_weights(0, 0)
            expert_weights(0, 1)
            with pe.Fori(1, E // 2) as t:
                expert_weights(t, 0)
                expert_weights(t, 1)
            pe.wait_ge(s["w1raw_ready"], E)
            pe.wait_ge(s["w2T_ready"], E)
            pe.wait_ge(s["b1_ready"], E)
            pe.wait_ge(s["route_init"], 3)
            for k in range(1, 4):
                step(k // 2, k % 2)
            with pe.Fori(2, NCH // 2) as t:
                step(t, 0)
                step(t, 1)
            for k in range(NCH, STEPS):
                step(k // 2, k % 2)
            pe.wait_ge(s["before_ready"], NCH)
            pe.matmul(pj_bank[:, 0:E], ones16[:, :], before[:, :], start=True, stop=True).then_inc(s["count_done"], 1)

            def turn_z(t, q):
                pe.wait_ge(s[f"tile_in{q}"], 16 * (t + 1))
                pe.transpose((misc, pj_bank)[q % 2][:, 0:P], tile_in[q][:, 0:D], ident[:, :]).then_inc(s["zt_done"], 1)

            def expert_of(i):
                return pe.value_load(tile_expert[0:1, bass.ds(i, 1)], min_val=0, max_val=E - 1)

            def up(t, q, e):
                i = UN * t + q
                pe.wait_ge(s["zT_ready"], i + 1)
                if not (isinstance(t, int) and i < 2):
                    pe.wait_ge(s["hid_ready"], i - 1)
                pe.matmul(s_bank[:, q % 2].rearrange("p a b -> p (a b)"), zT[q % 4], w1T[:, bass.ds(e, 1), :].rearrange("p o n -> p (o n)"),
                          start=True, stop=True).then_inc(s["up_done"], 1)

            def turn_hidden(t, q):
                i = UN * t + q
                pe.wait_ge(s["hid_ready"], i + 1)
                for c in range(FC):
                    last = pe.transpose(st_bank[:, q % 2, c, :], hid[q % 2][:, P * c:P * (c + 1)], ident[:, :])
                last.then_inc(s["ht_done"], 1)

            def down(t, q, e):
                i = UN * t + q
                pe.wait_ge(s["hidT_ready"], i + 1)
                if not (isinstance(t, int) and i < 2):
                    pe.wait_ge(s["ysum_ready"], i - 1)
                for c in range(FC):
                    last = pe.matmul(pv_bank[:, q % 2, 0:D], hidT[q % 2][:, P * c:P * (c + 1)],
                                     w2T[:, bass.ds(e, 1), D * c:D * (c + 1)].rearrange("p o n -> p (o n)"), start=(c == 0), stop=(c == FC - 1))
                last.then_inc(s["down_done"], 1)

            def tiles_of(t, first, last):
                e_last = None if first else expert_of(UN * t - 1)
                e = expert_of(UN * t)
                for q in range(UN):
                    if not (first and q == 0):
                        turn_hidden(t if q else t - 1, (q - 1) % UN)
                    up(t, q, e)
                    e_next = expert_of(UN * t + q + 1) if q < UN - 1 else None
                    if not (first and q == 0):
                        down(t if q else t - 1, (q - 1) % UN, e_last)
                    e_last, e = e, e_next
                    if not (last and q >= UN - 2):
                        turn_z(t if q < UN - 2 else t + 1, (q + 2) % UN)

            pe.wait_ge(s["table_ready"], 1)
            turn_z(0, 0)
            turn_z(0, 1)
            tiles_of(0, True, False)
            with pe.Fori(1, NTILE // UN - 1) as t:
                tiles_of(t, False, False)
            tiles_of(NTILE // UN - 1, False, True)
            turn_hidden(NTILE // UN - 1, UN - 1)
            down(NTILE // UN - 1, UN - 1, expert_of(NTILE - 1))


_INS = ['x', 'ctx_1024', '_lenS2', 'L0_xattn_Wq', 'L0_xattn_Wk', 'L0_xattn_Wv', 'L0_xattn_Wo', 'L0_ffn_centroids',
        'L0_ffn_gamma', 'L0_ffn_beta', 'L0_ffn_W1', 'L0_ffn_b1', 'L0_ffn_W2', 'L0_ffn_b2']
_OUT = (32, 128, 128)


def kernel(**inputs):
    import numpy as _np
    import concourse.bacc as _bacc
    from concourse import mybir as _mybir
    from concourse.bass_utils import run_bass_kernel_spmd as _run

    nc = _bacc.Bacc("TRN2", target_bir_lowering=False, num_devices=1)
    arrays, args = {}, []
    for name in _INS:
        a = _np.ascontiguousarray(inputs[name])
        arrays[f"in_{name}_dram"] = a
        args.append(nc.dram_tensor(f"in_{name}_dram", a.shape, _mybir.dt.from_np(a.dtype), kind="ExternalInput").ap())
    out = nc.dram_tensor("out_dram", _OUT, F32, kind="ExternalOutput").ap()
    xattn_ffn_kernel(nc, *args, out)
    r = _run(nc, [arrays], core_ids=[0])
    return r.results[0]["out_dram"]
```

```python
import struct
from contextlib import ExitStack

import concourse.bass as bass
from concourse import mybir

F32 = mybir.dt.float32
BF16 = mybir.dt.bfloat16
I32 = mybir.dt.int32
ALU = mybir.AluOpType
ACT = mybir.ActivationFunctionType
AX = mybir.AxisListType


def xattn_ffn_kernel(nc, x_dram, ctx_dram, lens_dram, wq_dram, wk_dram, wv_dram, wo_dram,
                     cent_dram, gamma_dram, beta_dram, w1_dram, b1_dram, w2_dram, b2_dram, out_dram):
    B, S, D = x_dram.shape
    P = 128
    H, DH = 16, D // 16
    CB = 4
    NCH = B // CB
    TOK = CB * S
    SG = 4
    SLOTS = CB * (H // SG)
    NPAIR = H // 2
    NT = 6
    HROWS = NT * DH
    SROWS = 2 * HROWS
    MROWS = SROWS + 3
    VW = 32
    QSCALE = float(DH) ** -0.5
    EPS = 1e-5
    ONE_ONE = struct.unpack("<f", struct.pack("<I", 0x3F803F80))[0]
    E, F, _ = w1_dram.shape
    FC = F // P
    T = B * S
    ROOM = T + P
    UN = 8
    NTILE = -(-(T // P + E - 1) // UN) * UN
    PW = 2 * D + 4
    GATE, TOKEN = 2 * D, 2 * D + 1
    NOWHERE = 1 << 20
    XT, QQ, CT, KK, VV, FT = 0, 1, 4, 6, 9, 12
    E_FIRST = 2
    PREPARE = (1, 3, 5, 8, 10, 12)
    SIDES = (range(FC // 2), range(FC // 2, FC))
    XN_AT = {6: (0, 1), 8: (2,), 10: (3,)}
    NPL = 5
    POS = SLOTS
    STEPS = NCH + 4
    assert S == P and D == P and DH == 8

    es = ExitStack()
    with es:
        def sb(name, shape, dt=F32):
            return es.enter_context(nc.sbuf_tensor(name, shape, dt))

        def psum(name, shape, dt=F32):
            return es.enter_context(nc.psum_tensor(name, shape, dt))

        def sem(name):
            return es.enter_context(nc.semaphore(name))

        q_scr = nc.dram_tensor("q_scr", (P, NT, TOK), BF16, kind="Internal").ap()
        k_scr = nc.dram_tensor("k_scr", (P, NT, TOK), BF16, kind="Internal").ap()
        m_scr = nc.dram_tensor("m_scr", (96, S), BF16, kind="Internal").ap()

        routed = nc.dram_tensor("routed", (E * ROOM + P, PW), F32, kind="Internal").ap()

        x_all = sb("x_all", [P, B, D])
        ctx_in = sb("ctx_in", [P, CB, D])
        ctx_first = sb("ctx_first", [P, CB, D])
        mask_chunk = sb("mask_chunk", [P, CB], I32)
        xn = sb("xn", [P, CB, D])
        xnT = sb("xnT", [P, TOK])
        ctxT = [sb(f"ctxT{i}", [P, TOK]) for i in range(2)]
        q_parts = sb("q_parts", [P, 3, TOK], BF16)
        k_parts = sb("k_parts", [P, 3, TOK], BF16)
        q_rest = sb("q_rest", [P, TOK])
        k_rest = sb("k_rest", [P, TOK])
        q_stack = [sb(f"q_stack{i}", [P, NPAIR, 2, TOK], BF16) for i in range(2)]
        k_stack = [sb(f"k_stack{i}", [P, NPAIR, TOK], BF16) for i in range(2)]
        v_blk = [sb(f"v_blk{i}", [P, CB, H, VW]) for i in range(2)]
        e_ring = sb("e_ring", [P, 4, SG, S])
        oT_raw = sb("oT_raw", [P, 2, 4 * S])
        o_norm = sb("o_norm", [P, H, DH])
        oT_norm = sb("oT_norm", [P, S])
        z_inv = sb("z_inv", [P, H, 1])
        neg_max = sb("neg_max", [P, 2, H])
        m_parts = sb("m_parts", [P, 3, H, 2], BF16)
        m_rest = sb("m_rest", [P, H, 2])
        mT = sb("mT", [96, S], BF16)
        ident = sb("ident", [P, P])
        ident16 = sb("ident16", [P, P], BF16)
        w_raw = sb("w_raw", [P, 4, D])
        wT = sb("wT", [P, 4, D])
        stats = sb("stats", [P, B, 6])
        x_neg_mean = sb("x_neg_mean", [P, B])
        x_bias = sb("x_bias", [P, B])
        rstd = sb("rstd", [P, B])
        x_vare = sb("x_vare", [P, B])
        tmp_a = sb("tmp_a", [P, B])
        tmp_b = sb("tmp_b", [P, B])
        neg_half = sb("neg_half", [P, B])
        lens_i = sb("lens_i", [P, B], I32)
        lens_f = sb("lens_f", [P, B])
        key_id = sb("key_id", [P, 1])
        nonempty = sb("nonempty", [P, B])
        masked_f = sb("masked_f", [P, B])
        masked_i = sb("masked_i", [P, B], I32)
        keep = sb("keep", [P, B])

        w1_stage = [sb(f"w1_stage{i}", [P, FC, D]) for i in range(4)]
        w2_stage = [sb(f"w2_stage{i}", [P, F]) for i in range(4)]
        w1_rawT = [sb(f"w1_rawT{i}", [P, F]) for i in range(2)]
        w1T = sb("w1T", [P, E, F])
        w2T = sb("w2T", [P, E, FC * D])
        b1_in = sb("b1_in", [E * FC, P])
        b1T = sb("b1T", [P, E * FC])
        b2_row = sb("b2_row", [P, E, D])
        gammaT = sb("gammaT", [P, E])
        betaT = sb("betaT", [P, E])
        cent = sb("cent", [E, D])
        centT = sb("centT", [P, E])
        f_stats = sb("f_stats", [P, CB, 6])
        f_mv = sb("f_mv", [P, CB, 2])
        f_vare = sb("f_vare", [P, CB])
        f_rstd = sb("f_rstd", [P, CB])
        p_tmp = sb("p_tmp", [P, CB])
        eps_t = sb("eps_t", [P, CB])
        feats = sb("feats", [P, CB, D])
        featsT = sb("featsT", [P, TOK])
        rows = [sb(f"rows{i}", [P, CB, PW]) for i in range(2)]
        score = sb("score", [P, CB, E])
        best = sb("best", [P, CB, 1])
        gate_e = sb("gate_e", [P, CB, 1])
        choice = sb("choice", [P, CB, 1])
        cand = sb("cand", [P, CB, E])
        onehot = sb("onehot", [P, CB, E], BF16)
        here = sb("here", [P, E], BF16)
        before = sb("before", [P, E], BF16)
        place_f = sb("place_f", [P, CB, E])
        place = [sb(f"place{i}", [P, CB], I32) for i in range(2)]
        token_f = sb("token_f", [P, CB])
        expert_id = sb("expert_id", [P, E])
        expert_base = sb("expert_base", [P, E])
        upto = sb("upto", [P, P], BF16)
        ones16 = sb("ones16", [P, P], BF16)
        count = sb("count", [P, E])
        pad_place = sb("pad_place", [P, E], I32)
        tile_bound = sb("tile_bound", [P, T // P])
        has_tile = sb("has_tile", [P, E, T // P])
        tiles = sb("tiles", [P, E])
        ones_e = sb("ones_e", [P, E])
        tiles_to = sb("tiles_to", [P, E])
        tile_id = sb("tile_id", [P, NTILE])
        passed = sb("passed", [P, NTILE, E])
        tile_e = sb("tile_e", [P, NTILE, 1])
        tile_b = sb("tile_b", [P, NTILE, 1])
        tile_row = sb("tile_row", [P, NTILE], I32)
        tile_expert = sb("tile_expert", [P, NTILE], I32)
        empty = sb("empty", [P, PW])
        stack_mem = q_stack[0][:, :, :, :].rearrange("p s i t -> p (s i t)").bitcast(F32)
        tile_in = [stack_mem[:, 512 * i:512 * i + PW] for i in range(UN)]
        zT = [oT_raw[:, 0, P * i:P * (i + 1)] for i in range(4)]
        w1_now = w1_rawT
        w2_now = w2_stage[2:4]
        hidT = w2_stage
        y_sum = [oT_raw[:, 1, D * i:D * (i + 1)] for i in range(2)]
        y_out = [xn[:, i] for i in range(4)]

        s_bank = psum("s_bank", [P, 2, SG, S])
        st_bank = psum("st_bank", [P, 2, SG, S])
        pv_bank = psum("pv_bank", [P, 2, 4 * S])
        pj_bank = psum("pj_bank", [P, TOK])
        misc = psum("misc", [P, 512])
        mT_ps = misc[0:96, 384:384 + S // 2].bitcast(BF16)
        score_ps = misc[:, 448:448 + CB * E]
        rank_ps = misc[:, 480:480 + CB * E]

        names = ("weights_in ident_done x_in x_first lens_in ctx_in_s wt_done wt_copied const_done mask_done "
                 "stats_done ln_step ln_pow rstd_ready vare_ready ln_done xn_ready ctx_ready mchunk xT_done q_done cT_done k_done xT_ready ctxT_ready "
                 "q_hi k_hi q_rest_r k_rest_r q_mid k_mid q_lo k_lo keep_cols v_done v_ready scr_written "
                 "stack_in s_done max_done m_hi m_rest1 m_mid m_rest2 mp_ready mt_done mT_ready m_written m_in "
                 "st_done exp_done pv_done otraw_ready oq_done zinv_ready on_ready onT_done onT_ready "
                 "wo_done x1_done out_done0 out_done1 out_done2 out_done3 stack_init0 stack_init1 ones_init v_init pool_turn sp_turn "
                 "vec_in b2_in w_in0 w_in1 w_in2 w_in3 w1t_done w2t_done w1raw_ready w2T_ready beta_done w1T_ready b1_ready "
                 "route_init stat_step stats_ready route_vars pl_step feats_ready z_ready residual_ready best_ready choice_step here_ready before_ready rank_read fT_done fT_ready score_done "
                 "gate_exp place_step place_ready onehot_ready rank_done row_ready score_read vec_turn token_next scattered vec_turned vecT_ready "
                 "count_done table_step pad_ready padded0 padded1 table_ready tile_in0 tile_in1 tile_in2 tile_in3 tile_in4 tile_in5 tile_in6 tile_in7 "
                 "zt_done zT_ready up_done0 up_done1 w1_here w2_here hidT_ready0 hidT_ready1 down_done ysum_ready y_ready").split()
        s = {n: sem(n) for n in names}

        block = es.enter_context(nc.Block())

        CREDIT = 2
        PV_CREDIT = 4

        def load_expert(engine, e):
            engine.dma_start(w1_stage[e % 4][:, :, :], w1_dram[e].rearrange("(c f) d -> f c d", f=P)).then_inc(s[f"w_in{e % 4}"], 16)
            engine.dma_start(w2_stage[e % 4][:, :], w2_dram[e]).then_inc(s[f"w_in{e % 4}"], 16)

        def pad(engine, i):
            engine.wait_ge(s["pad_ready"], 1)
            for e in range(i * E // 2, (i + 1) * E // 2):
                row = engine.value_load(pad_place[0:1, e:e + 1], min_val=0, max_val=E * ROOM - P)
                engine.dma_start(routed[bass.ds(row, P), :], empty[:, :]).then_inc(s[f"padded{i}"], 16)

        @block.sync
        def _(sp):
            sp.dma_start(x_all[:, 0:CB, :], x_dram[0:CB].rearrange("b t d -> t b d")).then_inc(s["x_first"], 16)
            sp.dma_start(lens_i[:, :], lens_dram.rearrange("(o b) -> o b", o=1).broadcast_to([P, B])).then_inc(s["lens_in"], 16)
            sp.dma_start(x_all[:, CB:2 * CB, :], x_dram[CB:2 * CB].rearrange("b t d -> t b d")).then_inc(s["x_first"], 16)
            for i, w in enumerate((wq_dram, wk_dram, wv_dram, wo_dram)):
                sp.dma_start(w_raw[:, i, :], w).then_inc(s["weights_in"], 16)

            def load_ctx(c):
                src = ctx_dram[bass.ds(CB * c, CB)]
                sp.dma_start(ctx_in[:, :, :], src.rearrange("b t d -> t b d")).then_inc(s["ctx_in_s"], 16)
                sp.dma_start(ctx_first[:, :, :], src[:, 0:1, :].rearrange("b o d -> o b d").broadcast_to([P, CB, D])).then_inc(s["ctx_in_s"], 16)

            load_ctx(0)
            with nc.allow_non_contiguous_dma(reason="8 x 128 values"):
                sp.dma_start(gammaT[:, :], gamma_dram.rearrange("e d -> d e")).then_inc(s["vec_in"], 16)
                sp.dma_start(betaT[:, :], beta_dram.rearrange("e d -> d e")).then_inc(s["vec_in"], 16)
            sp.dma_start(cent[:, :], cent_dram).then_inc(s["vec_in"], 16)
            sp.dma_start(b1_in[:, :], b1_dram.rearrange("e (c f) -> (e c) f", f=P)).then_inc(s["vec_in"], 16)
            for c in range(2, NCH, 2):
                sp.dma_start(x_all[:, CB * c:CB * (c + 2), :], x_dram[CB * c:CB * (c + 2)].rearrange("b t d -> t b d")).then_inc(s["x_in"], 16)
            for e in range(E_FIRST):
                load_expert(sp, e)

            def load_stack(r, half, columns):
                q_rows = q_scr.rearrange("(s i d) c t -> i (d c) s t", i=2, d=DH)
                for i in range(2):
                    sp.dma_start(q_stack[r][HROWS * i:HROWS * (i + 1), :, i, columns], q_rows[i][:, :, columns]).then_inc(s["stack_in"], 16)
                sp.dma_start(k_stack[r][0:SROWS, :, columns], k_scr.rearrange("(s i) c t -> (i c) s t", i=16)[:, :, columns]).then_inc(s["stack_in"], 16)

            def step(t, r):
                k = 2 * t + r
                known = isinstance(t, int)
                if not known or 1 <= k <= NCH:
                    if not known or k >= 3:
                        sp.wait_ge(s["st_done"], SLOTS * (k - 2))
                    sp.wait_ge(s["stack_in"], 96 * (k - 1) + 48)
                    sp.sem_inc(s["sp_turn"])
                    load_stack((r + 1) % 2, 1, slice(TOK // 2, TOK))
                if not known or k < NCH - 1:
                    sp.wait_ge(s["cT_done"], k + 1)
                    sp.sem_inc(s["sp_turn"])
                    load_ctx(k + 1)
                if not known or k < NCH:
                    if not (known and k == 0):
                        sp.wait_ge(s["stack_in"], 96 * k)
                    for ready, scr, (lo, hi), parts, (first, end) in (("q_hi", q_scr, (0, 3), q_parts, (0, 1)),
                                                                     ("q_mid", q_scr, (3, 5), q_parts, (1, 2)),
                                                                     ("q_lo", q_scr, (5, 6), q_parts, (2, 3)),
                                                                     ("k_hi", k_scr, (5, 6), k_parts, (0, 1)),
                                                                     ("k_mid", k_scr, (3, 5), k_parts, (0, 2)),
                                                                     ("k_lo", k_scr, (0, 3), k_parts, (0, 3))):
                        sp.wait_ge(s[ready], k + 1)
                        part = parts[:, first:end, :]
                        if hi - lo > end - first:
                            part = part.broadcast_to([P, hi - lo, TOK])
                        sp.dma_start(scr[:, lo:hi, :], part).then_inc(s["scr_written"], 16)
                    sp.wait_ge(s["scr_written"], 96 * (k + 1))
                    if not known or k >= 2:
                        sp.wait_ge(s["st_done"], SLOTS * (k - 2) + SLOTS // 2)
                    if known and k < 2:
                        sp.wait_ge(s[f"stack_init{r}"], 1)
                    sp.sem_inc(s["sp_turn"])
                    load_stack(r, 0, slice(0, TOK // 2))

            step(0, 0)
            for e in range(E_FIRST, 4):
                load_expert(sp, e)
            sp.dma_start(b2_row[:, :, :], b2_dram.rearrange("(o e) d -> o e d", o=1).broadcast_to([P, E, D])).then_inc(s["b2_in"], 16)
            step(0, 1)
            step(1, 0)
            step(1, 1)
            with sp.Fori(2, NCH // 2 - 1) as t:
                step(t, 0)
                step(t, 1)
            step(NCH // 2 - 1, 0)
            step(NCH // 2 - 1, 1)
            step(NCH // 2, 0)

            pad(sp, 0)
            sp.wait_ge(s["scattered"], 16 * (B + 1))
            for i in range(2):
                sp.wait_ge(s[f"padded{i}"], 16 * E // 2)
            sp.wait_ge(s["table_ready"], 1)

            def load_tile(t, q):
                i = UN * t + q
                if not (isinstance(t, int) and t == 0):
                    sp.wait_ge(s["y_ready"], i - UN + 1)
                    sp.sem_inc(s["sp_turn"])
                    sp.wait_ge(s[f"out_done{q % 4}"], 16 * (2 * t + q // 4 - 1))
                    sp.sem_inc(s["sp_turn"])
                row = sp.value_load(tile_row[0:1, bass.ds(i, 1)], min_val=0, max_val=E * ROOM)
                sp.dma_start(tile_in[q], routed[bass.ds(row, P), :]).then_inc(s[f"tile_in{q}"], 16)

            for q in range(UN):
                load_tile(0, q)
            with sp.Fori(1, NTILE // UN) as t:
                for q in range(UN):
                    load_tile(t, q)
            for q in range(4):
                sp.wait_ge(s[f"out_done{q}"], 16 * (NTILE // 4))

        @block.gpsimd
        def _(pool):
            def stack_constants(i):
                pool.memset(q_stack[i][:, :, :, :].rearrange("p a b t -> p (a b t)").bitcast(F32), 0.0).then_inc(s[f"stack_init{i}"], 1)

            def deviations(i, bs):
                pool.wait_ge(s["vare_ready"], i + 1)
                pool.tensor_tensor(rstd[:, bs], x_vare[:, bs], neg_half[:, bs], ALU.pow).then_inc(s["ln_pow"], 1)

            pool.iota(key_id[:, :], pattern=[[0, 1]], base=0, channel_multiplier=1,
                      allow_small_or_imprecise_dtypes=True).then_inc(s["const_done"], 1)
            for m in (ident, ident16):
                pool.memset(m[:, :], 0.0).then_inc(s["ident_done"], 1)
            pool.wait_ge(s["ident_done"], 2)
            for m in (ident, ident16):
                pool.affine_select(out=m[:, :], in_=m[:, :], compare_op=ALU.not_equal, fill=1.0, base=0,
                                   pattern=[[-1, P]], channel_multiplier=1).then_inc(s["ident_done"], 1)
            pool.memset(neg_half[:, :], -0.5).then_inc(s["const_done"], 1)
            pool.wait_ge(s["const_done"], 2)
            stack_constants(0)
            deviations(0, slice(0, 2 * CB))
            pool.memset(v_blk[0][:, :, :, :], 0.0).then_inc(s["v_init"], 1)
            def constants():
                pool.memset(v_blk[1][:, :, :, :], 0.0).then_inc(s["v_init"], 1)
                stack_constants(1)
                deviations(1, slice(2 * CB, B))
                pool.memset(empty[:, :], 0.0).then_inc(s["pool_turn"], 1)
                pool.memset(eps_t[:, :], EPS)
                pool.memset(ones16[:, :], 1.0)
                pool.memset(ones_e[:, :], 1.0)
                pool.memset(before[:, :], 0.0)
                for i in range(2):
                    pool.memset(rows[i][:, :, TOKEN + 1:PW], 0.0)
                pool.memset(upto[:, :], 1.0).then_inc(s["route_init"], 1)
                pool.wait_ge(s["route_init"], 1)
                pool.memset(empty[:, TOKEN:TOKEN + 1].bitcast(I32), NOWHERE).then_inc(s["route_init"], 1)
                pool.affine_select(out=upto[:, :], in_=upto[:, :], compare_op=ALU.is_gt, fill=0.0, base=0,
                                   pattern=[[1, P]], channel_multiplier=-1)
                pool.iota(expert_id[:, :], pattern=[[1, E]], base=0, channel_multiplier=0, allow_small_or_imprecise_dtypes=True)
                pool.iota(expert_base[:, :], pattern=[[ROOM, E]], base=0, channel_multiplier=0, allow_small_or_imprecise_dtypes=True)
                pool.iota(tile_bound[:, :], pattern=[[P, T // P]], base=0, channel_multiplier=0, allow_small_or_imprecise_dtypes=True)
                pool.iota(tile_id[:, :], pattern=[[1, NTILE]], base=0, channel_multiplier=0, allow_small_or_imprecise_dtypes=True)
                pool.iota(token_f[:, :], pattern=[[S, CB]], base=0, channel_multiplier=1,
                          allow_small_or_imprecise_dtypes=True).then_inc(s["route_init"], 1)
                pool.wait_ge(s["route_init"], 3)
                pool.dma_start(routed[E * ROOM:E * ROOM + P, :], empty[:, :]).then_inc(s["scattered"], 16)

            def route_vars(c):
                steps = ((f_rstd, f_vare[:, :], neg_half[:, 0:CB], ALU.pow), (p_tmp, f_rstd[:, :], f_rstd[:, :], ALU.mult),
                         (p_tmp, p_tmp[:, :], f_mv[:, :, 1], ALU.mult), (p_tmp, p_tmp[:, :], eps_t[:, :], ALU.add),
                         (p_tmp, p_tmp[:, :], neg_half[:, 0:CB], ALU.pow))
                pool.wait_ge(s["route_vars"], c + 1)
                for i, (out, a, b, op) in enumerate(steps):
                    if i:
                        pool.wait_ge(s["pl_step"], NPL * c + i)
                    pool.tensor_tensor(out[:, :], a, b, op).then_inc(s["pl_step"], 1)
                assert NPL == len(steps)

            def residual(c, buf):
                if not (isinstance(c, int) and c == 0):
                    pool.wait_ge(s["scattered"], 16 + 16 * CB * (c - 1))
                pool.wait_ge(s["feats_ready"], c + 1)
                pool.tensor_tensor(rows[buf][:, :, D:2 * D], feats[:, :, :], x_all[:, bass.ds(CB * c, CB), :], ALU.add).then_inc(s["residual_ready"], 1)

            def normalise_again(c, buf):
                if not (isinstance(c, int) and c == 0):
                    pool.wait_ge(s["scattered"], 16 + 16 * CB * (c - 1))
                pool.wait_ge(s["pl_step"], NPL * (c + 1))
                pool.wait_ge(s["feats_ready"], c + 1)
                pool.tensor_tensor(rows[buf][:, :, 0:D], feats[:, :, :], p_tmp[:, :].unsqueeze(2).broadcast_to([P, CB, D]), ALU.mult).then_inc(s["z_ready"], 1)

            def scatter(c, buf):
                pool.wait_ge(s["residual_ready"], c + 1)
                pool.wait_ge(s["z_ready"], c + 1)
                pool.wait_ge(s["place_ready"], c + 1)
                pool.sem_inc(s["pool_turn"])
                for b in range(CB):
                    pool.indirect_dma_start(out=routed, out_offset=bass.IndirectOffsetOnAxis(ap=place[buf][:, b:b + 1], axis=0),
                                            in_=rows[buf][:, b, :], in_offset=None).then_inc(s["scattered"], 16)

            def low_part(k, parts, rest, ready, lo):
                pool.wait_ge(s[ready], k + 1)
                pool.tensor_tensor(parts[:, 2, :], rest[:, :], parts[:, 1, :], ALU.subtract).then_inc(s[lo], 1)

            def keep_columns(c, buf):
                if isinstance(c, int) and c == 0:
                    pool.wait_ge(s["v_init"], 2)
                if not (isinstance(c, int) and c < 2):
                    pool.wait_ge(s["pv_done"], PV_CREDIT + SLOTS * (c - 1))
                pool.sem_inc(s["pool_turn"])
                pool.tensor_copy(v_blk[buf][:, :, :, DH:2 * DH],
                                 keep[:, bass.ds(CB * c, CB)].unsqueeze(2).unsqueeze(3).broadcast_to([P, CB, H, DH])).then_inc(s["keep_cols"], 1)

            def step(t, r):
                k = 2 * t + r
                known = isinstance(t, int)
                if not known or k < NCH:
                    low_part(k, q_parts, q_rest, "q_mid", "q_lo")
                if not known or 1 <= k <= NCH:
                    keep_columns(k - 1, (r + 1) % 2)
                if not known or k < NCH:
                    low_part(k, k_parts, k_rest, "k_mid", "k_lo")
                if not known or 3 <= k < NCH + 3:
                    route_vars(k - 3)
                    residual(k - 3, (r + 1) % 2)
                    normalise_again(k - 3, (r + 1) % 2)
                if not known or 4 <= k < NCH + 4:
                    scatter(k - 4, r)

            step(0, 0)
            constants()
            for k in range(1, 4):
                step(k // 2, k % 2)
            with pool.Fori(2, NCH // 2) as t:
                step(t, 0)
                step(t, 1)
            for k in range(NCH, STEPS):
                step(k // 2, k % 2)
            out_rows = out_dram.rearrange("b t d -> (b t) d")

            def store(t, q):
                pool.wait_ge(s["y_ready"], UN * t + q + 1)
                pool.sem_inc(s["pool_turn"])
                pool.indirect_dma_start(out=out_rows, out_offset=bass.IndirectOffsetOnAxis(ap=tile_in[q][:, TOKEN:TOKEN + 1].bitcast(I32), axis=0),
                                        in_=y_out[q % 4], in_offset=None, bounds_check=T - 1, oob_is_err=False).then_inc(s[f"out_done{q % 4}"], 16)

            with pool.Fori(0, NTILE // UN) as t:
                for q in range(UN):
                    store(t, q)

        @block.scalar
        def _(act):
            act.sem_inc(s["exp_done"], CREDIT)
            act.sem_inc(s["otraw_ready"], CREDIT)
            act.wait_ge(s["wt_done"], 1)
            act.activation(wT[:, :, :].rearrange("p a b -> p (a b)"), pj_bank[:, :], ACT.Copy).then_inc(s["wt_copied"], 1)

            def expert_weights(e):
                r = e % 2
                act.wait_ge(s["w1t_done"], e + 1)
                if e >= 2:
                    act.wait_ge(s["beta_done"], e - 1)
                    act.wait_ge(s["w1T_ready"], e - 1)
                act.activation(w1_rawT[r][:, :], st_bank[:, r].rearrange("p a b -> p (a b)"), ACT.Copy).then_inc(s["w1raw_ready"], 1)
                act.wait_ge(s["w2t_done"], e + 1)
                act.activation(w2T[:, e, :], pv_bank[:, r, :], ACT.Copy).then_inc(s["w2T_ready"], 1)
                if E_FIRST <= e and e + 2 < E:
                    load_expert(act, e + 2)

            def normalise(c, batches):
                act.wait_ge(s["ln_done"], (1 if isinstance(c, int) and c < 2 else 2))
                for b in batches:
                    act.activation(xn[:, b, :], x_all[:, bass.ds(CB * c + b, 1), :].rearrange("p o d -> p (o d)"), ACT.Identity,
                                   bias=x_bias[:, bass.ds(CB * c + b, 1)], scale=rstd[:, bass.ds(CB * c + b, 1)]).then_inc(s["xn_ready"], 1)

            def outputs_out(c, b):
                act.wait_ge(s["pv_done"], PV_CREDIT + SLOTS * c + 4 * b + 4)
                act.wait_ge(s["oq_done"], CB * c + b + 1)
                act.activation(oT_raw[:, b % 2, :], pv_bank[:, b % 2, :], ACT.Copy).then_inc(s["otraw_ready"], 1)

            def normed_out(c, b):
                act.wait_ge(s["onT_done"], 1 + CB * c + b + 1)
                act.activation(oT_norm[:, :], misc[:, 0:S], ACT.Copy).then_inc(s["onT_ready"], 1)

            def max_out(c, half):
                act.wait_ge(s["mt_done"], 2 * c + half + 1)
                if not (isinstance(c, int) and c == 0 and half == 0):
                    act.wait_ge(s["m_in"], 16 * (2 * c + half))
                act.activation(mT[:, :], mT_ps, ACT.Copy).then_inc(s["mT_ready"], 1)
                act.wait_ge(s["mT_ready"], 2 * c + half + 1)
                act.dma_start(m_scr, mT[:, :]).then_inc(s["m_written"], 16)

            def max_rows(c, half, buf):
                act.wait_ge(s["m_written"], 16 * (2 * c + half + 1))
                act.dma_start(q_stack[buf][SROWS:MROWS, :, :, 2 * S * half:2 * S * (half + 1)].rearrange("p s i t -> p (s i) t"),
                              m_scr.rearrange("(p h b) t -> p h (b t)", p=3, b=2)).then_inc(s["m_in"], 16)

            def step(t, r):
                k = 2 * t + r
                known = isinstance(t, int)
                proj, vals, sc = (not known or a <= k < a + NCH for a in (0, 1, 1))
                st, tail, pick = (not known or a <= k < a + NCH for a in (2, 3, 4))
                more = not known or k < NCH - 1
                xt, qq, ct, kk, keys_bank = (0, 1, 0, 1, misc) if known and k == 0 else (XT, QQ, CT, KK, pj_bank)
                for pos in range(POS):
                    if st:
                        act.wait_ge(s["st_done"], SLOTS * (k - 2) + pos + 1)
                        act.wait_ge(s["pv_done"], SLOTS * (k - 2) + pos + 1)
                        act.activation(e_ring[:, pos % 4], st_bank[:, pos % 2], ACT.Exp).then_inc(s["exp_done"], 1)
                    if proj and pos == xt:
                        act.wait_ge(s["xT_done"], k + 1)
                        act.activation(xnT[:, :], pj_bank[:, :], ACT.Copy).then_inc(s["xT_ready"], 1)
                    if proj and pos == qq:
                        act.wait_ge(s["q_done"], k + 1)
                        if not (known and k == 0):
                            act.wait_ge(s["scr_written"], 96 * k)
                        act.activation(q_parts[:, 0, :], pj_bank[:, :], ACT.Copy, scale=QSCALE).then_inc(s["q_hi"], 1)
                    if proj and pos == qq + 2:
                        act.wait_ge(s["q_rest_r"], k + 1)
                        act.activation(q_parts[:, 1, :], q_rest[:, :], ACT.Copy).then_inc(s["q_mid"], 1)
                    if vals and pos == VV:
                        act.wait_ge(s["v_done"], k)
                        if known and k == 1:
                            act.wait_ge(s["v_init"], 2)
                        if not known or k >= 3:
                            act.wait_ge(s["pv_done"], PV_CREDIT + SLOTS * (k - 2))
                        for b in range(CB):
                            act.activation(v_blk[(r + 1) % 2][:, b, :, 0:DH], pj_bank[:, S * b:S * (b + 1)].rearrange("p (h d) -> p h d", h=H),
                                           ACT.Copy, scale=keep[:, bass.ds(CB * (k - 1) + b, 1)]).then_inc(s["v_ready"], 1)
                    if proj and pos == ct:
                        act.wait_ge(s["cT_done"], k + 1)
                        act.activation(ctxT[r][:, :], keys_bank[:, :], ACT.Copy).then_inc(s["ctxT_ready"], 1)
                    if proj and pos == kk:
                        act.wait_ge(s["k_done"], k + 1)
                        act.activation(k_parts[:, 0, :], keys_bank[:, :], ACT.Copy).then_inc(s["k_hi"], 1)
                    if proj and pos == kk + 2:
                        act.wait_ge(s["k_rest_r"], k + 1)
                        act.activation(k_parts[:, 1, :], k_rest[:, :], ACT.Copy).then_inc(s["k_mid"], 1)
                    if st and pos in (5, 9, 13):
                        outputs_out(k - 2, (pos - 5) // 4)
                    if tail and pos == 1:
                        outputs_out(k - 3, 3)
                    if st and pos in (8, 12):
                        normed_out(k - 2, (pos - 8) // 4)
                    if tail and pos in (0, 4):
                        normed_out(k - 3, 2 + pos // 4)
                    if sc and pos == 10:
                        max_out(k - 1, 0)
                    if sc and pos == 13:
                        max_rows(k - 1, 0, (r + 1) % 2)
                    if st and pos == 2:
                        max_out(k - 2, 1)
                    if st and pos == 4:
                        max_rows(k - 2, 1, r)
                    if pick and pos == 3:
                        act.wait_ge(s["best_ready"], k - 3)
                        act.activation(gate_e[:, :, :], best[:, :, :], ACT.Exp, scale=-1.0).then_inc(s["gate_exp"], 1)
                    if tail and pos == FT:
                        act.wait_ge(s["fT_done"], k - 2)
                        act.activation(featsT[:, :], pj_bank[:, :], ACT.Copy).then_inc(s["fT_ready"], 1)
                    if more and pos in XN_AT and not (known and k == 1):
                        act.wait_ge(s["xT_done"], k + 1)
                        normalise(k + 1, XN_AT[pos])
                    if known and k == 1 and pos == 14:
                        act.wait_ge(s["xT_done"], k + 1)
                        normalise(k + 1, range(CB))
                    if known and k == 1 and pos in PREPARE:
                        expert_weights(PREPARE.index(pos) + E_FIRST)

            normalise(0, range(CB))
            step(0, 0)
            act.wait_ge(s["vec_turned"], 1)
            act.activation(centT[:, :], pj_bank[:, 0:E], ACT.Copy)
            act.activation(b1T[:, :], pj_bank[:, 64:64 + E * FC], ACT.Copy).then_inc(s["vecT_ready"], 1)
            for e in range(E_FIRST):
                expert_weights(e)
            for k in range(1, 4):
                if k == 3:
                    act.wait_ge(s["route_init"], 3)
                step(k // 2, k % 2)
            with act.Fori(2, NCH // 2 - 1) as t:
                step(t, 0)
                step(t, 1)
            for k in range(NCH - 2, STEPS):
                step(k // 2, k % 2)

            def fetch_w1(t, q):
                i = UN * t + q
                e = act.value_load(tile_expert[0:1, bass.ds(i, 1)], min_val=0, max_val=E - 1)
                if not (isinstance(t, int) and i < 2):
                    act.wait_ge(s["up_done1"], i - 1)
                act.activation(w1_now[q % 2][:, :], w1T[:, bass.ds(e, 1), :].rearrange("p o n -> p (o n)"), ACT.Copy).then_inc(s["w1_here"], 1)
                return e

            def turned_z(t, q):
                i = UN * t + q
                act.wait_ge(s["zt_done"], i + 1)
                if not (isinstance(t, int) and i < 4):
                    act.wait_ge(s["up_done1"], i - 3)
                act.activation(zT[q % 4], (misc, pj_bank)[q % 2][:, 0:P], ACT.Copy).then_inc(s["zT_ready"], 1)

            def hidden(t, q, e):
                i = UN * t + q
                act.wait_ge(s["up_done1"], i + 1)
                if not (isinstance(t, int) and i < 2):
                    act.wait_ge(s["down_done"], i - 1)
                for c in SIDES[1]:
                    last = act.activation(hidT[q % 2][:, P * c:P * (c + 1)], st_bank[:, q % 2, c, :], ACT.Relu,
                                          bias=b1T[:, bass.ds(FC * e + c, 1)])
                last.then_inc(s["hidT_ready1"], 1)

            pad(act, 1)
            act.wait_ge(s["table_ready"], 1)
            fetch_w1(0, 0)
            turned_z(0, 0)
            turned_z(0, 1)

            def tiles_of(t, last):
                e = act.value_load(tile_expert[0:1, bass.ds(UN * t, 1)], min_val=0, max_val=E - 1)
                for q in range(UN):
                    e_next = None if last and q == UN - 1 else fetch_w1(t if q < UN - 1 else t + 1, (q + 1) % UN)
                    hidden(t, q, e)
                    e = e_next
                    if not (last and q >= UN - 2):
                        turned_z(t if q < UN - 2 else t + 1, (q + 2) % UN)

            tiles_of(0, False)
            with act.Fori(1, NTILE // UN - 1) as t:
                tiles_of(t, False)
            tiles_of(NTILE // UN - 1, True)

        @block.vector
        def _(dve):
            dve.sem_inc(s["max_done"], CREDIT)
            dve.sem_inc(s["x1_done"], 1)
            def ones_rows(i):
                dve.memset(k_stack[i][SROWS:MROWS, :, :].rearrange("p s t -> p (s t)").bitcast(F32), ONE_ONE).then_inc(s["ones_init"], 1)

            ones_rows(0)
            dve.wait_ge(s["lens_in"], 16)
            dve.wait_ge(s["const_done"], 1)
            dve.tensor_copy(lens_f[:, :], lens_i[:, :]).then_inc(s["mchunk"], 1)
            dve.wait_ge(s["mchunk"], 1)
            dve.tensor_scalar(nonempty[:, :], lens_f[:, :], 0.0, None, ALU.is_gt).then_inc(s["mchunk"], 1)
            dve.tensor_scalar(masked_f[:, :], lens_f[:, :], key_id[:, 0:1], None, ALU.is_le).then_inc(s["mchunk"], 1)
            dve.wait_ge(s["mchunk"], 3)
            dve.tensor_tensor(tmp_a[:, :], masked_f[:, :], nonempty[:, :], ALU.mult).then_inc(s["mchunk"], 1)
            dve.wait_ge(s["mchunk"], 4)
            dve.tensor_copy(masked_i[:, :], tmp_a[:, :]).then_inc(s["mchunk"], 1)
            dve.tensor_scalar(keep[:, :], tmp_a[:, :], -1.0, 1.0, ALU.mult, ALU.add).then_inc(s["mask_done"], 1)
            def x_stats(i, lo, hi):
                if i == 0:
                    dve.wait_ge(s["x_first"], 32)
                    for b in range(lo, hi):
                        last = dve.bn_stats(stats[:, b, :], x_all[:, b, :])
                    last.then_inc(s["stats_done"], 1)
                    dve.wait_ge(s["stats_done"], 1)
                else:
                    dve.wait_ge(s["x_in"], 16 * (NCH // 2 - 1))
                    with dve.Fori(lo // 8, hi // 8) as c:
                        for b in range(8):
                            last = dve.bn_stats(stats[:, bass.ds(8 * c + b, 1), :], x_all[:, bass.ds(8 * c + b, 1), :])
                        last.then_inc(s["stats_done"], 1)
                    dve.wait_ge(s["stats_done"], 1 + (hi - lo) // 8)
                bs = slice(lo, hi)
                n = 3 * i
                dve.tensor_tensor(x_neg_mean[:, bs], stats[:, bs, 1], stats[:, bs, 4], ALU.add)
                dve.tensor_tensor(tmp_a[:, bs], stats[:, bs, 1], stats[:, bs, 4], ALU.subtract)
                dve.tensor_tensor(tmp_b[:, bs], stats[:, bs, 2], stats[:, bs, 5], ALU.add).then_inc(s["ln_step"], 1)
                dve.wait_ge(s["ln_step"], n + 1)
                dve.tensor_scalar(x_neg_mean[:, bs], x_neg_mean[:, bs], -0.5, None, ALU.mult)
                dve.scalar_tensor_tensor(out=tmp_a[:, bs], in0=tmp_a[:, bs], scalar=D / 4.0, in1=tmp_a[:, bs], op0=ALU.mult,
                                         op1=ALU.mult).then_inc(s["ln_step"], 1)
                dve.wait_ge(s["ln_step"], n + 2)
                dve.tensor_tensor(tmp_b[:, bs], tmp_b[:, bs], tmp_a[:, bs], ALU.add).then_inc(s["ln_step"], 1)
                dve.wait_ge(s["ln_step"], n + 3)
                dve.tensor_scalar(x_vare[:, bs], tmp_b[:, bs], 1.0 / D, EPS, ALU.mult, ALU.add).then_inc(s["vare_ready"], 1)

            def x_scales(i, lo, hi):
                dve.wait_ge(s["ln_pow"], i + 1)
                dve.tensor_tensor(rstd[:, lo:hi], rstd[:, lo:hi], nonempty[:, lo:hi], ALU.mult).then_inc(s["rstd_ready"], 1)
                dve.wait_ge(s["rstd_ready"], i + 1)
                dve.tensor_tensor(x_bias[:, lo:hi], x_neg_mean[:, lo:hi], rstd[:, lo:hi], ALU.mult).then_inc(s["ln_done"], 1)

            def mask_ctx(c):
                dve.tensor_copy(mask_chunk[:, :], masked_i[:, bass.ds(CB * c, CB)]).then_inc(s["mchunk"], 1)
                dve.wait_ge(s["mchunk"], 6 + c)
                dve.wait_ge(s["ctx_in_s"], 32 * (c + 1))
                dve.copy_predicated(ctx_in[:, :, :], mask_chunk[:, :].unsqueeze(2).broadcast_to([P, CB, D]), ctx_first[:, :, :]).then_inc(s["ctx_ready"], 1)

            x_stats(0, 0, 2 * CB)
            mask_ctx(0)
            x_scales(0, 0, 2 * CB)
            ones_rows(1)

            def max_parts(c, bp, known):
                nm = neg_max[:, :, :].rearrange("q b h -> q h b")
                dve.wait_ge(s["max_done"], CREDIT + SLOTS * c + 8 * bp + 8)
                if not (known and c == 0 and bp == 0):
                    dve.wait_ge(s["mt_done"], 2 * c + bp)
                n = 2 * c + bp + 1
                dve.tensor_copy(m_parts[:, 0], nm).then_inc(s["m_hi"], 1)
                dve.wait_ge(s["m_hi"], n)
                dve.tensor_tensor(m_rest[:, :, :], nm, m_parts[:, 0], ALU.subtract).then_inc(s["m_rest1"], 1)
                dve.wait_ge(s["m_rest1"], n)
                dve.tensor_copy(m_parts[:, 1], m_rest[:, :, :]).then_inc(s["m_mid"], 1)
                dve.wait_ge(s["m_mid"], n)
                dve.tensor_tensor(m_parts[:, 2], m_rest[:, :, :], m_parts[:, 1], ALU.subtract).then_inc(s["mp_ready"], 1)

            def expert_weights(e):
                r = e % 2
                dve.wait_ge(s["w1raw_ready"], e + 1)
                dve.tensor_scalar(w1T[:, e, :], w1_rawT[r][:, :], gammaT[:, e:e + 1], None, ALU.mult).then_inc(s["w1T_ready"], 1)

            def hidden_bias(e):
                r = e % 2
                dve.wait_ge(s["beta_done"], e + 1)
                br = b1T[:, FC * e:FC * (e + 1)]
                dve.tensor_tensor(br, st_bank[:, r, 0, 0:FC], br, ALU.add).then_inc(s["b1_ready"], 1)

            def row_stats(c, batches):
                dve.wait_ge(s["x1_done"], 1 + CB * c + batches[-1] + 1)
                for b in batches:
                    dve.bn_stats(f_stats[:, b, :], x_all[:, bass.ds(CB * c + b, 1), :]).then_inc(s["stat_step"], 1)

            def moments(c):
                if not (isinstance(c, int) and c == 0):
                    dve.wait_ge(s["pl_step"], NPL * c)
                dve.wait_ge(s["stat_step"], CB * (c + 1))
                dve.sem_inc(s["vec_turn"])
                for b in range(CB):
                    last = dve.bn_aggr(f_mv[:, b, :], f_stats[:, b, :])
                last.then_inc(s["stats_ready"], 1)
                dve.wait_ge(s["stats_ready"], c + 1)
                dve.tensor_scalar(f_vare[:, :], f_mv[:, :, 1], EPS, None, ALU.add).then_inc(s["route_vars"], 1)

            def normalise_rows(c):
                dve.wait_ge(s["pl_step"], NPL * c + 1)
                if not (isinstance(c, int) and c == 0):
                    dve.wait_ge(s["residual_ready"], c)
                    dve.wait_ge(s["z_ready"], c)
                    dve.wait_ge(s["fT_done"], c)
                for b in range(CB):
                    last = dve.tensor_scalar(feats[:, b, :], x_all[:, bass.ds(CB * c + b, 1), :].rearrange("p o d -> p (o d)"),
                                             f_mv[:, b, 0:1], f_rstd[:, b:b + 1], ALU.subtract, ALU.mult)
                last.then_inc(s["feats_ready"], 1)

            wide = [P, CB, E]
            every_expert = expert_id[:, :].unsqueeze(1).broadcast_to(wide)

            def choose(c, part):
                n = 3 * c
                if part == 0:
                    dve.wait_ge(s["score_done"], c + 1)
                    dve.tensor_copy(score[:, :, :], score_ps.rearrange("p (b e) -> p b e", e=E)).then_inc(s["score_read"], 1)
                    dve.wait_ge(s["score_read"], c + 1)
                    dve.tensor_reduce(best[:, :, 0], score[:, :, :], AX.X, ALU.max).then_inc(s["best_ready"], 1)
                if part == 1:
                    dve.wait_ge(s["best_ready"], c + 1)
                    dve.tensor_tensor(cand[:, :, :], score[:, :, :], best[:, :, :].broadcast_to(wide), ALU.is_lt).then_inc(s["choice_step"], 1)
                if part == 2:
                    dve.wait_ge(s["choice_step"], n + 1)
                    dve.scalar_tensor_tensor(out=cand[:, :, :], in0=cand[:, :, :], scalar=float(E), in1=every_expert,
                                             op0=ALU.mult, op1=ALU.add).then_inc(s["choice_step"], 1)
                if part == 3:
                    dve.wait_ge(s["choice_step"], n + 2)
                    dve.tensor_reduce(choice[:, :, 0], cand[:, :, :], AX.X, ALU.min).then_inc(s["choice_step"], 1)
                if part == 4:
                    dve.wait_ge(s["choice_step"], n + 3)
                    dve.tensor_tensor(onehot[:, :, :], choice[:, :, :].broadcast_to(wide), every_expert, ALU.is_equal).then_inc(s["onehot_ready"], 1)

            def placing(c, buf, part):
                if part == 0:
                    dve.wait_ge(s["onehot_ready"], c + 1)
                    with nc.allow_low_precision(reason="counts up to 32"):
                        dve.tensor_reduce(here[:, :], onehot[:, :, :].rearrange("p b e -> p e b"), AX.X, ALU.add).then_inc(s["here_ready"], 1)
                    dve.wait_ge(s["rank_done"], c + 1)
                    dve.tensor_tensor(place_f[:, :, :], rank_ps.rearrange("p (b e) -> p b e", e=E),
                                      expert_base[:, :].unsqueeze(1).broadcast_to(wide), ALU.add).then_inc(s["rank_read"], 1)
                    dve.wait_ge(s["gate_exp"], c + 1)
                    dve.tensor_scalar(gate_e[:, :, :], gate_e[:, :, :], 1.0, None, ALU.add).then_inc(s["place_step"], 1)
                if part == 1:
                    dve.wait_ge(s["rank_read"], c + 1)
                    dve.tensor_tensor(place_f[:, :, :], place_f[:, :, :], onehot[:, :, :], ALU.mult).then_inc(s["place_step"], 1)
                    dve.wait_ge(s["here_ready"], c + 1)
                    dve.tensor_tensor(before[:, :], before[:, :], here[:, :], ALU.add).then_inc(s["before_ready"], 1)
                if part == 2:
                    if not (isinstance(c, int) and c == 0):
                        dve.wait_ge(s["scattered"], 16 + 16 * CB * (c - 1))
                    dve.wait_ge(s["place_step"], 2 * c + 2)
                    dve.reciprocal(rows[buf][:, :, GATE:GATE + 1], gate_e[:, :, :])
                    dve.tensor_copy(rows[buf][:, :, TOKEN].bitcast(I32), token_f[:, :]).then_inc(s["row_ready"], 1)
                    with nc.allow_low_precision(reason="whole numbers below 2**24, one of them not zero"):
                        dve.tensor_reduce(place[buf][:, :], place_f[:, :, :], AX.X, ALU.add).then_inc(s["place_ready"], 1)
                    dve.wait_ge(s["row_ready"], c + 1)
                    dve.tensor_scalar(token_f[:, :], token_f[:, :], float(TOK), None, ALU.add).then_inc(s["token_next"], 1)
                    dve.wait_ge(s["token_next"], c + 1)

            def weigh(c, b):
                oq = misc[:, :].rearrange("q (h w) -> q h w", w=VW)
                n = CB * c + b
                dve.wait_ge(s["oq_done"], CREDIT + n + 1)
                dve.reciprocal(z_inv[:, :, :], oq[:, :, DH:DH + 1]).then_inc(s["zinv_ready"], 1)
                dve.wait_ge(s["zinv_ready"], n + 1)
                dve.wait_ge(s["onT_done"], 1 + n)
                dve.tensor_tensor(o_norm[:, :, :], oq[:, :, 0:DH], z_inv[:, :, :].broadcast_to([P, H, DH]), ALU.mult).then_inc(s["on_ready"], 1)

            def add_to_x(c, b):
                dve.wait_ge(s["wo_done"], CB * c + b + 1)
                xr = x_all[:, bass.ds(CB * c + b, 1), :].rearrange("p o d -> p (o d)")
                dve.tensor_tensor(xr, misc[:, S:2 * S], xr, ALU.add).then_inc(s["x1_done"], 1)

            def step(t, r):
                k = 2 * t + r
                known = isinstance(t, int)
                proj, sc = (not known or a <= k < a + NCH for a in (0, 1))
                st, tail, pick = (not known or a <= k < a + NCH for a in (2, 3, 4))
                more = not known or k < NCH - 1
                xt, qq, ct, kk, keys_bank = (0, 1, 0, 1, misc) if known and k == 0 else (XT, QQ, CT, KK, pj_bank)
                for pos in range(POS):
                    if tail and pos in (2, 6):
                        add_to_x(k - 3, 2 + pos // 4)
                    if st and pos in (10, 14):
                        add_to_x(k - 2, (pos - 10) // 4)
                    if proj and pos == qq + 1:
                        dve.wait_ge(s["q_hi"], k + 1)
                        if not (known and k == 0):
                            dve.wait_ge(s["q_lo"], k)
                        dve.scalar_tensor_tensor(out=q_rest[:, :], in0=pj_bank[:, :], scalar=QSCALE, in1=q_parts[:, 0, :],
                                                 op0=ALU.mult, op1=ALU.subtract).then_inc(s["q_rest_r"], 1)
                    if proj and pos == kk + 1:
                        dve.wait_ge(s["k_hi"], k + 1)
                        if not (known and k == 0):
                            dve.wait_ge(s["k_lo"], k)
                        dve.tensor_tensor(k_rest[:, :], keys_bank[:, :], k_parts[:, 0, :], ALU.subtract).then_inc(s["k_rest_r"], 1)
                    if pick and pos < 4:
                        choose(k - 4, pos + 1)
                    if sc:
                        dve.wait_ge(s["s_done"], SLOTS * (k - 1) + pos + 1)
                        if pos % 8 == 0 and not (known and k == 1 and pos == 0):
                            dve.wait_ge(s["mp_ready"], 2 * (k - 1) + pos // 8)
                        dve.tensor_reduce(neg_max[:, (pos // 4) % 2, SG * (pos % 4):SG * (pos % 4 + 1)], s_bank[:, pos % 2], AX.X, ALU.max,
                                          negate=True).then_inc(s["max_done"], 1)
                    if tail and pos == 14:
                        choose(k - 3, 0)
                    if st and pos in (7, 11, 15):
                        weigh(k - 2, (pos - 7) // 4)
                    if sc and pos % 8 == 7:
                        max_parts(k - 1, pos // 8, known)
                    if tail and pos == 4:
                        row_stats(k - 3, (0, 1, 2))
                    if tail and pos == 7:
                        row_stats(k - 3, (3,))
                        moments(k - 3)
                    if tail and pos == 3:
                        weigh(k - 3, 3)
                    if pick and pos == 6:
                        placing(k - 4, r, 0)
                    if pick and pos == 9:
                        placing(k - 4, r, 1)
                    if pick and pos == 12:
                        placing(k - 4, r, 2)
                    if tail and pos == 10:
                        normalise_rows(k - 3)
                    if more and pos == 15:
                        dve.wait_ge(s["cT_done"], k + 1)
                        mask_ctx(k + 1)
                    if known and k == 1 and pos - 1 in PREPARE:
                        expert_weights(PREPARE.index(pos - 1) + E_FIRST)
                    if known and k == 1 and pos - 3 in PREPARE:
                        hidden_bias(PREPARE.index(pos - 3) + E_FIRST)
                    if known and k == 1 and pos == 5:
                        x_scales(1, 2 * CB, B)

            step(0, 0)
            x_stats(1, 2 * CB, B)
            dve.wait_ge(s["vec_in"], 64)
            dve.wait_ge(s["vecT_ready"], 1)
            for e in range(E_FIRST):
                expert_weights(e)
                hidden_bias(e)
            for k in range(1, 4):
                if k == 3:
                    dve.wait_ge(s["route_init"], 3)
                step(k // 2, k % 2)
            with dve.Fori(2, NCH // 2 - 1) as t:
                step(t, 0)
                step(t, 1)
            for k in range(NCH - 2, STEPS):
                step(k // 2, k % 2)

            n = [0]

            def link(ins):
                n[0] += 1
                ins.then_inc(s["table_step"], 1)
                dve.wait_ge(s["table_step"], n[0])

            dve.wait_ge(s["count_done"], 1)
            link(dve.tensor_copy(count[:, :], pj_bank[:, 0:E]))
            dve.tensor_tensor(pad_place[:, :], count[:, :], expert_base[:, :], ALU.add).then_inc(s["pad_ready"], 1)
            link(dve.tensor_tensor(has_tile[:, :, :], count[:, :].unsqueeze(2).broadcast_to([P, E, T // P]),
                                   tile_bound[:, :].unsqueeze(1).broadcast_to([P, E, T // P]), ALU.is_gt))
            link(dve.tensor_reduce(tiles[:, :], has_tile[:, :, :], AX.X, ALU.add))
            link(dve.tensor_tensor_scan(tiles_to[:, :], ones_e[:, :], tiles[:, :], 0.0, ALU.mult, ALU.add))
            wide = [P, NTILE, E]
            link(dve.tensor_tensor(passed[:, :, :], tile_id[:, :].unsqueeze(2).broadcast_to(wide), tiles_to[:, :].unsqueeze(1).broadcast_to(wide), ALU.is_ge))
            link(dve.tensor_reduce(tile_e[:, :, 0], passed[:, :, :], AX.X, ALU.add))
            link(dve.tensor_tensor(passed[:, :, :], passed[:, :, :], tiles[:, :].unsqueeze(1).broadcast_to(wide), ALU.mult))
            link(dve.tensor_reduce(tile_b[:, :, 0], passed[:, :, :], AX.X, ALU.add))
            link(dve.scalar_tensor_tensor(out=tile_b[:, :, 0], in0=tile_e[:, :, 0], scalar=float(ROOM // P), in1=tile_b[:, :, 0], op0=ALU.mult, op1=ALU.subtract))
            link(dve.tensor_tensor(tile_b[:, :, 0], tile_b[:, :, 0], tile_id[:, :], ALU.add))
            dve.tensor_scalar(tile_expert[:, :], tile_e[:, :, 0], float(E - 1), None, ALU.min)
            dve.tensor_scalar(tile_row[:, :], tile_b[:, :, 0], float(P), float(E * ROOM), ALU.mult, ALU.min).then_inc(s["table_ready"], 1)
            dve.wait_ge(s["table_ready"], 1)
            dve.wait_ge(s["b2_in"], 16)

            def expert_of(i):
                return dve.value_load(tile_expert[0:1, bass.ds(i, 1)], min_val=0, max_val=E - 1)

            def fetch_w2(t, q, e):
                i = UN * t + q
                if not (isinstance(t, int) and i < 2):
                    dve.wait_ge(s["down_done"], i - 1)
                dve.tensor_copy(w2_now[q % 2][:, :], w2T[:, bass.ds(e, 1), :].rearrange("p o n -> p (o n)")).then_inc(s["w2_here"], 1)

            def hidden(t, q, e):
                i = UN * t + q
                dve.wait_ge(s["up_done0"], i + 1)
                if not (isinstance(t, int) and i < 2):
                    dve.wait_ge(s["down_done"], i - 1)
                for c in SIDES[0]:
                    last = dve.tensor_scalar(hidT[q % 2][:, P * c:P * (c + 1)], s_bank[:, q % 2, c, :],
                                             b1T[:, bass.ds(FC * e + c, 1)], 0.0, ALU.add, ALU.max)
                last.then_inc(s["hidT_ready0"], 1)

            def add_b2(t, q, e):
                i = UN * t + q
                dve.wait_ge(s["down_done"], i + 1)
                dve.tensor_tensor(y_sum[q % 2], pv_bank[:, q % 2, 0:D], b2_row[:, bass.ds(e, 1), :].rearrange("p o n -> p (o n)"),
                                  ALU.add).then_inc(s["ysum_ready"], 1)

            def finish(t, q):
                i = UN * t + q
                if not (isinstance(t, int) and i < 4):
                    dve.wait_ge(s[f"out_done{q % 4}"], 16 * (2 * t + q // 4))
                dve.wait_ge(s["ysum_ready"], i + 1)
                dve.scalar_tensor_tensor(out=y_out[q % 4], in0=y_sum[q % 2], scalar=tile_in[q][:, GATE:GATE + 1],
                                         in1=tile_in[q][:, D:2 * D], op0=ALU.mult, op1=ALU.add).then_inc(s["y_ready"], 1)

            def tiles_of(t, first):
                e_last = None if first else expert_of(UN * t - 1)
                e = expert_of(UN * t)
                for q in range(UN):
                    hidden(t, q, e)
                    fetch_w2(t, q, e)
                    if not (first and q == 0):
                        add_b2(t if q else t - 1, (q - 1) % UN, e_last)
                    e_next = expert_of(UN * t + q + 1) if q < UN - 1 else None
                    if not (first and q == 0):
                        finish(t if q else t - 1, (q - 1) % UN)
                    e_last, e = e, e_next

            tiles_of(0, True)
            with dve.Fori(1, NTILE // UN) as t:
                tiles_of(t, False)
            add_b2(NTILE // UN - 1, UN - 1, expert_of(NTILE - 1))
            finish(NTILE // UN - 1, UN - 1)

        @block.tensor
        def _(pe):
            pe.sem_inc(s["pv_done"], PV_CREDIT)
            pe.sem_inc(s["oq_done"], CREDIT)
            pe.sem_inc(s["onT_done"], 1)
            pe.wait_ge(s["weights_in"], 64)
            pe.wait_ge(s["ident_done"], 4)
            for i in range(4):
                last = pe.transpose(pj_bank[:, D * i:D * (i + 1)], w_raw[:, i, :], ident[:, :])
            last.then_inc(s["wt_done"], 1)
            pe.wait_ge(s["wt_copied"], 1)

            def expert_weights(e):
                r = e % 2
                pe.wait_ge(s[f"w_in{e % 4}"], 32 * (e // 4 + 1))
                if e >= 2:
                    pe.wait_ge(s["b1_ready"], e - 1)
                    pe.wait_ge(s["w2T_ready"], e - 1)
                for c in range(FC):
                    last = pe.transpose(st_bank[:, r, c, :], w1_stage[e % 4][:, c, :], ident[:, :])
                last.then_inc(s["w1t_done"], 1)
                for c in range(FC):
                    last = pe.transpose(pv_bank[:, r, P * c:P * (c + 1)], w2_stage[e % 4][:, P * c:P * (c + 1)], ident[:, :])
                last.then_inc(s["w2t_done"], 1)

            def beta_part(e):
                pe.wait_ge(s["w1raw_ready"], e + 1)
                for c in range(FC):
                    last = pe.matmul(st_bank[:, e % 2, 0, c:c + 1], w1_rawT[e % 2][:, P * c:P * (c + 1)], betaT[:, e:e + 1], start=True, stop=True)
                last.then_inc(s["beta_done"], 1)

            def queries_first(c, b):
                n = CB * c + b
                pe.wait_ge(s["otraw_ready"], CREDIT + n + 1)
                pe.wait_ge(s["x1_done"], 1 + n)
                for g in range(4):
                    last = pe.transpose(misc[:, S * g:S * (g + 1)], oT_raw[:, b % 2, S * g:S * (g + 1)], ident[:, :])
                last.then_inc(s["oq_done"], 1)

            def heads_first(c, b):
                pe.wait_ge(s["on_ready"], CB * c + b + 1)
                pe.transpose(misc[:, 0:S], o_norm[:, :, :].rearrange("q h d -> q (h d)"), ident[:, :]).then_inc(s["onT_done"], 1)

            def through_wo(c, b):
                pe.wait_ge(s["onT_ready"], CB * c + b + 1)
                pe.matmul(misc[:, S:2 * S], oT_norm[:, :], wT[:, 3, :], start=True, stop=True).then_inc(s["wo_done"], 1)

            def turn_max(c, half):
                pe.wait_ge(s["mp_ready"], 2 * c + half + 1)
                if not (isinstance(c, int) and c == 0 and half == 0):
                    pe.wait_ge(s["mT_ready"], 2 * c + half)
                pe.transpose(mT_ps, m_parts[:, :, :, :].rearrange("q p h b -> q (p h b)"), ident16[:, :]).then_inc(s["mt_done"], 1)

            def weighed(c, b, g, buf):
                n = SG * b + g
                if n == 0:
                    pe.wait_ge(s["v_ready"], CB * (c + 1))
                    pe.wait_ge(s["keep_cols"], c + 1)
                if g == 0:
                    pe.wait_ge(s["otraw_ready"], CB * c + b + 1)
                pe.wait_ge(s["exp_done"], CREDIT + SLOTS * c + n + 1)
                for j in range(SG):
                    last = pe.matmul(pv_bank[32 * j:32 * (j + 1), b % 2, S * g:S * (g + 1)], v_blk[buf][:, b, SG * g + j, :],
                                     e_ring[:, n % 4, j, :], start=True, stop=True)
                last.then_inc(s["pv_done"], 1)

            def step(t, r):
                k = 2 * t + r
                known = isinstance(t, int)
                proj, vals, sc = (not known or a <= k < a + NCH for a in (0, 1, 1))
                st, tail, pick = (not known or a <= k < a + NCH for a in (2, 3, 4))
                xt, qq, ct, kk, keys_bank = (0, 1, 0, 1, misc) if known and k == 0 else (XT, QQ, CT, KK, pj_bank)
                for pos in range(POS):
                    b, g = pos // 4, pos % 4
                    if st and known and k == 2 and pos == 0:
                        pe.wait_ge(s["ones_init"], 2)
                    if st:
                        if pos % 8 == 0:
                            pe.wait_ge(s["m_in"], 16 * (2 * (k - 2) + pos // 8 + 1))
                        pe.wait_ge(s["exp_done"], SLOTS * (k - 2) + pos + 1)
                        for j in range(2):
                            last = pe.matmul(st_bank[:, pos % 2, 2 * j:2 * j + 2, :], k_stack[r][0:MROWS, 2 * g + j, S * b:S * (b + 1)],
                                             q_stack[r][0:MROWS, 2 * g + j, :, S * b:S * (b + 1)], start=True, stop=True)
                        last.then_inc(s["st_done"], 1)
                    if sc:
                        if pos % 8 == 0:
                            pe.wait_ge(s["stack_in"], 96 * (k - 1) + 6 * pos + 48)
                        pe.wait_ge(s["max_done"], SLOTS * (k - 1) + pos + 1)
                        for j in range(4):
                            pr = 2 * g + j // 2
                            last = pe.matmul(s_bank[:, pos % 2, j, :], q_stack[(r + 1) % 2][0:SROWS, pr, j % 2, S * b:S * (b + 1)],
                                             k_stack[(r + 1) % 2][0:SROWS, pr, S * b:S * (b + 1)], start=True, stop=True)
                        last.then_inc(s["s_done"], 1)
                    if st and pos >= 2:
                        weighed(k - 2, (pos - 2) // 4, (pos - 2) % 4, r)
                    if tail and pos < 2:
                        weighed(k - 3, 3, 2 + pos, (r + 1) % 2)
                    if proj and pos == xt:
                        pe.wait_ge(s["xn_ready"], CB * (k + 1))
                        if not known or k >= 4:
                            pe.wait_ge(s["fT_ready"], k - 3)
                        elif k == 1:
                            pe.wait_ge(s["vecT_ready"], 1)
                        elif k:
                            pe.wait_ge(s["v_ready"], CB * (k - 1))
                        for b in range(CB):
                            last = pe.transpose(pj_bank[:, S * b:S * (b + 1)], xn[:, b, :], ident[:, :])
                        last.then_inc(s["xT_done"], 1)
                    if proj and pos == qq:
                        pe.wait_ge(s["xT_ready"], k + 1)
                        pe.matmul(pj_bank[:, :], wT[:, 0, :], xnT[:, :], start=True, stop=True).then_inc(s["q_done"], 1)
                    if vals and pos == VV:
                        if proj:
                            pe.wait_ge(s["k_rest_r"], k + 1)
                        else:
                            pe.wait_ge(s["fT_ready"], k - 3)
                        for b in range(CB):
                            last = pe.matmul(pj_bank[:, S * b:S * (b + 1)], ctxT[(r + 1) % 2][:, S * b:S * (b + 1)], wT[:, 2, :], start=True, stop=True)
                        last.then_inc(s["v_done"], 1)
                    if proj and pos == ct:
                        pe.wait_ge(s["ctx_ready"], k + 1)
                        if not (known and k == 0):
                            pe.wait_ge(s["q_rest_r"], k + 1)
                        for b in range(CB):
                            last = pe.transpose(keys_bank[:, S * b:S * (b + 1)], ctx_in[:, b, :], ident[:, :])
                        last.then_inc(s["cT_done"], 1)
                    if proj and pos == kk:
                        pe.wait_ge(s["ctxT_ready"], k + 1)
                        pe.matmul(keys_bank[:, :], wT[:, 1, :], ctxT[r][:, :], start=True, stop=True).then_inc(s["k_done"], 1)
                    if tail and pos == FT:
                        pe.wait_ge(s["feats_ready"], k - 2)
                        if vals:
                            pe.wait_ge(s["v_ready"], CB * k)
                        else:
                            pe.wait_ge(s["fT_ready"], k - 3)
                        for b in range(CB):
                            last = pe.transpose(pj_bank[:, S * b:S * (b + 1)], feats[:, b, :], ident[:, :])
                        last.then_inc(s["fT_done"], 1)
                    if tail and pos == 3:
                        if st:
                            pe.wait_ge(s["mT_ready"], 2 * (k - 1))
                        queries_first(k - 3, 3)
                    if st and pos in (7, 11, 15):
                        if pos == 7 and pick:
                            pe.wait_ge(s["rank_read"], k - 3)
                        if pos == 11 and sc:
                            pe.wait_ge(s["mT_ready"], 2 * (k - 1) + 1)
                        if pos == 15 and tail:
                            pe.wait_ge(s["score_read"], k - 2)
                        queries_first(k - 2, (pos - 7) // 4)
                    if st and pos in (8, 12):
                        heads_first(k - 2, (pos - 8) // 4)
                    if tail and pos in (0, 4):
                        heads_first(k - 3, 2 + pos // 4)
                    if st and pos in (9, 13):
                        through_wo(k - 2, (pos - 9) // 4)
                    if tail and pos in (1, 5):
                        through_wo(k - 3, 2 + pos // 4)
                    if sc and pos == 10:
                        if st:
                            pe.wait_ge(s["x1_done"], 1 + CB * (k - 2) + 1)
                        turn_max(k - 1, 0)
                    if st and pos == 2:
                        if tail:
                            pe.wait_ge(s["x1_done"], 1 + CB * (k - 3) + 3)
                        turn_max(k - 2, 1)
                    if tail and pos == 14:
                        pe.wait_ge(s["fT_ready"], k - 2)
                        pe.wait_ge(s["x1_done"], 1 + (CB * (k - 2) + 2 if st else CB * (k - 2)))
                        for b in range(CB):
                            last = pe.matmul(score_ps[:, E * b:E * (b + 1)], featsT[:, S * b:S * (b + 1)], centT[:, :], start=True, stop=True)
                        last.then_inc(s["score_done"], 1)
                    if known and k == 1 and pos in PREPARE:
                        expert_weights(PREPARE.index(pos) + E_FIRST)
                    if known and k == 1 and pos - 2 in PREPARE:
                        beta_part(PREPARE.index(pos - 2) + E_FIRST)
                    if pick and pos == 6:
                        if tail:
                            pe.wait_ge(s["x1_done"], 1 + CB * (k - 2))
                        pe.wait_ge(s["onehot_ready"], k - 3)
                        pe.wait_ge(s["before_ready"], k - 4) if not (known and k == 4) else None
                        pe.matmul(rank_ps, upto[:, :], onehot[:, :, :].rearrange("p b e -> p (b e)"), start=True, stop=False)
                        pe.matmul(rank_ps, ones16[:, :], before[:, :].unsqueeze(1).broadcast_to([P, CB, E]), start=False, stop=False)
                        for b in range(CB - 1):
                            last = pe.matmul(rank_ps[:, E * (b + 1):], ones16[:, :], onehot[:, b:b + 1, :].broadcast_to([P, CB - 1 - b, E]),
                                             start=False, stop=(b == CB - 2))
                        last.then_inc(s["rank_done"], 1)

            step(0, 0)
            pe.wait_ge(s["vec_in"], 64)
            pe.wait_ge(s["k_rest_r"], 1)
            pe.transpose(pj_bank[:, 0:E], cent[:, :], ident[0:E, 0:E])
            pe.transpose(pj_bank[:, 64:64 + E * FC], b1_in[:, :], ident[0:E * FC, 0:E * FC]).then_inc(s["vec_turned"], 1)
            for e in range(E_FIRST):
                expert_weights(e)
                beta_part(e)
            step(0, 1)
            pe.wait_ge(s["w2T_ready"], E)
            pe.wait_ge(s["b1_ready"], E)
            step(1, 0)
            pe.wait_ge(s["route_init"], 3)
            step(1, 1)
            with pe.Fori(2, NCH // 2) as t:
                step(t, 0)
                step(t, 1)
            for k in range(NCH, STEPS):
                step(k // 2, k % 2)
            pe.wait_ge(s["before_ready"], NCH)
            pe.matmul(pj_bank[:, 0:E], ones16[:, :], before[:, :], start=True, stop=True).then_inc(s["count_done"], 1)

            def turn_z(t, q):
                pe.wait_ge(s[f"tile_in{q}"], 16 * (t + 1))
                pe.transpose((misc, pj_bank)[q % 2][:, 0:P], tile_in[q][:, 0:D], ident[:, :]).then_inc(s["zt_done"], 1)

            def up(t, q):
                i = UN * t + q
                pe.wait_ge(s["zT_ready"], i + 1)
                pe.wait_ge(s["w1_here"], i + 1)
                for side in range(2):
                    if not (isinstance(t, int) and i < 2):
                        pe.wait_ge(s[f"hidT_ready{side}"], i - 1)
                    for c in SIDES[side]:
                        last = pe.matmul((s_bank, st_bank)[side][:, q % 2, c, :], w1_now[q % 2][:, P * c:P * (c + 1)], zT[q % 4], start=True, stop=True)
                    last.then_inc(s[f"up_done{side}"], 1)

            def down(t, q):
                i = UN * t + q
                pe.wait_ge(s["w2_here"], i + 1)
                pe.wait_ge(s["hidT_ready0"], i + 1)
                pe.wait_ge(s["hidT_ready1"], i + 1)
                if not (isinstance(t, int) and i < 2):
                    pe.wait_ge(s["ysum_ready"], i - 1)
                for c in range(FC):
                    last = pe.matmul(pv_bank[:, q % 2, 0:D], hidT[q % 2][:, P * c:P * (c + 1)], w2_now[q % 2][:, D * c:D * (c + 1)],
                                     start=(c == 0), stop=(c == FC - 1))
                last.then_inc(s["down_done"], 1)

            def tiles_of(t, first, last):
                for q in range(UN):
                    up(t, q)
                    if not (first and q == 0):
                        down(t if q else t - 1, (q - 1) % UN)
                    if not (last and q >= UN - 2):
                        turn_z(t if q < UN - 2 else t + 1, (q + 2) % UN)

            pe.wait_ge(s["table_ready"], 1)
            turn_z(0, 0)
            turn_z(0, 1)
            tiles_of(0, True, False)
            with pe.Fori(1, NTILE // UN - 1) as t:
                tiles_of(t, False, False)
            tiles_of(NTILE // UN - 1, False, True)
            down(NTILE // UN - 1, UN - 1)


_INS = ['x', 'ctx_1024', '_lenS2', 'L0_xattn_Wq', 'L0_xattn_Wk', 'L0_xattn_Wv', 'L0_xattn_Wo', 'L0_ffn_centroids',
        'L0_ffn_gamma', 'L0_ffn_beta', 'L0_ffn_W1', 'L0_ffn_b1', 'L0_ffn_W2', 'L0_ffn_b2']
_OUT = (32, 128, 128)


def kernel(**inputs):
    import numpy as _np
    import concourse.bacc as _bacc
    from concourse import mybir as _mybir
    from concourse.bass_utils import run_bass_kernel_spmd as _run

    nc = _bacc.Bacc("TRN2", target_bir_lowering=False, num_devices=1)
    arrays, args = {}, []
    for name in _INS:
        a = _np.ascontiguousarray(inputs[name])
        arrays[f"in_{name}_dram"] = a
        args.append(nc.dram_tensor(f"in_{name}_dram", a.shape, _mybir.dt.from_np(a.dtype), kind="ExternalInput").ap())
    out = nc.dram_tensor("out_dram", _OUT, F32, kind="ExternalOutput").ap()
    xattn_ffn_kernel(nc, *args, out)
    r = _run(nc, [arrays], core_ids=[0])
    return r.results[0]["out_dram"]
```
